# Optimizing a Trainium2 kernel written in Bass

```python
import numpy as np
import jax
import jax.numpy as jnp

def _softmax(x, axis=-1):
    return jax.nn.softmax(x, axis=axis)

def _gelu(x):
    return jax.nn.gelu(x, approximate=True)

def _silu(x):
    return jax.nn.silu(x)

def _sigmoid(x):
    return jax.nn.sigmoid(x)

def _layernorm(x, axis=-1, eps=1e-05):
    m = jnp.mean(x, axis=axis, keepdims=True)
    v = jnp.var(x, axis=axis, keepdims=True)
    return (x - m) / jnp.sqrt(v + eps)

def _scatter_add(tgt, idx, src, axis=0):
    return tgt.at[idx].add(src)

def _segment_sum(src, seg, n):
    return jax.ops.segment_sum(src, seg, n)
kernel_name = 'mk_vit_tower_postln_d1_tok_img768_r4_53dbd1'

def setup_inputs(seed: int=0):
    np.random.seed(seed)
    _w = jnp.asarray

    def _rec_inputs():
        import jax
        import jax.numpy as jnp
        _rk = jax.random.key(seed)
        x = -0.000505798 + 1.00042 * jax.random.normal(jax.random.fold_in(_rk, 1), (16, 3, 112, 112), jnp.float32)
        return x
    x = _rec_inputs()

    def _L0_tok_setup():
        import jax, jax.numpy as jnp
        from jax import lax
        import numpy as np
        import math
        B, C, H, W = (8, 3, 96, 96)
        P = 16
        E = 192
        VOCAB = 256

        def _conv2d(x, w, b, stride=1, pad=1):
            y = lax.conv_general_dilated(x, w, (stride, stride), [(pad, pad), (pad, pad)], dimension_numbers=('NCHW', 'OIHW', 'NCHW'))
            return y + b[None, :, None, None]

        def _group_norm(x, g, b, groups=32, eps=1e-05):
            N, Ch, Hh, Ww = x.shape
            xr = x.reshape(N, groups, Ch // groups, Hh, Ww)
            m = xr.mean(axis=(2, 3, 4), keepdims=True)
            v = xr.var(axis=(2, 3, 4), keepdims=True)
            xn = ((xr - m) / jnp.sqrt(v + eps)).reshape(N, Ch, Hh, Ww)
            return xn * g[None, :, None, None] + b[None, :, None, None]
        key = jax.random.key(seed)
        ks = jax.random.split(key, 8)
        f32 = jnp.float32
        return {'pixel_values': jax.random.normal(ks[0], (B, C, H, W), f32), 'conv1_w': jax.random.normal(ks[1], (64, C, 3, 3), f32) * 0.05, 'conv1_b': jnp.zeros((64,), f32), 'gn1_g': jnp.ones((64,), f32), 'gn1_b': jnp.zeros((64,), f32), 'rconv1_w': jax.random.normal(ks[2], (64, 64, 3, 3), f32) * 0.05, 'rconv1_b': jnp.zeros((64,), f32), 'gn2_g': jnp.ones((64,), f32), 'gn2_b': jnp.zeros((64,), f32), 'rconv2_w': jax.random.normal(ks[3], (64, 64, 3, 3), f32) * 0.05, 'rconv2_b': jnp.zeros((64,), f32), 'proj_w': jax.random.normal(ks[4], (E, 64, P, P), f32) * 0.02, 'proj_b': jnp.zeros((E,), f32), 'row_emb': jax.random.normal(ks[5], (VOCAB, E), f32) * 0.02, 'col_emb': jax.random.normal(ks[6], (VOCAB, E), f32) * 0.02}
    _L0_tok_all = _L0_tok_setup()
    _L0_tok_in = {k: v for k, v in _L0_tok_all.items() if k in ('conv1_w', 'conv1_b', 'gn1_g', 'gn1_b', 'rconv1_w', 'rconv1_b', 'gn2_g', 'gn2_b', 'rconv2_w', 'rconv2_b', 'proj_w', 'proj_b', 'row_emb', 'col_emb')}
    del _L0_tok_all

    def _L0_attn_setup():
        import jax, jax.numpy as jnp
        import numpy as np
        B, S, D, H = (64, 577, 192, 12)
        DH = D // H
        key = jax.random.key(seed)
        ks = jax.random.split(key, 9)
        sc = 0.02
        return {'x': jax.random.normal(ks[0], (B, S, D), jnp.float32), 'Wq': jax.random.normal(ks[1], (H, D, DH), jnp.float32) * sc, 'bq': jnp.zeros((H, DH), jnp.float32), 'Wk': jax.random.normal(ks[2], (H, D, DH), jnp.float32) * sc, 'bk': jnp.zeros((H, DH), jnp.float32), 'Wv': jax.random.normal(ks[3], (H, D, DH), jnp.float32) * sc, 'bv': jnp.zeros((H, DH), jnp.float32), 'Wo': jax.random.normal(ks[4], (D, D), jnp.float32) * sc, 'bo': jnp.zeros((D,), jnp.float32)}
    _L0_attn_all = _L0_attn_setup()
    _L0_attn_in = {k: v for k, v in _L0_attn_all.items() if k in ('Wq', 'bq', 'Wk', 'bk', 'Wv', 'bv', 'Wo', 'bo')}
    del _L0_attn_all

    def _L0_ffn_setup():
        import jax, jax.numpy as jnp
        import numpy as np
        B, N, D, H, E, HID, TOPK = (8, 197, 192, 12, 8, 768, 2)

        def _layernorm(x, w, b, eps=1e-05):
            mu = jnp.mean(x, axis=-1, keepdims=True)
            var = jnp.mean((x - mu) ** 2, axis=-1, keepdims=True)
            return (x - mu) * jax.lax.rsqrt(var + eps) * w + b
        key = jax.random.key(seed)
        ks = jax.random.split(key, 8)
        s = 0.02
        return {'x': jax.random.normal(ks[0], (B, N, D), jnp.float32), 'norm1_w': jnp.ones((D,), jnp.float32), 'norm1_b': jnp.zeros((D,), jnp.float32), 'qkv_w': jax.random.normal(ks[1], (3 * D, D), jnp.float32) * s, 'qkv_b': jnp.zeros((3 * D,), jnp.float32), 'proj_w': jax.random.normal(ks[2], (D, D), jnp.float32) * s, 'proj_b': jnp.zeros((D,), jnp.float32), 'norm2_w': jnp.ones((D,), jnp.float32), 'norm2_b': jnp.zeros((D,), jnp.float32), 'w_gate': jax.random.normal(ks[3], (D, E), jnp.float32) * s, 'W1': jax.random.normal(ks[4], (E, D, HID), jnp.float32) * s, 'b1': jnp.zeros((E, HID), jnp.float32), 'W2': jax.random.normal(ks[5], (E, HID, D), jnp.float32) * s, 'b2': jnp.zeros((E, D), jnp.float32)}
    _L0_ffn_all = _L0_ffn_setup()
    _L0_ffn_in = {k: v for k, v in _L0_ffn_all.items() if k in ('norm1_w', 'norm1_b', 'qkv_w', 'qkv_b', 'proj_w', 'proj_b', 'norm2_w', 'norm2_b', 'w_gate', 'W1', 'b1', 'W2', 'b2')}
    del _L0_ffn_all
    return {'x': x, 'L0_tok_conv1_w': _L0_tok_in['conv1_w'], 'L0_tok_conv1_b': _L0_tok_in['conv1_b'], 'L0_tok_gn1_g': _L0_tok_in['gn1_g'], 'L0_tok_gn1_b': _L0_tok_in['gn1_b'], 'L0_tok_rconv1_w': _L0_tok_in['rconv1_w'], 'L0_tok_rconv1_b': _L0_tok_in['rconv1_b'], 'L0_tok_gn2_g': _L0_tok_in['gn2_g'], 'L0_tok_gn2_b': _L0_tok_in['gn2_b'], 'L0_tok_rconv2_w': _L0_tok_in['rconv2_w'], 'L0_tok_rconv2_b': _L0_tok_in['rconv2_b'], 'L0_tok_proj_w': _L0_tok_in['proj_w'], 'L0_tok_proj_b': _L0_tok_in['proj_b'], 'L0_tok_row_emb': _L0_tok_in['row_emb'], 'L0_tok_col_emb': _L0_tok_in['col_emb'], 'L0_attn_Wq': _L0_attn_in['Wq'], 'L0_attn_bq': _L0_attn_in['bq'], 'L0_attn_Wk': _L0_attn_in['Wk'], 'L0_attn_bk': _L0_attn_in['bk'], 'L0_attn_Wv': _L0_attn_in['Wv'], 'L0_attn_bv': _L0_attn_in['bv'], 'L0_attn_Wo': _L0_attn_in['Wo'], 'L0_attn_bo': _L0_attn_in['bo'], 'L0_ffn_norm1_w': _L0_ffn_in['norm1_w'], 'L0_ffn_norm1_b': _L0_ffn_in['norm1_b'], 'L0_ffn_qkv_w': _L0_ffn_in['qkv_w'], 'L0_ffn_qkv_b': _L0_ffn_in['qkv_b'], 'L0_ffn_proj_w': _L0_ffn_in['proj_w'], 'L0_ffn_proj_b': _L0_ffn_in['proj_b'], 'L0_ffn_norm2_w': _L0_ffn_in['norm2_w'], 'L0_ffn_norm2_b': _L0_ffn_in['norm2_b'], 'L0_ffn_w_gate': _L0_ffn_in['w_gate'], 'L0_ffn_W1': _L0_ffn_in['W1'], 'L0_ffn_b1': _L0_ffn_in['b1'], 'L0_ffn_W2': _L0_ffn_in['W2'], 'L0_ffn_b2': _L0_ffn_in['b2']}

def reference(x, L0_tok_conv1_w, L0_tok_conv1_b, L0_tok_gn1_g, L0_tok_gn1_b, L0_tok_rconv1_w, L0_tok_rconv1_b, L0_tok_gn2_g, L0_tok_gn2_b, L0_tok_rconv2_w, L0_tok_rconv2_b, L0_tok_proj_w, L0_tok_proj_b, L0_tok_row_emb, L0_tok_col_emb, L0_attn_Wq, L0_attn_bq, L0_attn_Wk, L0_attn_bk, L0_attn_Wv, L0_attn_bv, L0_attn_Wo, L0_attn_bo, L0_ffn_norm1_w, L0_ffn_norm1_b, L0_ffn_qkv_w, L0_ffn_qkv_b, L0_ffn_proj_w, L0_ffn_proj_b, L0_ffn_norm2_w, L0_ffn_norm2_b, L0_ffn_w_gate, L0_ffn_W1, L0_ffn_b1, L0_ffn_W2, L0_ffn_b2):
    import jax
    import jax.numpy as jnp

    def _L0_tok_ref(pixel_values, conv1_w, conv1_b, gn1_g, gn1_b, rconv1_w, rconv1_b, gn2_g, gn2_b, rconv2_w, rconv2_b, proj_w, proj_b, row_emb, col_emb):
        import jax, jax.numpy as jnp
        from jax import lax
        import numpy as np
        import math
        B, C, H, W = (8, 3, 96, 96)
        P = 16
        E = 192
        VOCAB = 256

        def _conv2d(x, w, b, stride=1, pad=1):
            y = lax.conv_general_dilated(x, w, (stride, stride), [(pad, pad), (pad, pad)], dimension_numbers=('NCHW', 'OIHW', 'NCHW'))
            return y + b[None, :, None, None]

        def _group_norm(x, g, b, groups=32, eps=1e-05):
            N, Ch, Hh, Ww = x.shape
            xr = x.reshape(N, groups, Ch // groups, Hh, Ww)
            m = xr.mean(axis=(2, 3, 4), keepdims=True)
            v = xr.var(axis=(2, 3, 4), keepdims=True)
            xn = ((xr - m) / jnp.sqrt(v + eps)).reshape(N, Ch, Hh, Ww)
            return xn * g[None, :, None, None] + b[None, :, None, None]
        bsz, c, h, w = pixel_values.shape
        h0, w0 = (h // P, w // P)
        seq_len = h0 * w0
        x = pixel_values.reshape(bsz, c, h0, P, w0, P)
        x = x.transpose(0, 2, 4, 1, 3, 5).reshape(bsz * h0 * w0, c, P, P)
        mean = x.mean(axis=(-2, -1), keepdims=True)
        std = jnp.std(x, axis=(-2, -1), keepdims=True, ddof=1)
        x = (x - mean) / (1e-06 + std)
        x = x / math.sqrt(P)
        x = _conv2d(x, conv1_w, conv1_b)
        residual = x
        x = _group_norm(x, gn1_g, gn1_b)
        x = jax.nn.gelu(x, approximate=False)
        x = _conv2d(x, rconv1_w, rconv1_b)
        x = _group_norm(x, gn2_g, gn2_b)
        x = jax.nn.gelu(x, approximate=False)
        x = _conv2d(x, rconv2_w, rconv2_b)
        x = residual + x
        x = _conv2d(x, proj_w, proj_b, stride=P, pad=0)
        embeddings = x.reshape(bsz, seq_len, E)
        seq_idx = jnp.arange(seq_len)
        row_idx = seq_idx // w0
        col_idx = seq_idx % w0
        col_hi = ((col_idx + 1).astype(jnp.float32) / w0 * VOCAB).astype(jnp.int32)
        col_lo = (col_idx.astype(jnp.float32) / w0 * VOCAB).astype(jnp.int32)
        row_hi = ((row_idx + 1).astype(jnp.float32) / h0 * VOCAB).astype(jnp.int32)
        row_lo = (row_idx.astype(jnp.float32) / h0 * VOCAB).astype(jnp.int32)
        row_pos = (row_lo + row_hi) // 2
        col_pos = (col_lo + col_hi) // 2
        embeddings = embeddings + row_emb[row_pos][None] + col_emb[col_pos][None]
        return embeddings

    def _L0_attn_ref(x, Wq, bq, Wk, bk, Wv, bv, Wo, bo):
        import jax, jax.numpy as jnp
        import numpy as np
        B, S, D, H = (64, 577, 192, 12)
        DH = D // H
        q = jnp.einsum('bsd,hde->bhse', x, Wq) + bq[None, :, None, :]
        k = jnp.einsum('bsd,hde->bhse', x, Wk) + bk[None, :, None, :]
        v = jnp.einsum('bsd,hde->bhse', x, Wv) + bv[None, :, None, :]
        scale = np.float32(1.0 / np.sqrt(DH))
        scores = jnp.einsum('bhqe,bhke->bhqk', q, k) * scale
        probs = jax.nn.softmax(scores, axis=2)
        ctx = jnp.einsum('bhqk,bhke->bhqe', probs, v)
        ctx = ctx.transpose(0, 2, 1, 3).reshape(x.shape[0], x.shape[1], H * DH)
        return ctx @ Wo + bo

    def _L0_ffn_ref(x, norm1_w, norm1_b, qkv_w, qkv_b, proj_w, proj_b, norm2_w, norm2_b, w_gate, W1, b1, W2, b2):
        import jax, jax.numpy as jnp
        import numpy as np
        B, N, D, H, E, HID, TOPK = (8, 197, 192, 12, 8, 768, 2)

        def _layernorm(x, w, b, eps=1e-05):
            mu = jnp.mean(x, axis=-1, keepdims=True)
            var = jnp.mean((x - mu) ** 2, axis=-1, keepdims=True)
            return (x - mu) * jax.lax.rsqrt(var + eps) * w + b
        Bx, Nx, C = x.shape
        hd = C // H
        scale = hd ** (-0.5)
        xn = _layernorm(x, norm1_w, norm1_b)
        qkv = (xn @ qkv_w.T + qkv_b).reshape(Bx, Nx, 3, H, hd).transpose(2, 0, 3, 1, 4)
        q, k, v = (qkv[0], qkv[1], qkv[2])
        attn = jax.nn.softmax(jnp.einsum('bhqd,bhkd->bhqk', q, k) * scale, axis=-1)
        o = jnp.einsum('bhqk,bhkd->bqhd', attn, v).reshape(Bx, Nx, C)
        x = x + (o @ proj_w.T + proj_b)
        xn2 = _layernorm(x, norm2_w, norm2_b).reshape(-1, C)
        T = xn2.shape[0]
        logits = xn2 @ w_gate
        top_vals, top_idx = jax.lax.top_k(logits, TOPK)
        gates = jax.nn.softmax(top_vals, axis=-1)
        gates_full = jnp.zeros((T, E), xn2.dtype).at[jnp.arange(T)[:, None], top_idx].add(gates)

        def body(acc, p):
            w1, bb1, w2, bb2, g = p
            h = jax.nn.gelu(xn2 @ w1 + bb1, approximate=False)
            return (acc + g[:, None] * (h @ w2 + bb2), None)
        moe_out, _ = jax.lax.scan(body, jnp.zeros_like(xn2), (W1, b1, W2, b2, gates_full.T))
        return x + moe_out.reshape(Bx, Nx, C)
    h = _L0_tok_ref(x, L0_tok_conv1_w, L0_tok_conv1_b, L0_tok_gn1_g, L0_tok_gn1_b, L0_tok_rconv1_w, L0_tok_rconv1_b, L0_tok_gn2_g, L0_tok_gn2_b, L0_tok_rconv2_w, L0_tok_rconv2_b, L0_tok_proj_w, L0_tok_proj_b, L0_tok_row_emb, L0_tok_col_emb)
    h = _layernorm(h + _L0_attn_ref(h, L0_attn_Wq, L0_attn_bq, L0_attn_Wk, L0_attn_bk, L0_attn_Wv, L0_attn_bv, L0_attn_Wo, L0_attn_bo), axis=-1)
    h = _layernorm(h + _L0_ffn_ref(h, L0_ffn_norm1_w, L0_ffn_norm1_b, L0_ffn_qkv_w, L0_ffn_qkv_b, L0_ffn_proj_w, L0_ffn_proj_b, L0_ffn_norm2_w, L0_ffn_norm2_b, L0_ffn_w_gate, L0_ffn_W1, L0_ffn_b1, L0_ffn_W2, L0_ffn_b2), axis=-1)
    return h

_drawn_inputs = setup_inputs


def setup_inputs(seed=0):
    import zlib

    import numpy as np

    out = dict(_drawn_inputs(seed))
    spreads = {'L0_tok_conv1_b': (0.0, 0.1),
     'L0_tok_gn1_g': (1.0, 0.2),
     'L0_tok_gn1_b': (0.0, 0.1),
     'L0_tok_rconv1_b': (0.0, 0.1),
     'L0_tok_gn2_g': (1.0, 0.2),
     'L0_tok_gn2_b': (0.0, 0.1),
     'L0_tok_rconv2_b': (0.0, 0.1),
     'L0_tok_proj_b': (0.0, 0.1),
     'L0_attn_bq': (0.0, 0.8),
     'L0_attn_bk': (0.0, 0.8),
     'L0_attn_bv': (0.0, 0.542),
     'L0_attn_bo': (0.0, 0.1),
     'L0_ffn_norm1_w': (1.0, 0.6),
     'L0_ffn_norm1_b': (0.0, 0.8),
     'L0_ffn_qkv_b': (0.0, 0.509),
     'L0_ffn_proj_b': (0.0, 0.1),
     'L0_ffn_norm2_w': (1.0, 0.6),
     'L0_ffn_norm2_b': (0.0, 0.529),
     'L0_ffn_b1': (0.0, 0.739),
     'L0_ffn_b2': (0.0, 0.1)}
    factors = {'L0_tok_row_emb': 5.552,
     'L0_tok_col_emb': 5.518,
     'L0_attn_Wq': 6.124,
     'L0_attn_Wk': 6.026,
     'L0_ffn_qkv_w': 2.717}
    for name, (base, spread) in spreads.items():
        noise = np.random.default_rng([zlib.crc32(name.encode()), seed]).standard_normal(out[name].shape)
        drawn = base * np.exp(spread * noise) if base else spread * noise
        out[name] = jnp.asarray(drawn.astype(out[name].dtype))
    for name, factor in factors.items():
        out[name] = (out[name] * factor).astype(out[name].dtype)
    return out
```

```python
from contextlib import ExitStack

import concourse.bass as bass
import numpy as np
from concourse import mybir

F32 = mybir.dt.float32
F16 = mybir.dt.float16
U32 = mybir.dt.uint32
ALU = mybir.AluOpType
ACT = mybir.ActivationFunctionType
AX_X = mybir.AxisListType.X

B, CIN, HW, P = 16, 3, 112, 16
HP = HW // P
SEQ = HP * HP
TOK = B * SEQ
GT = B * HP
NG = TOK // GT
PIX = P * P
PAD = P + 2
PP = PAD * PAD
CH = 64
E = 192
EK = E // 2
QN = 4
NBAT = 2 * QN
QUADS = TOK // QN
GQ = GT // QN
RING = 4
AHEAD = 3
WBAT = E // NBAT
HALF = PIX // 2
TAPS = 9
IMR = CIN * TAPS
IML = NBAT * PP - 2 * PAD - 2
S = 16.0
EPS = 1e-5
VOCAB = 256
KQ = CIN * 2
HEADS, DH = 12, 16
HPAD = 32
NCH = HEADS * HPAD // 128
NPAIR = B // 2
SC = NCH * SEQ
NE, HID = 8, 768
HC = HID // 128
HT = TOK // 2


def build(nc, a, out):
    with ExitStack() as ctx:
        def sb(name, shape, dt=F32):
            return ctx.enter_context(nc.sbuf_tensor(name, shape, dt))

        def ps(name, shape):
            return ctx.enter_context(nc.psum_tensor(name, shape, F32))

        h_tok = sb("h_tok", [GT, NG, E])
        ident = sb("ident", [128, 128])
        expo = sb("expo", [128, 32])
        PS = [ps(f"bank{i}", [128, 512]) for i in range(8)]
        tokenizer(nc, a, h_tok, ident, expo, PS)
        tower(nc, a, out, h_tok, ident, expo, PS)


def tokenizer(nc, a, h_tok, ident, expo, PS):
    with ExitStack() as ctx:
        def sb(name, shape, dt=F32):
            return ctx.enter_context(nc.sbuf_tensor(name, shape, dt))

        def sem(name):
            return ctx.enter_context(nc.semaphore(name))

        xh_dram = nc.dram_tensor("xh_dram", [CIN, TOK * PP], F16, kind="Internal").ap()
        xl_dram = nc.dram_tensor("xl_dram", [CIN, TOK * PP], F16, kind="Internal").ap()
        z_dram = nc.dram_tensor("z_dram", [IMR, E, PP], F32, kind="Internal").ap()

        big = sb("big", [128, HALF * E])
        mid = sb("mid", [128, GT * HALF])
        wc = big[:, :].bitcast(F16).rearrange("p (q m e) -> p q m e", m=2, e=E)
        g2_h = mid[:, 0:GT * HALF // 2].bitcast(F16).rearrange("p (q n) -> p q n", n=GT)
        g2_l = mid[:, GT * HALF // 2:GT * HALF].bitcast(F16).rearrange("p (q n) -> p q n", n=GT)

        CW = CIN * HP
        o = 0
        x_raw = big[0:GT, o:o + CW * PIX].rearrange("p (c q) -> p c q", q=PIX); o += CW * PIX
        x_n = big[0:GT, o:o + CW * PIX].rearrange("p (c q) -> p c q", q=PIX); o += CW * PIX
        x_h = big[0:GT, o:o + CW * PP // 2].bitcast(F16); o += CW * PP // 2
        x_l = big[0:GT, o:o + CW * PP // 2].bitcast(F16)
        x_hp = x_h.rearrange("p (c r q) -> p c r q", r=PAD, q=PAD)
        x_lp = x_l.rearrange("p (c r q) -> p c r q", r=PAD, q=PAD)

        o = 0
        xnT = mid[:, o:o + KQ * TOK].rearrange("p (k t) -> p k t", t=TOK); o += KQ * TOK
        z_in = mid[0:EK, o:o + IMR * PP].rearrange("p (t r q) -> p t r q", r=PAD, q=PAD)
        assert o + IMR * PP <= GT * HALF
        proj_in = []
        for i in range(2):
            proj_in.append(mid[:, o:o + NBAT * PIX].rearrange("p (n q) -> p n q", q=PIX)); o += NBAT * PIX
        z_pad = []
        for i in range(2):
            z_pad.append(mid[0:IMR, o:o + NBAT * PP].rearrange("p (n r q) -> p n r q", r=PAD, q=PAD)); o += NBAT * PP
        assert o <= GT * HALF

        img = [sb(f"img{i}", [128, NBAT, PAD, PAD], F16) for i in range(2)]
        im2 = [sb(f"im2_{i}", [3 * IMR, NBAT, PAD, PAD], F16) for i in range(2)]
        g1 = [sb(f"g1_{i}", [128, QN, PIX]) for i in range(2)]
        g2b = sb("g2b", [128, 2, QN, HALF])
        g2 = [g2b[:, i] for i in range(2)]
        v_t = sb("v_t", [EK, 2, PIX])
        v_sb = sb("v_sb", [128, KQ, E])
        w_f = g1[0][:, :, :].rearrange("p a b -> p (a b)")[:, 0:TAPS * CH].rearrange("p (t c) -> p t c", c=CH)
        w_f2 = g1[1][:, :, :].rearrange("p a b -> p (a b)")[:, 0:TAPS * CH].rearrange("p (t c) -> p t c", c=CH)
        onehot = g2b[0:2 * HP + 1].rearrange("p a b c -> p (a b c)")[:, 0:TOK]
        emb_rows = g2b[0:2 * HP + 1].rearrange("p a b c -> p (a b c)")[:, TOK:TOK + E]

        r1_h, r1_l = sb("r1_h", [128, TAPS, CH], F16), sb("r1_l", [128, TAPS, CH], F16)
        r2_h, r2_l = sb("r2_h", [128, TAPS, CH], F16), sb("r2_l", [128, TAPS, CH], F16)
        c1_f = sb("c1_f", [3 * IMR, 128])
        c1_w, c1_l = sb("c1_w", [3 * IMR, 128], F16), sb("c1_l", [3 * IMR, 128], F16)
        cz_f = sb("cz_f", [128, IMR])
        cz_h, cz_l = sb("cz_h", [128, IMR], F16), sb("cz_l", [128, IMR], F16)
        vecs = sb("vecs", [128, 7])
        sv = sb("sv", [128, 4])
        bb = sb("bb", [CH, 1])
        bbr = sb("bbr", [CH, GT])
        avg = [sb("avg1", [128, 128]), sb("avg2", [128, 128])]
        psum_w = sb("psum_w", [CH, E])

        st0 = sb("st0", [GT, CW, 6])
        m0 = sb("m0", [GT, 6, CW])
        st = [[sb(f"st{L}{i}", [128, QN, 6]) for i in range(2)] for L in range(2)]
        rr = [sb(f"rr{L}", [128, 2, QN, 2]) for L in range(2)]
        sq = [sb(f"sq{L}", [128, QN, 2]) for L in range(2)]
        ms = [sb(f"ms{L}", [128, 2, QN]) for L in range(2)]
        vv = [sb(f"vv{L}", [128, 4, QN]) for L in range(2)]
        gn = [[sb(f"gn{L}{i}", [128, 2, QN]) for i in range(2)] for L in range(2)]
        acc_tmp = sb("acc_tmp", [GT, E])

        c1p = [PS[0:2], PS[2:4]]
        cab = [PS[4], PS[5]]
        accp, stp = PS[6], PS[7]

        s_x = sem("s_x"); s_xc = sem("s_xc"); s_const = sem("s_const"); s_r1 = sem("s_r1")
        s_w = sem("s_w"); s_c1l = sem("s_c1l"); s_exp = sem("s_exp"); s_bb = sem("s_bb"); s_w2 = sem("s_w2")
        s_d0 = sem("s_d0"); s_p0 = sem("s_p0"); s_xn = sem("s_xn"); s_xz = sem("s_xz"); s_xh = sem("s_xh")
        s_xs = sem("s_xs"); s_xst = sem("s_xst"); s_tr = sem("s_tr"); s_trc = sem("s_trc"); s_imz = sem("s_imz")
        w_in = [sem("w_in0"), sem("w_in1")]; w_sc = sem("w_sc"); w_hi = sem("w_hi"); w_split = sem("w_split")
        w_free = sem("w_free"); w_z = sem("w_z"); w_zc = sem("w_zc"); w_zcp = sem("w_zcp"); w_zst = [sem("w_zst0"), sem("w_zst1")]
        w_conv = sem("w_conv"); w_evh = sem("w_evh"); w_evl = sem("w_evl")
        v_in = sem("v_in"); v_d = sem("v_d"); v_sum = sem("v_sum"); v_tr = sem("v_tr"); v_trc = sem("v_trc")
        s_res = sem("s_res"); s_resc = sem("s_resc")
        im_in = [sem("im_in0"), sem("im_in1")]; p_c1 = sem("p_c1"); p_gelu1 = sem("p_gelu1"); p_h1 = sem("p_h1")
        p_img = sem("p_img"); p_conv = sem("p_conv"); p_gelu2 = sem("p_gelu2"); p_h2 = sem("p_h2")
        p_g2 = sem("p_g2")
        p_bn = [sem("p_bn1"), sem("p_bn2")]
        p_r = [sem("p_r1"), sem("p_r2")]
        p_av = [sem("p_av1"), sem("p_av2")]
        p_avc = [sem("p_avc1"), sem("p_avc2")]
        p_var = [sem("p_var1"), sem("p_var2")]
        p_pow = [sem("p_pow1"), sem("p_pow2")]
        p_gn = [sem("p_gn1"), sem("p_gn2")]
        p_acc = sem("p_acc"); p_accc = sem("p_accc"); chain = [sem("chain1"), sem("chain2")]

        block = ctx.enter_context(nc.Block())
        CONST = [
            (vecs[:], a["vecs"]), (ident[:], a["ident"]), (avg[0][:], a["avg1"]), (avg[1][:], a["avg2"]),
            (c1_f[:], a["c1"]), (onehot, a["onehot"]), (emb_rows, a["emb_rows"]),
            (cz_f[0:CH], a["cz"]), (cz_f[CH:128], a["cz"]),
            (w_f[0:CH], a["r2"]), (w_f[CH:128], a["r2"]), (w_f2[0:CH], a["r1"]), (w_f2[CH:128], a["r1"]),
        ]
        NCONST = 16 * len(CONST)

        def conv(pe, slot, q, bank, wh, wl, lo, hi):
            for n in range(lo, hi):
                w = (wh, wl)[n // TAPS]
                t = n % TAPS
                dy, dx = divmod(t, 3)
                for h in range(2):
                    last = pe.matmul(bank[CH * h:CH * h + CH, :], w[:, t, :],
                                     img[slot][:, QN * q:QN * q + QN, dy + 8 * h:dy + 8 * h + 8, dx:dx + P],
                                     start=(n == 0), stop=(n == 2 * TAPS - 1))
            return last

        def schedule(eng, steps):
            steps(0, first=True)
            with eng.Fori(1, NG) as r:
                steps(r)
            with eng.Fori(1, NG - 1) as g:
                steps(g * 7, done=g)
                with eng.Fori(1, 7) as r:
                    steps(g * 7 + r)
            steps(7 * (NG - 1), done=NG - 1)
            with eng.Fori(1, 6) as r:
                steps(r + 7 * (NG - 1))
            steps(7 * NG - 1, last=True)

        def interior(t):
            return t[:, :, 1:1 + P, 1:1 + P]

        @block.sync
        def _(sp):
            for c in range(CIN):
                sp.dma_start(x_raw[:, c * HP:(c + 1) * HP, :], a["x"][:, c]).then_inc(s_x, 16)
            for dst, src in CONST:
                sp.dma_start(dst, src).then_inc(s_const, 16)
            sp.wait_ge(s_w, 8)
            sp.dma_start(c1_w[2 * IMR:3 * IMR, :], c1_l[2 * IMR:3 * IMR, :]).then_inc(s_c1l, 16)
            with sp.Fori(0, WBAT // 2) as i:
                for s in range(2):
                    sp.wait_ge(w_free, i * 2 + (s + 1))
                    sp.wait_ge(w_split, i * 2 + (s + 1))
                    for h in range(2):
                        sp.dma_start(proj_in[s][CH * h:CH * h + CH],
                                     a["proj"][:, bass.ds(i * (2 * NBAT) + s * NBAT, NBAT), :]).then_inc(w_in[s], 16)

            def im_load(b, s):
                for j, t in enumerate((xh_dram, xl_dram, xh_dram)):
                    for c in range(CIN):
                        at = t[c, bass.ds(b * (NBAT * PP), IML)]
                        src = bass.AP(at.tensor, at.offset, [[PAD, 3], [1, 3], [1, IML]])
                        r0 = j * IMR + c * TAPS
                        dst = im2[s][r0:r0 + TAPS].rearrange("p n r q -> p (n r q)")[:, 0:IML]
                        sp.dma_start(dst, src).then_inc(im_in[s], 16)

            sp.wait_ge(s_xst, 6 * 16)
            im_load(0, 0)
            im_load(1, 1)
            for s in range(2):
                sp.wait_ge(w_zst[s], 16 * (WBAT // 2) + 16)
            sp.wait_ge(w_free, WBAT + 2)
            sp.wait_ge(w_split, WBAT + 2)
            for h in range(2):
                if h:
                    sp.wait_ge(v_sum, CIN)
                sp.dma_start(z_in.rearrange("p t r q -> p t (r q)"),
                             z_dram[:, h * EK:(h + 1) * EK, :].rearrange("t e q -> e t q")).then_inc(v_in, 16)
            with sp.Fori(0, QUADS // 4 - 1) as i:
                for s in range(2):
                    sp.wait_ge(p_c1, i * 4 + (2 * s + 2))
                    im_load(i * 2 + (s + 2), s)

        @block.tensor
        def _(pe):
            pe.wait_ge(s_const, NCONST)
            n = 0
            for w in range(HP):
                for k in range(KQ):
                    bank = PS[(n // 4) % 4]
                    if n == 0:
                        pe.wait_ge(s_xn, CW)
                    if n % 4 == 0 and n >= 16:
                        pe.wait_ge(s_trc, n // 4 - 3)
                    c, hh = divmod(k, 2)
                    mm = pe.transpose(bank[:, (n % 4) * GT:(n % 4) * GT + GT],
                                      x_n[:, c * HP + w, hh * 128:hh * 128 + 128], ident[0:GT, 0:GT])
                    n += 1
                    if n % 4 == 0 or n == HP * KQ:
                        mm.then_inc(s_tr, 1)
            pe.wait_ge(s_w, 8)
            pe.wait_ge(s_trc, (HP * KQ + 3) // 4)
            with pe.Fori(0, WBAT // 2) as i:
                for s in range(2):
                    k1 = i * 2 + (s + 1)
                    pe.wait_ge(w_split, k1 + 2)
                    pe.wait_ge(w_zc, k1)
                    for q in range(2):
                        for h in range(2):
                            for m, w in enumerate((cz_h, cz_l)):
                                mm = pe.matmul(PS[2 * q + h][0:IMR, :], w[:, :],
                                               img[s][:, QN * q:QN * q + QN, 1 + 8 * h:9 + 8 * h, 1:1 + P],
                                               start=(m == 0), stop=(m == 1))
                    mm.then_inc(w_z, 1)
                    for q in range(2):
                        pe.wait_ge(w_evl, i * 4 + (2 * s + q + 1))
                        conv(pe, s, q, cab[q], r2_h, r2_l, 0, 2 * TAPS).then_inc(w_conv, 1)
            for h in range(2):
                for c in range(CIN):
                    pe.wait_ge(v_sum, h * CIN + c + 1)
                    if h * CIN + c >= 1:
                        pe.wait_ge(v_trc, h * CIN + c)
                    for hh in range(2):
                        mm = pe.transpose(PS[0][:, hh * EK:hh * EK + EK], v_t[:, (h * CIN + c) % 2, hh * 128:hh * 128 + 128],
                                          ident[0:EK, 0:EK])
                    mm.then_inc(v_tr, 1)
            pe.wait_ge(v_trc, 2 * CIN)
            pe.wait_ge(s_bb, 1)
            for g in range(NG):
                bank = PS[1 + g % 2]
                if g >= 2:
                    pe.wait_ge(s_resc, g - 1)
                tk = slice(g * GT, g * GT + GT)
                for k in range(KQ):
                    pe.matmul(bank[0:GT, 0:E], xnT[:, k, tk], v_sb[:, k, :], start=(k == 0), stop=False)
                pe.matmul(bank[0:GT, 0:E], bbr[:, :], psum_w[:, :], start=False, stop=False)
                pe.matmul(bank[0:GT, 0:E], onehot[:, tk], emb_rows, start=False, stop=True).then_inc(s_res, 1)

            pe.wait_ge(s_c1l, 16)
            pe.wait_ge(s_resc, NG)

            def conv1(v, j, load):
                if j % 2 == 0:
                    pe.wait_ge(im_in[j // 2], load * 144 + 144)
                pe.wait_ge(p_gelu1, v + 1)
                for b in range(2):
                    mm = pe.matmul(c1p[j % 2][b][:, :], c1_w[:, :],
                                   im2[j // 2][:, QN * (j % 2) + 2 * b:QN * (j % 2) + 2 * b + 2, 0:P, 0:P],
                                   start=True, stop=True)
                mm.then_inc(p_c1, 1)

            def average(L, v, other):
                pe.wait_ge(p_r[L], v + 1)
                if other is not None:
                    pe.wait_ge(p_avc[1 - L], other)
                for m in range(2):
                    mm = pe.matmul(stp[:, L * 2 * QN:(L + 1) * 2 * QN], avg[L][:, :], rr[L][:, :, :, m],
                                   start=(m == 0), stop=(m == 1))
                mm.then_inc(p_av[L], 1)

            def product(g):
                pe.wait_ge(p_g2, g * GQ + 2)
                if not isinstance(g, int) or g > 1:
                    pe.wait_ge(p_accc, g - 1)
                for q in range(HALF):
                    pe.matmul(accp[0:GT, 0:2 * E], g2_h[:, q, :], wc[:, q, :, :], start=(q == 0),
                              stop=(q == HALF - 1), skip_group_check=True)
                    mm = pe.matmul(accp[0:GT, 0:E], g2_l[:, q, :], wc[:, q, 0, :], start=False,
                                   stop=(q == HALF - 1), skip_group_check=True)
                mm.then_inc(p_acc, 1)

            def pe_steps(i, first=False, last=False, done=None):
                for j in range(RING):
                    u = i * 4 + j
                    v = i * 4 + (j + AHEAD)
                    nxt = not (last and j >= 1)
                    prev = not (first and j == 0)
                    if nxt:
                        conv1(v, (j + AHEAD) % 4, i + (j + AHEAD) // 4)
                    pe.wait_ge(p_img, i * 4 + (j + 3))
                    pe.wait_ge(p_gelu2, i * 4 + (j + 1))
                    sl, q, bank = j // 2, j % 2, cab[j % 2]
                    conv(pe, sl, q, bank, r1_h, r1_l, 0, 6)
                    if prev:
                        average(1, i * 4 + (j - 1), i * 4 + (j + 3) if not (last and j >= 2) else QUADS)
                    conv(pe, sl, q, bank, r1_h, r1_l, 6, 15)
                    if nxt:
                        average(0, v, i * 4 + j if prev else None)
                    conv(pe, sl, q, bank, r1_h, r1_l, 15, 18).then_inc(p_conv, 1)
                    if j == 1 and done is not None:
                        product(done)

            for v in range(AHEAD):
                conv1(v, v, 0)
                average(0, v, None)
            schedule(pe, pe_steps)
            average(1, QUADS - 1, QUADS)
            product(NG)

        @block.scalar
        def _(act):
            act.wait_ge(s_imz, 4)
            act.sem_inc(w_zc, 1)
            act.sem_inc(p_gelu1, 2)
            act.sem_inc(p_gelu2, 2)
            act.wait_ge(s_xc, 1)
            for c in range(CW):
                act.activation(x_n[:, c, :], x_raw[:, c, :], ACT.Identity, bias=m0[:, 4, c:c + 1],
                               scale=m0[:, 5, c:c + 1]).then_inc(s_xn, 1)
            act.wait_ge(s_xn, CW)
            act.wait_ge(s_xz, 2)
            x_n4 = x_n.rearrange("p c (r q) -> p c r q", q=P)
            act.activation(interior(x_hp), x_n4, ACT.Copy).then_inc(s_xh, 1)
            for r in range((HP * KQ + 3) // 4):
                act.wait_ge(s_tr, r + 1)
                for n in range(4 * r, min(4 * r + 4, HP * KQ)):
                    w, k = divmod(n, KQ)
                    cp = act.activation(xnT[:, k, :].rearrange("p (t w) -> p t w", w=HP)[:, :, w],
                                        PS[r % 4][:, (n % 4) * GT:(n % 4) * GT + GT], ACT.Copy)
                cp.then_inc(s_trc, 1)
            act.wait_ge(s_xh, 1)
            act.wait_ge(s_xs, 1)
            for c in range(CIN):
                for src, dst in ((x_h, xh_dram), (x_l, xl_dram)):
                    act.dma_start(dst[c, :].rearrange("(p q) -> p q", p=GT),
                                 src[:, c * HP * PP:(c + 1) * HP * PP]).then_inc(s_xst, 16)
            with act.Fori(0, WBAT // 2) as i:
                for s in range(2):
                    act.wait_ge(w_z, i * 2 + (s + 1))
                    act.wait_ge(w_zst[s], i * 16 + 16)
                    for q in range(2):
                        for h in range(2):
                            cp = act.activation(z_pad[s][:, QN * q:QN * q + QN, 1 + 8 * h:9 + 8 * h, 1:1 + P],
                                                PS[2 * q + h][0:IMR, :].rearrange("p (n r c) -> p n r c", n=QN, r=8),
                                                ACT.Copy)
                            cp.then_inc(w_zcp, 1)
                    act.wait_ge(w_zcp, i * 8 + (4 * s + 4))
                    act.sem_inc(w_zc, 1)
                    act.dma_start(z_dram[:, bass.ds(i * (2 * NBAT) + s * NBAT, NBAT), :],
                                  z_pad[s].rearrange("p n r c -> p n (r c)")).then_inc(w_zst[s], 16)
                    for q in range(2):
                        act.wait_ge(w_conv, i * 4 + (2 * s + q + 1))
                        act.wait_ge(s_xst, 6 * 16)
                        act.activation(wc[:, :, 0, bass.ds(i * (2 * NBAT) + (s * NBAT + QN * q), QN)],
                                       cab[q][:, :].rearrange("p (n q) -> p q n", n=QN), ACT.Copy).then_inc(w_evh, 1)
            for n in range(2 * CIN):
                h, c = divmod(n, CIN)
                act.wait_ge(v_tr, n + 1)
                for hh in range(2):
                    cp = act.activation(v_sb[:, 2 * c + hh, h * EK:h * EK + EK], PS[0][:, hh * EK:hh * EK + EK],
                                        ACT.Copy, scale=1.0 / (S * S))
                cp.then_inc(v_trc, 1)

            def gelu(L, w, j):
                act.wait_ge(p_gn[L], w + 1)
                act.wait_ge((p_img, p_g2)[L], w + 1)
                for n in range(QN):
                    coef = gn[L][j % 2]
                    if L == 0:
                        src = c1p[j % 2][n // 2][:, (n % 2) * PIX:(n % 2) * PIX + PIX]
                        dst = g1[j % 2][:, n, :]
                    else:
                        src = cab[j % 2][:, n * HALF:n * HALF + HALF]
                        dst = g2[j % 2][:, n, :]
                    op = act.activation(dst, src, ACT.Gelu, bias=coef[:, 1, n:n + 1], scale=coef[:, 0, n:n + 1])
                op.then_inc((p_gelu1, p_gelu2)[L], 1)

            def high1(w, j):
                act.wait_ge(p_gelu1, w + 3)
                act.activation(interior(img[j // 2][:, QN * (j % 2):QN * (j % 2) + QN]),
                               g1[j % 2][:, :, :].rearrange("p n (r q) -> p n r q", q=P), ACT.Copy)\
                    .then_inc(p_h1, 1)

            def act_steps(i, first=False, last=False, done=None):
                for j in range(RING):
                    if not (first and j == 0):
                        gelu(1, i * 4 + (j - 1), (j - 1) % 4)
                    if not (last and j >= 2):
                        high1(i * 4 + (j + AHEAD - 1), (j + AHEAD - 1) % 4)
                    if not (last and j >= 1):
                        gelu(0, i * 4 + (j + AHEAD), (j + AHEAD) % 4)

            for v in range(AHEAD):
                if v:
                    high1(v - 1, v - 1)
                gelu(0, v, v)
            schedule(act, act_steps)
            gelu(1, QUADS - 1, 3)

        @block.vector
        def _(dve):
            def memzero(t):
                return dve.memset(t, 0.0)
            for i in range(2):
                dve.memset(img[i][:, :, :, :].rearrange("p n r q -> p (n r q)").bitcast(U32), 0).then_inc(s_imz, 1)
                dve.memset(z_pad[i].rearrange("p n r q -> p (n r q)"), 0.0).then_inc(s_imz, 1)
            dve.memset(x_h.bitcast(U32), 0).then_inc(s_xz, 1)
            dve.memset(x_l.bitcast(U32), 0).then_inc(s_xz, 1)
            dve.memset(expo[:, 0:8], -0.5).then_inc(s_exp, 1)
            dve.memset(expo[:, 8:32], 0.5).then_inc(s_exp, 1)
            dve.sem_inc(w_free, 2)
            dve.sem_inc(w_split, 2)
            dve.sem_inc(w_evl, 2)
            for s in range(2):
                dve.sem_inc(w_zst[s], 16)
            dve.sem_inc(p_img, 2)
            dve.sem_inc(p_g2, 2)
            dve.wait_ge(s_x, 16 * CIN)
            dn = [0]

            def d_link(ins):
                dn[0] += 1
                ins.then_inc(s_d0, 1)
                dve.wait_ge(s_d0, dn[0])

            for c in range(CW):
                ins = dve.bn_stats(st0[:, c, :], x_raw[:, c, :])
            d_link(ins)
            me, mo, qe, qo = st0[:, :, 1], st0[:, :, 4], st0[:, :, 2], st0[:, :, 5]
            d_link(dve.tensor_tensor(m0[:, 0, :], me, mo, ALU.add))
            d_link(dve.tensor_scalar(m0[:, 0, :], m0[:, 0, :], 0.5, None, ALU.mult))
            d_link(dve.tensor_tensor(m0[:, 1, :], me, mo, ALU.subtract))
            d_link(dve.tensor_tensor(m0[:, 1, :], m0[:, 1, :], m0[:, 1, :], ALU.mult))
            d_link(dve.tensor_tensor(m0[:, 2, :], qe, qo, ALU.add))
            d_link(dve.scalar_tensor_tensor(m0[:, 2, :], m0[:, 1, :], PIX / 4.0, m0[:, 2, :], ALU.mult, ALU.add))
            dve.tensor_scalar(m0[:, 2, :], m0[:, 2, :], 1.0 / (PIX - 1), None, ALU.mult).then_inc(s_p0, 1)
            dve.wait_ge(s_p0, 2)
            d_link(dve.tensor_scalar(m0[:, 4, :], m0[:, 3, :], 1e-6, 4.0, ALU.add, ALU.mult))
            d_link(dve.reciprocal(m0[:, 5, :], m0[:, 4, :]))
            d_link(dve.scalar_tensor_tensor(m0[:, 4, :], m0[:, 0, :], -1.0, m0[:, 5, :], ALU.mult, ALU.mult))
            dve.sem_inc(s_xc, 1)
            dve.wait_ge(s_const, NCONST)
            wn = [0]

            def w_link(ins):
                wn[0] += 1
                ins.then_inc(s_w2, 1)
                dve.wait_ge(s_w2, wn[0])

            for f, hi, lo in ((w_f, r2_h[:, :, :], r2_l[:, :, :]), (w_f2, r1_h[:, :, :], r1_l[:, :, :]),
                              (c1_f[:, :], c1_w[:, :], c1_l[:, :]), (cz_f[:, :], cz_h[:, :], cz_l[:, :])):
                w_link(dve.tensor_scalar(f, f, S, None, ALU.mult))
                w_link(dve.tensor_copy(hi, f))
                dve.tensor_tensor(lo, f, hi, ALU.subtract).then_inc(s_w, 2)
            for n, (src, f) in enumerate(((0, S), (0, -S), (3, S), (3, -S))):
                w_link(dve.tensor_scalar(sv[:, n:n + 1], vecs[:, src:src + 1], f, None, ALU.mult))
            w_link(dve.tensor_tensor(bb[:, :], vecs[0:CH, 0:1], vecs[0:CH, 6:7], ALU.add))
            w_link(dve.memset(bbr[:, :], 1.0 / S))
            w_link(dve.tensor_scalar(bbr[:, :], bbr[:, :], bb[:, 0:1], None, ALU.mult))
            dve.wait_ge(s_imz, 4)

            def split_rows(k, s, i, n):
                rows = proj_in[s].rearrange("p n (r q) -> p n r q", q=P)
                dve.wait_ge(w_in[s], n * 32 + 32)
                dve.tensor_scalar(proj_in[s], proj_in[s], S, None, ALU.mult).then_inc(w_sc, 1)
                dve.wait_ge(w_sc, k + 1)
                dve.tensor_copy(interior(img[s]), rows).then_inc(w_hi, 1)
                dve.tensor_reduce(psum_w[:, bass.ds(k * NBAT, NBAT)], proj_in[s][0:CH], AX_X, ALU.add)\
                    .then_inc(w_free, 1)

            def low_weights(i, s):
                for q in range(2):
                    dve.wait_ge(w_evh, i * 4 + (2 * s + q + 1))
                    at = bass.ds(i * (2 * NBAT) + (s * NBAT + QN * q), QN)
                    dve.tensor_tensor(wc[:, :, 1, at], cab[q][:, :].rearrange("p (n q) -> p q n", n=QN),
                                      wc[:, :, 0, at], ALU.subtract).then_inc(w_evl, 1)

            split_rows(0, 0, 0, 0)
            with dve.Fori(0, WBAT // 2 - 1) as i:
                split_rows(i * 2 + 1, 1, i, i)
                low_weights(i, 0)
                split_rows(i * 2 + 2, 0, i, i + 1)
                low_weights(i, 1)
            split_rows(WBAT - 1, 1, 0, WBAT // 2 - 1)
            low_weights(WBAT // 2 - 1, 0)
            low_weights(WBAT // 2 - 1, 1)
            dve.wait_ge(w_free, WBAT + 2)
            dve.sem_inc(s_bb, 1)
            vd = 0
            for h in range(2):
                dve.wait_ge(v_in, 16 * h + 16)
                for c in range(CIN):
                    n = h * CIN + c
                    if n >= 2:
                        dve.wait_ge(v_tr, n - 1)
                    o = v_t[:, n % 2, :].rearrange("p (r q) -> p r q", q=P)
                    for t in range(TAPS):
                        dy, dx = divmod(t, 3)
                        part = z_in[:, c * TAPS + t, 2 - dy:2 - dy + P, 2 - dx:2 - dx + P]
                        if t == 0:
                            ins = dve.tensor_copy(o, part)
                        else:
                            dve.wait_ge(v_d, vd)
                            ins = dve.tensor_tensor(o, part, o, ALU.add)
                        vd += 1
                        ins.then_inc(v_d, 1)
                    dve.wait_ge(v_d, vd)
                    dve.sem_inc(v_sum, 1)
            for g in range(NG):
                dve.wait_ge(s_res, g + 1)
                dve.tensor_copy(h_tok[:, g, :], PS[1 + g % 2][0:GT, 0:E]).then_inc(s_resc, 1)

            LINKS = 5

            def stats(L, w, j, patches):
                dve.wait_ge((p_c1, p_conv)[L], w + 1)
                for n in patches:
                    src = c1p[j % 2][n // 2][:, (n % 2) * PIX:(n % 2) * PIX + PIX] if L == 0 else \
                        cab[j % 2][:, n * HALF:n * HALF + HALF]
                    op = dve.bn_stats(st[L][j % 2][:, n, :], src)
                    if n == QN - 1:
                        op.then_inc(p_bn[L], 1)

            def mean(L, w, j):
                f = st[L][j % 2][:, :, :].rearrange("p n (m f) -> p n m f", f=3)
                dve.wait_ge(p_bn[L], w + 1)
                dve.tensor_scalar(rr[L][:, 0], f[:, :, :, 1], sv[:, 2 * L:2 * L + 1], None, ALU.add).then_inc(chain[L], 1)

            def mean_square(L, w, j):
                dve.wait_ge(chain[L], w * LINKS + 1)
                dve.tensor_tensor(sq[L][:, :, :], rr[L][:, 0], rr[L][:, 0], ALU.mult).then_inc(chain[L], 1)

            def second_moment(L, w, j):
                f = st[L][j % 2][:, :, :].rearrange("p n (m f) -> p n m f", f=3)
                dve.wait_ge(chain[L], w * LINKS + 2)
                dve.scalar_tensor_tensor(rr[L][:, 1], f[:, :, :, 2], 1.0 / (PIX / 2 if L == 0 else HALF / 2),
                                         sq[L][:, :, :], ALU.mult, ALU.add).then_inc(p_r[L], 1)

            def copy_average(L, w, j):
                dve.wait_ge(p_av[L], w + 1)
                dve.tensor_copy(ms[L][:, :, :].rearrange("p a b -> p (a b)"),
                                stp[:, L * 2 * QN:(L + 1) * 2 * QN]).then_inc(p_avc[L], 1)

            def minus_square(L, w, j):
                m = ms[L][:, 0, :]
                dve.wait_ge(p_avc[L], w + 1)
                dve.scalar_tensor_tensor(vv[L][:, 0, :], m, -1.0, m, ALU.mult, ALU.mult).then_inc(chain[L], 1)

            def variance(L, w, j):
                dve.wait_ge(chain[L], w * LINKS + 3)
                dve.scalar_tensor_tensor(vv[L][:, 1, :], vv[L][:, 0, :], EPS * S * S, ms[L][:, 1, :],
                                         ALU.add, ALU.add).then_inc(p_var[L], 1)

            def scale(L, w, j):
                dve.wait_ge(p_pow[L], w + 1)
                dve.wait_ge((p_gelu1, p_gelu2)[L], w + 1)
                dve.tensor_scalar(gn[L][j % 2][:, 0, :], vv[L][:, 2, :], vecs[:, 1 + 3 * L:2 + 3 * L], None,
                                  ALU.mult).then_inc(chain[L], 1)

            def shift(L, w, j):
                dve.wait_ge(chain[L], w * LINKS + 4)
                dve.scalar_tensor_tensor(vv[L][:, 3, :], ms[L][:, 0, :], sv[:, 2 * L + 1:2 * L + 2],
                                         gn[L][j % 2][:, 0, :], ALU.add, ALU.mult).then_inc(chain[L], 1)

            def bias(L, w, j):
                dve.wait_ge(chain[L], w * LINKS + 5)
                dve.tensor_scalar(gn[L][j % 2][:, 1, :], vv[L][:, 3, :], -1.0, vecs[:, 2 + 3 * L:3 + 3 * L],
                                  ALU.mult, ALU.add).then_inc(p_gn[L], 1)

            def high2(w, j, at):
                dve.wait_ge(p_gelu2, w + 3)
                dve.tensor_scalar(g2_h[:, :, at], g2[j % 2].rearrange("p n q -> p q n"), 1.0, None, ALU.mult)\
                    .then_inc(p_h2, 1)

            def low2(w, j, at):
                dve.wait_ge(p_h2, w + 1)
                dve.tensor_tensor(g2_l[:, :, at], g2[j % 2].rearrange("p n q -> p q n"), g2_h[:, :, at], ALU.subtract)\
                    .then_inc(p_g2, 1)

            def take_product(g):
                dve.wait_ge(p_acc, g)
                dve.tensor_scalar(acc_tmp[:, :], accp[0:GT, E:2 * E], 1.0 / (S * S), None, ALU.mult).then_inc(s_d0, 1)
                gi = g - 1
                hg = h_tok[:, gi, :] if isinstance(g, int) else h_tok[:, bass.ds(gi, 1), :].rearrange("p o e -> p (o e)")
                dve.wait_ge(s_d0, gi * 3 + (dn[0] + 1))
                dve.tensor_tensor(hg, hg, acc_tmp[:, :], ALU.add).then_inc(s_d0, 1)
                dve.wait_ge(s_d0, gi * 3 + (dn[0] + 2))
                dve.scalar_tensor_tensor(hg, accp[0:GT, 0:E], 1.0 / (S * S), hg, ALU.mult, ALU.add).then_inc(s_d0, 1)
                dve.wait_ge(s_d0, gi * 3 + (dn[0] + 3))
                dve.sem_inc(p_accc, 1)

            def dve_steps(i, first=False, last=False, done=None, at=None):
                r = at
                for j in range(RING):
                    prev, nxt, spl = not (first and j == 0), not (last and j >= 1), not (first and j <= 1)
                    w, jw = i * 4 + (j - 1), (j - 1) % 4
                    v, jv = i * 4 + (j + AHEAD), (j + AHEAD) % 4
                    if spl:
                        if j >= 2:
                            c = bass.ds(r * (4 * QN) + (j - 2) * QN, QN)
                        elif done is not None:
                            c = bass.ds(GT - 2 * QN + j * QN, QN)
                        else:
                            c = bass.ds(r * (4 * QN) + (j * QN - 2 * QN), QN)
                    if prev:
                        stats(1, w, jw, range(QN))
                    if nxt:
                        stats(0, v, jv, range(0, 1))
                    if prev:
                        mean(1, w, jw)
                    if nxt:
                        stats(0, v, jv, range(1, 2))
                    if prev:
                        mean_square(1, w, jw)
                    if nxt:
                        stats(0, v, jv, range(2, 3))
                    if prev:
                        second_moment(1, w, jw)
                    if nxt:
                        stats(0, v, jv, range(3, 4))
                    if done is not None and j == 2:
                        take_product(done)
                    if spl:
                        high2(i * 4 + (j - 2), (j - 2) % 4, c)
                    if nxt:
                        mean(0, v, jv)
                    if prev:
                        copy_average(1, w, jw)
                    if nxt:
                        mean_square(0, v, jv)
                    if prev:
                        minus_square(1, w, jw)
                    if nxt:
                        second_moment(0, v, jv)
                    if prev:
                        variance(1, w, jw)
                    if spl:
                        low2(i * 4 + (j - 2), (j - 2) % 4, c)
                    if prev:
                        scale(1, w, jw)
                    if nxt:
                        copy_average(0, v, jv)
                    if prev:
                        shift(1, w, jw)
                    if nxt:
                        minus_square(0, v, jv)
                    if prev:
                        bias(1, w, jw)
                    if nxt:
                        variance(0, v, jv)
                        scale(0, v, jv)
                        shift(0, v, jv)
                        bias(0, v, jv)

            def whole_chain(L, w, j):
                stats(L, w, j, range(QN))
                mean(L, w, j)
                mean_square(L, w, j)
                second_moment(L, w, j)
                copy_average(L, w, j)
                minus_square(L, w, j)
                variance(L, w, j)
                scale(L, w, j)
                shift(L, w, j)
                bias(L, w, j)

            for v in range(AHEAD):
                whole_chain(0, v, v)
            dve_steps(0, first=True, at=0)
            with dve.Fori(1, 7) as r:
                dve_steps(r, at=r)
            with dve.Fori(1, NG - 1) as g:
                dve_steps(g * 7, done=g, at=0)
                with dve.Fori(1, 7) as r:
                    dve_steps(g * 7 + r, at=r)
            dve_steps(7 * (NG - 1), done=NG - 1, at=0)
            with dve.Fori(1, 6) as r:
                dve_steps(r + 7 * (NG - 1), at=r)
            dve_steps(7 * NG - 1, last=True, at=6)
            high2(QUADS - 2, 2, bass.ds(GT - 2 * QN, QN))
            low2(QUADS - 2, 2, bass.ds(GT - 2 * QN, QN))
            whole_chain(1, QUADS - 1, 3)
            high2(QUADS - 1, 3, bass.ds(GT - QN, QN))
            low2(QUADS - 1, 3, bass.ds(GT - QN, QN))
            take_product(NG)

        @block.gpsimd
        def _(pool):
            pool.wait_ge(s_exp, 2)
            pool.wait_ge(s_p0, 1)
            pool.tensor_tensor(m0[:, 3, :], m0[:, 2, :], expo[0:GT, 8:8 + CW], ALU.pow).then_inc(s_p0, 1)
            x_n4 = x_n.rearrange("p c (r q) -> p c r q", q=P)
            pool.wait_ge(s_xh, 1)
            pool.tensor_tensor(interior(x_lp), x_n4, interior(x_hp), ALU.subtract).then_inc(s_xs, 1)
            pool.wait_ge(s_xs, 1)
            with pool.Fori(0, WBAT // 2) as i:
                for s in range(2):
                    rows = proj_in[s].rearrange("p n (r q) -> p n r q", q=P)
                    pool.wait_ge(w_hi, i * 2 + (s + 1))
                    pool.tensor_tensor(interior(img[s])[CH:128], rows[CH:128], interior(img[s])[CH:128],
                                       ALU.subtract).then_inc(w_split, 1)

            def power(L, w):
                pool.wait_ge(p_var[L], w + 1)
                pool.tensor_tensor(vv[L][:, 2, :], vv[L][:, 1, :], expo[:, 0:QN], ALU.pow).then_inc(p_pow[L], 1)

            def low1(w, j):
                dst = interior(img[j // 2][:, QN * (j % 2):QN * (j % 2) + QN])[CH:128]
                src = g1[j % 2][CH:128, :, :].rearrange("p n (r q) -> p n r q", q=P)
                pool.wait_ge(p_h1, w + 1)
                pool.tensor_tensor(dst, src, dst, ALU.subtract).then_inc(p_img, 1)

            def pool_steps(i, first=False, last=False, done=None):
                for j in range(RING):
                    if last and j == 2:
                        pool.wait_ge(p_img, QUADS + 2)
                    if not (first and j == 0):
                        power(1, i * 4 + (j - 1))
                        pool.wait_ge(p_pow[1], i * 4 + j)
                    else:
                        pool.wait_ge(p_pow[0], AHEAD)
                    if not (last and j >= 2):
                        low1(i * 4 + (j + AHEAD - 1), (j + AHEAD - 1) % 4)
                    if not (last and j >= 1):
                        pool.wait_ge(p_img, i * 4 + (j + AHEAD + 2))
                        power(0, i * 4 + (j + AHEAD))

            for v in range(AHEAD):
                if v:
                    pool.wait_ge(p_pow[0], v)
                    low1(v - 1, v - 1)
                    pool.wait_ge(p_img, v + 2)
                else:
                    pool.wait_ge(w_split, WBAT + 2)
                power(0, v)
            schedule(pool, pool_steps)
            power(1, QUADS - 1)


def tower(nc, a, out, h_tok, ident, expo, PS):
    with ExitStack() as ctx:
        def sb(name, shape, dt=F32):
            return ctx.enter_context(nc.sbuf_tensor(name, shape, dt))

        def sem(name):
            return ctx.enter_context(nc.semaphore(name))

        x_tok = sb("x_tok", [GT, NG, E])
        h1_tok = sb("h1_tok", [GT, NG, E])
        x_T = sb("x_T", [EK, 2 * TOK + 64])
        x_T2 = x_T[:, 0:2 * TOK].rearrange("p (k t) -> p k t", t=TOK)
        qk_T = [sb("q_T", [128, NCH * TOK + 64]), sb("k_T", [128, NCH * TOK + 64])]
        ctx_T = sb("ctx_T", [128, NCH, TOK])
        v1 = sb("v1", [128, NPAIR, HEADS, HPAD])
        v2 = sb("v2", [64, B, HEADS, HPAD])
        vn = sb("vn", [128, HEADS, HPAD])
        prob = [sb(f"prob{i}", [128, HEADS, SEQ]) for i in range(2)]
        prob_T = sb("prob_T", [SEQ, HEADS, 128])
        mx, sm, ri = sb("mx", [128, HEADS]), sb("sm", [128, HEADS]), sb("ri", [128, HEADS])
        wqk = [[sb(f"w{n}{L}", [EK, 2, 128 * NCH]) for n in "qk"] for L in range(2)]
        wv = [sb(f"wv{L}", [EK, 2, E]) for L in range(2)]
        wo = [sb(f"wo{L}", [128, NCH, E]) for L in range(2)]
        bqk = [sb(f"bqk{L}", [128, 2 * NCH]) for L in range(2)]
        rows = sb("rows", [128, 8, E])
        wg = sb("wg", [EK, 2, NE])
        b1 = [sb(f"b1_{i}", [128, HC]) for i in range(2)]
        b2 = sb("b2", [NE, E])
        iota = sb("iota", [GT, NE])
        ln_st, ln_mv = sb("ln_st", [GT, NG, 6]), sb("ln_mv", [GT, NG, 2])
        ln_r = sb("ln_r", [GT, 2, NG])
        lg, top, gate, gtmp = (sb(n, [GT, NG, NE]) for n in ("lg", "top", "gate", "gtmp"))
        topi = sb("topi", [GT, NG, NE], U32)
        idx = sb("idx", [GT, NG, 2])
        gg = sb("gg", [GT, 4, NG])
        gate_T = sb("gate_T", [NE, NG * GT])
        w1 = [sb(f"w1_{i}", [EK, 2, HID]) for i in range(2)]
        w2 = [sb(f"w2_{i}", [128, HC, E]) for i in range(2)]
        hid = sb("hid", [128, HC, TOK])

        t_const = sem("t_const"); t_attn = [sem("t_attn0"), sem("t_attn1")]
        t_x = sem("t_x")
        t_tr = sem("t_tr"); t_trc = sem("t_trc")
        t_qk = sem("t_qk"); t_qkc = sem("t_qkc"); t_v = sem("t_v"); t_vc = sem("t_vc")
        t_sc = sem("t_sc"); t_sub = sem("t_sub"); t_exp = sem("t_exp"); t_p = sem("t_p")
        t_ptr = sem("t_ptr"); t_ptc = sem("t_ptc"); t_ctx = sem("t_ctx"); t_ctxc = sem("t_ctxc")
        t_o = sem("t_o"); t_oc = sem("t_oc")
        t_var = sem("t_var"); t_rs = sem("t_rs"); t_d = sem("t_d"); t_z = sem("t_z")
        t_lg = sem("t_lg"); t_lgd = sem("t_lgd"); t_ge = sem("t_ge"); t_gate = sem("t_gate")
        t_gt = sem("t_gt"); t_gtc = sem("t_gtc"); t_b2 = sem("t_b2"); t_b2c = sem("t_b2c")
        e_w = [sem("e_w0"), sem("e_w1")]; e_used = sem("e_used")
        e_h = sem("e_h"); e_hg = sem("e_hg"); e_y = sem("e_y"); e_yc = sem("e_yc")
        t_done = sem("t_done"); t_h1 = sem("t_h1"); s_out = sem("s_out")
        block = ctx.enter_context(nc.Block())

        CONST = [(rows[:], a["rows"]), (wg[:], a["wg"]), (b2[:], a["b2"]), (iota[:], a["iota"])]
        ATTN = [[(wqk[L][0][:], a[f"wq{L}"]), (wqk[L][1][:], a[f"wk{L}"]), (wv[L][:], a[f"wv{L}"]),
                 (wo[L][:], a[f"wo{L}"]), (bqk[L][:], a[f"bqk{L}"])] for L in range(2)]
        NBANK = 4

        def score_view(bank_cols=SC):
            return [PS[j][:, 0:SC] for j in range(4)]

        @block.sync
        def _(sp):
            for L in range(2):
                for dst, src in ATTN[L]:
                    sp.dma_start(dst, src).then_inc(t_attn[L], 16)
                if L == 0:
                    for dst, src in CONST:
                        sp.dma_start(dst, src).then_inc(t_const, 16)
            with sp.Fori(0, NE // 2) as i:
                for s in range(2):
                    sp.wait_ge(e_used, i * 2 + (s + 1))
                    sp.dma_start(w1[s][:], a["w1"][bass.ds(i * 2 + s, 1)].rearrange("o p k h -> (o p) k h"))\
                        .then_inc(e_w[s], 16)
                    sp.dma_start(w2[s][:], a["w2"][bass.ds(i * 2 + s, 1)].rearrange("o p k h -> (o p) k h"))\
                        .then_inc(e_w[s], 16)
                    sp.dma_start(b1[s][:], a["b1"][bass.ds(i * 2 + s, 1)].rearrange("o p k -> (o p) k"))\
                        .then_inc(e_w[s], 16)
            sp.wait_ge(t_done, 1)
            sp.dma_start(out.rearrange("(g p) e -> p g e", p=GT), h_tok[:, :, :]).then_inc(s_out, 16)
            sp.wait_ge(s_out, 16)

        @block.tensor
        def _(pe):
            def transpose_tokens(n, src):
                pe.wait_ge(t_x, n + 1)
                for g in range(NG):
                    k = n * NG + g
                    if g >= 2 or n:
                        pe.wait_ge(t_trc, k - 1)
                    for c in range(2):
                        mm = pe.transpose(PS[6 + g % 2][0:EK, c * GT:c * GT + GT], src[:, g, c * EK:c * EK + EK],
                                          ident[0:GT, 0:GT])
                    mm.then_inc(t_tr, 1)

            def attention(L):
                pe.wait_ge(t_attn[L], 16 * len(ATTN[L]))
                pe.wait_ge(t_trc, (L + 1) * NG)
                n = 0
                for m in range(2):
                    for j in range(NCH):
                        for h in range(2):
                            k = L * 12 + n
                            if k >= 2:
                                pe.wait_ge(t_qkc, k - 1)
                            for c in range(2):
                                mm = pe.matmul(PS[4 + n % 2][:, 0:HT], wqk[L][m][:, c, 128 * j:128 * j + 128],
                                               x_T2[:, c, h * HT:h * HT + HT], start=(c == 0), stop=(c == 1))
                            mm.then_inc(t_qk, 1)
                            n += 1
                for n in range(NPAIR):
                    k = L * NPAIR + n
                    if k >= 2:
                        pe.wait_ge(t_vc, k - 1)
                    for r in range(2):
                        o = PS[6 + n % 2][64 * r:64 * r + 64, 0:E] if L == 0 else PS[6 + n % 2][0:64, r * E:r * E + E]
                        t0 = (2 * n + r) * SEQ
                        for c in range(2):
                            mm = pe.matmul(o, x_T[:, c * TOK + t0:c * TOK + t0 + 64], wv[L][:, c, :],
                                           start=(c == 0), stop=(c == 1))
                    mm.then_inc(t_v, 1)
                pe.wait_ge(t_qkc, (L + 1) * 12)
                pe.wait_ge(t_vc, (L + 1) * NPAIR)
                lhs, rhs = (qk_T[1], qk_T[0]) if L == 0 else (qk_T[0], qk_T[1])
                for n in range(NPAIR + 1):
                    k = L * NPAIR + n
                    if n < NPAIR:
                        if k >= 1:
                            pe.wait_ge(t_sub, k)
                        for j in range(4):
                            for r in range(2):
                                for c in range(NCH):
                                    t0 = c * TOK + (2 * n + r) * SEQ
                                    mm = pe.matmul(PS[j][64 * r:64 * r + 64, c * SEQ:c * SEQ + SEQ],
                                                   lhs[32 * j:32 * j + 32, t0:t0 + 64],
                                                   rhs[32 * j:32 * j + 32, t0:t0 + SEQ], start=True, stop=True)
                        mm.then_inc(t_sc, 1)
                    if n == 0:
                        continue
                    k, n0 = k - 1, n - 1
                    pe.wait_ge(t_p, k + 1)
                    if L == 0:
                        if k >= 1:
                            pe.wait_ge(t_ctxc, k)
                        for r in range(2):
                            for hd in range(HEADS):
                                c, j = divmod(hd, 4)
                                mm = pe.matmul(PS[4 + r][32 * j:32 * j + 32, c * SEQ:c * SEQ + SEQ],
                                               vn[64 * r:64 * r + SEQ, hd, :],
                                               prob[n0 % 2][64 * r:64 * r + SEQ, c * 4 + j, :], start=True, stop=True)
                        mm.then_inc(t_ctx, 1)
                    else:
                        if n0 >= 1:
                            pe.wait_ge(t_ptc, n0)
                        for hd in range(HEADS):
                            mm = pe.transpose(PS[4 + hd // 4][0:SEQ, (hd % 4) * 128:(hd % 4) * 128 + 128],
                                              prob[n0 % 2][:, hd, :], ident[:, :])
                        mm.then_inc(t_ptr, 1)
                        pe.wait_ge(t_ptc, n0 + 1)
                        pe.wait_ge(t_ctxc, k)
                        for r in range(2):
                            for hd in range(HEADS):
                                c, j = divmod(hd, 4)
                                mm = pe.matmul(PS[7][32 * j:32 * j + 32, (r * NCH + c) * SEQ:(r * NCH + c) * SEQ + SEQ],
                                               v2[0:SEQ, 2 * n0 + r, hd, :], prob_T[:, hd, 64 * r:64 * r + SEQ],
                                               start=True, stop=True)
                        mm.then_inc(t_ctx, 1)
                pe.wait_ge(t_ctxc, (L + 1) * NPAIR)
                for g in range(NG):
                    k = L * NG + g
                    if k >= 2:
                        pe.wait_ge(t_oc, k - 1)
                    for c in range(NCH):
                        mm = pe.matmul(PS[g % 2][0:GT, 0:E], ctx_T[:, c, g * GT:g * GT + GT], wo[L][:, c, :],
                                       start=(c == 0), stop=(c == NCH - 1))
                    mm.then_inc(t_o, 1)

            pe.wait_ge(t_z, 2)
            transpose_tokens(0, h_tok)
            attention(0)
            transpose_tokens(1, x_tok)
            attention(1)
            transpose_tokens(2, x_tok)
            pe.wait_ge(t_trc, 3 * NG)
            pe.wait_ge(t_const, 16 * len(CONST))
            for g in range(NG):
                for c in range(2):
                    mm = pe.matmul(PS[0][0:GT, g * NE:g * NE + NE], x_T2[:, c, g * GT:g * GT + GT], wg[:, c, :],
                                   start=(c == 0), stop=(c == 1))
            mm.then_inc(t_lg, 1)
            pe.wait_ge(t_gate, 1)
            for g in range(NG):
                mm = pe.transpose(PS[1 + g // 4][0:NE, (g % 4) * GT:(g % 4) * GT + GT], gate[:, g, :], ident[0:GT, 0:GT])
            mm.then_inc(t_gt, 1)
            pe.wait_ge(t_gtc, 1)
            for g in range(NG):
                if g >= 2:
                    pe.wait_ge(t_b2c, g - 1)
                pe.matmul(PS[3 + g % 2][0:GT, 0:E], gate_T[:, g * GT:g * GT + GT], b2[:, :], start=True, stop=True)\
                    .then_inc(t_b2, 1)
            pe.wait_ge(t_b2c, NG)
            with pe.Fori(0, NE // 2) as i:
                for s in range(2):
                    pe.wait_ge(e_w[s], i * 48 + 48)
                    for n in range(2 * HC):
                        hc, h = n // 2, n % 2
                        pe.wait_ge(e_hg, i * (4 * HC) + (s * 2 * HC + n + 1))
                        for c in range(2):
                            mm = pe.matmul(PS[n % 4][:, 0:HT], w1[s][:, c, 128 * hc:128 * hc + 128],
                                           x_T2[:, c, h * HT:h * HT + HT], start=(c == 0), stop=(c == 1))
                        mm.then_inc(e_h, 1)
                    pe.wait_ge(e_hg, i * (4 * HC) + (s * 2 * HC + 2 * HC + 4))
                    for g in range(NG):
                        pe.wait_ge(e_yc, i * (2 * NG) + (s * NG + g + 1))
                        for hc in range(HC):
                            mm = pe.matmul(PS[4 + (s * NG + g) % 2][0:GT, 0:E], hid[:, hc, g * GT:g * GT + GT],
                                           w2[s][:, hc, :], start=(hc == 0), stop=(hc == HC - 1))
                        mm.then_inc(e_y, 1)

        @block.scalar
        def _(act):
            act.sem_inc(e_hg, 4)

            def tokens_out(n):
                for g in range(NG):
                    act.wait_ge(t_tr, n * NG + g + 1)
                    act.activation(x_T2[:, :, g * GT:g * GT + GT],
                                   PS[6 + g % 2][0:EK, 0:2 * GT].rearrange("p (k t) -> p k t", t=GT), ACT.Copy)\
                        .then_inc(t_trc, 1)

            def attention(L):
                n = 0
                for m in range(2):
                    for j in range(NCH):
                        for h in range(2):
                            act.wait_ge(t_qk, L * 12 + n + 1)
                            act.activation(qk_T[m][:, j * TOK + h * HT:j * TOK + h * HT + HT], PS[4 + n % 2][:, 0:HT],
                                           ACT.Identity, bias=bqk[L][:, m * NCH + j:m * NCH + j + 1]).then_inc(t_qkc, 1)
                            n += 1
                for n in range(NPAIR + 1):
                    if n < NPAIR:
                        k = L * NPAIR + n
                        act.wait_ge(t_sub, k + 1)
                        p = prob[n % 2][:, :, :]
                        act.activation(p, p, ACT.Exp, scale=DH ** -0.5).then_inc(t_exp, 1)
                    if n >= 1:
                        k, n0 = L * NPAIR + n - 1, n - 1
                        if L == 1:
                            act.wait_ge(t_ptr, n0 + 1)
                            for b in range(3):
                                cp = act.activation(prob_T[:, 4 * b:4 * b + 4, :],
                                                    PS[4 + b][0:SEQ, :].rearrange("p (h t) -> p h t", t=128), ACT.Copy)
                            cp.then_inc(t_ptc, 1)
                        act.wait_ge(t_ctx, k + 1)
                        for r in range(2):
                            src = PS[4 + r][:, 0:SC] if L == 0 else PS[7][:, r * SC:r * SC + SC]
                            t0 = (2 * n0 + r) * SEQ
                            cp = act.activation(ctx_T[:, :, t0:t0 + SEQ], src.rearrange("p (c t) -> p c t", t=SEQ), ACT.Copy)
                        cp.then_inc(t_ctxc, 1)

            tokens_out(0)
            attention(0)
            tokens_out(1)
            attention(1)
            tokens_out(2)
            act.wait_ge(t_ge, 1)
            act.activation(gg[:, 1, :], gg[:, 0, :], ACT.Exp).then_inc(t_ge, 1)
            act.wait_ge(t_gt, 1)
            act.activation(gate_T[:, 0:4 * GT], PS[1][0:NE, 0:4 * GT], ACT.Copy)
            act.activation(gate_T[:, 4 * GT:NG * GT], PS[2][0:NE, 0:3 * GT], ACT.Copy).then_inc(t_gtc, 1)
            with act.Fori(0, NE // 2) as i:
                for s in range(2):
                    act.wait_ge(e_used, i * 2 + (s + 2))
                    act.wait_ge(e_w[s], i * 48 + 48)
                    for n in range(2 * HC):
                        hc, h = n // 2, n % 2
                        act.wait_ge(e_h, i * (4 * HC) + (s * 2 * HC + n + 1))
                        act.activation(hid[:, hc, h * HT:h * HT + HT], PS[n % 4][:, 0:HT], ACT.Gelu,
                                       bias=b1[s][:, hc:hc + 1]).then_inc(e_hg, 1)

        @block.gpsimd
        def _(pool):
            for n in range(4):
                pool.wait_ge(t_var, n + 1)
                pool.tensor_tensor(ln_r[:, 1, :], ln_r[:, 0, :], expo[0:GT, 0:NG], ALU.pow).then_inc(t_rs, 1)

        @block.vector
        def _(dve):
            dn = [0]

            def link(ins):
                dn[0] += 1
                ins.then_inc(t_d, 1)
                dve.wait_ge(t_d, dn[0])

            lns = [0]

            def layernorm(dst, w=None):
                for g in range(NG):
                    ins = dve.bn_stats(ln_st[:, g, :], h_tok[:, g, :])
                link(ins)
                for g in range(NG):
                    ins = dve.bn_aggr(ln_mv[:, g, :], ln_st[:, g, :])
                link(ins)
                dve.tensor_scalar(ln_r[:, 0, :], ln_mv[:, :, 1], EPS, None, ALU.add).then_inc(t_var, 1)
                lns[0] += 1
                dve.wait_ge(t_rs, lns[0])
                for g in range(NG):
                    ins = dve.tensor_scalar(dst[:, g, :], h_tok[:, g, :], ln_mv[:, g, 0:1], ln_r[:, 1, g:g + 1],
                                            ALU.subtract, ALU.mult)
                link(ins)
                if w is not None:
                    wb, bb = (rows[0:GT, w + m:w + m + 1, :].to_broadcast([GT, NG, E]) for m in range(2))
                    link(dve.tensor_tensor(dst[:, :, :], dst[:, :, :], wb, ALU.mult))
                    link(dve.tensor_tensor(dst[:, :, :], dst[:, :, :], bb, ALU.add))

            def attention(L):
                for n in range(NPAIR):
                    dve.wait_ge(t_v, L * NPAIR + n + 1)
                    if L == 0:
                        dve.tensor_tensor(v1[:, n, :, 0:DH], PS[6 + n % 2][:, 0:E].rearrange("p (h d) -> p h d", d=DH),
                                          rows[:, 0, :].rearrange("p (h d) -> p h d", d=DH), ALU.add).then_inc(t_vc, 1)
                    else:
                        for r in range(2):
                            ins = dve.tensor_tensor(v2[:, 2 * n + r, :, 0:DH],
                                                    PS[6 + n % 2][0:64, r * E:r * E + E].rearrange("p (h d) -> p h d", d=DH),
                                                    rows[0:64, 1, :].rearrange("p (h d) -> p h d", d=DH), ALU.add)
                        ins.then_inc(t_vc, 1)
                for n in range(NPAIR):
                    k = L * NPAIR + n
                    dve.wait_ge(t_sc, k + 1)
                    p = prob[n % 2]
                    pj = p[:, :, :].rearrange("p (c j) t -> p j c t", j=4)
                    mj = mx[:, :].rearrange("p (c j) -> p j c", j=4)
                    for j in range(4):
                        ins = dve.tensor_reduce(mj[:, j, :], PS[j][:, 0:SC].rearrange("p (c t) -> p c t", t=SEQ), AX_X, ALU.max)
                    link(ins)
                    if k >= 2:
                        dve.wait_ge(t_ctx, k - 1)
                    for j in range(4):
                        ins = dve.tensor_tensor(pj[:, j], PS[j][:, 0:SC].rearrange("p (c t) -> p c t", t=SEQ),
                                                mj[:, j, :].unsqueeze(2).to_broadcast([128, NCH, SEQ]), ALU.subtract)
                    ins.then_inc(t_sub, 1)
                    dve.wait_ge(t_exp, k + 1)
                    link(dve.tensor_reduce(sm[:, :], p[:, :, :], AX_X, ALU.add))
                    link(dve.reciprocal(ri[:, :], sm[:, :]))
                    if L == 0:
                        if k >= 1:
                            dve.wait_ge(t_ctx, k)
                        dve.tensor_tensor(vn[:, :, :], v1[:, n, :, :], ri[:, :].unsqueeze(2).to_broadcast([128, HEADS, HPAD]),
                                          ALU.mult).then_inc(t_p, 1)
                    else:
                        dve.tensor_tensor(p[:, :, :], p[:, :, :], ri[:, :].unsqueeze(2).to_broadcast([128, HEADS, SEQ]),
                                          ALU.mult).then_inc(t_p, 1)
                for g in range(NG):
                    dve.wait_ge(t_o, L * NG + g + 1)
                    dve.tensor_tensor(h_tok[:, g, :], h_tok[:, g, :], PS[g % 2][0:GT, 0:E], ALU.add).then_inc(t_oc, 1)
                dve.wait_ge(t_oc, (L + 1) * NG)
                link(dve.tensor_tensor(h_tok[:, :, :], h_tok[:, :, :], rows[0:GT, 2 + L:3 + L, :].to_broadcast([GT, NG, E]),
                                       ALU.add))

            dve.memset(v1[:, :, :, :], 0.0).then_inc(t_z, 1)
            link(dve.memset(v2[:, :, :, :], 0.0))
            for t in (x_T[:, 2 * TOK:], qk_T[0][:, NCH * TOK:], qk_T[1][:, NCH * TOK:]):
                ins = dve.memset(t, 0.0)
            ins.then_inc(t_z, 1)
            dve.sem_inc(e_used, 2)
            dve.sem_inc(e_yc, 2)
            dve.wait_ge(t_z, 2)
            dve.wait_ge(t_const, 16 * len(CONST))
            dve.sem_inc(t_x, 1)
            attention(0)
            layernorm(h_tok)
            layernorm(x_tok, 4)
            dve.sem_inc(t_x, 1)
            dve.tensor_copy(h1_tok[:, :, :], h_tok[:, :, :]).then_inc(t_h1, 1)
            attention(1)
            layernorm(x_tok, 6)
            dve.sem_inc(t_x, 1)
            dve.wait_ge(t_h1, 1)
            link(dve.tensor_tensor(h_tok[:, :, :], h_tok[:, :, :], h1_tok[:, :, :], ALU.add))
            dve.wait_ge(t_lg, 1)
            link(dve.tensor_copy(lg[:, :, :].rearrange("p g e -> p (g e)"), PS[0][0:GT, 0:NG * NE]))
            for g in range(NG):
                ins = dve.max(top[:, g, :], lg[:, g, :])
            link(ins)
            for g in range(NG):
                ins = dve.max_index(topi[:, g, :], top[:, g, :], lg[:, g, :])
            link(ins)
            link(dve.tensor_copy(idx[:, :, :], topi[:, :, 0:2]))
            dve.tensor_tensor(gg[:, 0, :], top[:, :, 1], top[:, :, 0], ALU.subtract).then_inc(t_ge, 1)
            dve.wait_ge(t_ge, 2)
            link(dve.tensor_scalar(gg[:, 2, :], gg[:, 1, :], 1.0, None, ALU.add))
            link(dve.reciprocal(gg[:, 2, :], gg[:, 2, :]))
            link(dve.tensor_tensor(gg[:, 3, :], gg[:, 1, :], gg[:, 2, :], ALU.mult))
            for m, t in enumerate((gate, gtmp)):
                link(dve.tensor_tensor(t[:, :, :], iota[:, :].unsqueeze(1).to_broadcast([GT, NG, NE]),
                                       idx[:, :, m:m + 1].to_broadcast([GT, NG, NE]), ALU.is_equal))
                link(dve.tensor_tensor(t[:, :, :], t[:, :, :], gg[:, 2 + m, :].unsqueeze(2).to_broadcast([GT, NG, NE]),
                                       ALU.mult))
            dve.tensor_tensor(gate[:, :, :], gate[:, :, :], gtmp[:, :, :], ALU.add).then_inc(t_gate, 1)
            for g in range(NG):
                dve.wait_ge(t_b2, g + 1)
                dve.tensor_tensor(h_tok[:, g, :], h_tok[:, g, :], PS[3 + g % 2][0:GT, 0:E], ALU.add).then_inc(t_b2c, 1)
            dve.wait_ge(t_b2c, NG)
            dve.wait_ge(t_gate, 1)
            with dve.Fori(0, NE // 2) as i:
                for s in range(2):
                    for g in range(NG):
                        dve.wait_ge(e_y, i * (2 * NG) + (s * NG + g + 1))
                        dve.wait_ge(e_yc, i * (2 * NG) + (s * NG + 2))
                        dve.scalar_tensor_tensor(h_tok[:, g, :], PS[4 + (s * NG + g) % 2][0:GT, 0:E],
                                                 gate[:, g, bass.ds(i * 2 + s, 1)], h_tok[:, g, :], ALU.mult, ALU.add)\
                            .then_inc(e_yc, 1)
                    dve.sem_inc(e_used, 1)
            dve.wait_ge(e_yc, NE * NG + 2)
            layernorm(h_tok)
            dve.sem_inc(t_done, 1)


def laid_out(i):
    f = np.float32
    x = np.asarray(i["x"]).reshape(B, CIN, HP, P, HP, P).transpose(0, 2, 1, 4, 3, 5)
    r = {"x": x.reshape(GT, CIN, HP, PIX)}
    c1 = np.asarray(i["L0_tok_conv1_w"])
    r["c1"] = np.tile(c1.reshape(CH, IMR).T, (3, 2))
    r["cz"] = c1.reshape(CH, IMR)
    r["r1"] = np.asarray(i["L0_tok_rconv1_w"]).transpose(1, 2, 3, 0).reshape(CH, TAPS, CH)
    r2 = np.asarray(i["L0_tok_rconv2_w"])
    r["r2"] = r2[:, :, ::-1, ::-1].transpose(0, 2, 3, 1).reshape(CH, TAPS, CH)
    r["proj"] = np.asarray(i["L0_tok_proj_w"]).reshape(E, CH, PIX).transpose(1, 0, 2)
    names = ["conv1_b", "gn1_g", "gn1_b", "rconv1_b", "gn2_g", "gn2_b", "rconv2_b"]
    r["vecs"] = np.tile(np.stack([np.asarray(i["L0_tok_" + n]) for n in names], 1), (2, 1))
    r["ident"] = np.eye(128, dtype=f)
    ch = np.arange(128)
    pair = (ch[:, None] % CH) // 2 == (ch[None, :] % CH) // 2
    r["avg1"] = np.where(pair & (ch[:, None] // CH == ch[None, :] // CH), 0.25, 0.0).astype(f)
    r["avg2"] = np.where(pair, 0.125, 0.0).astype(f)
    at = np.arange(HP, dtype=f)
    lo = (at / f(HP) * f(VOCAB)).astype(np.int32)
    hi = ((at + 1) / f(HP) * f(VOCAB)).astype(np.int32)
    pos = (lo + hi) // 2
    r["emb_rows"] = np.concatenate([np.asarray(i["L0_tok_row_emb"])[pos], np.asarray(i["L0_tok_col_emb"])[pos],
                                    np.asarray(i["L0_tok_proj_b"])[None]])
    t = np.arange(TOK) % SEQ
    hot = np.zeros((2 * HP + 1, TOK), f)
    hot[t // HP, np.arange(TOK)] = 1
    hot[HP + t % HP, np.arange(TOK)] = 1
    hot[2 * HP] = 1
    r["onehot"] = hot
    def pad_heads(w):
        o = np.zeros((*w.shape[:-1], HEADS, HPAD), f)
        o[..., :DH] = w.reshape(*w.shape[:-1], HEADS, DH)
        return o.reshape(*w.shape[:-1], HEADS * HPAD)

    def two(w):
        return w.reshape(2, EK, w.shape[-1]).transpose(1, 0, 2)

    qkv = np.asarray(i["L0_ffn_qkv_w"]).reshape(3, E, E)
    qkvb = np.asarray(i["L0_ffn_qkv_b"]).reshape(3, E)
    w = [[np.asarray(i[f"L0_attn_W{n}"]).transpose(1, 0, 2).reshape(E, E) for n in "qkv"], [m.T for m in qkv]]
    bias = [[np.asarray(i[f"L0_attn_b{n}"]).reshape(E) for n in "qkv"], list(qkvb)]
    wo = [np.asarray(i["L0_attn_Wo"]), np.asarray(i["L0_ffn_proj_w"]).T]
    for L in range(2):
        r[f"wq{L}"], r[f"wk{L}"] = two(pad_heads(w[L][0])), two(pad_heads(w[L][1]))
        r[f"wv{L}"] = two(w[L][2])
        r[f"wo{L}"] = pad_heads(wo[L].T).T.reshape(NCH, 128, E).transpose(1, 0, 2)
        r[f"bqk{L}"] = np.concatenate([pad_heads(b[None]).reshape(NCH, 128).T for b in bias[L][:2]], 1)
    rows = [bias[0][2], bias[1][2], i["L0_attn_bo"], i["L0_ffn_proj_b"], i["L0_ffn_norm1_w"], i["L0_ffn_norm1_b"],
            i["L0_ffn_norm2_w"], i["L0_ffn_norm2_b"]]
    r["rows"] = np.tile(np.stack([np.asarray(v) for v in rows])[None], (128, 1, 1))
    r["wg"] = two(np.asarray(i["L0_ffn_w_gate"]))
    r["w1"] = np.asarray(i["L0_ffn_W1"]).reshape(NE, 2, EK, HID).transpose(0, 2, 1, 3)
    r["w2"] = np.asarray(i["L0_ffn_W2"]).reshape(NE, HC, 128, E).transpose(0, 2, 1, 3)
    r["b1"] = np.asarray(i["L0_ffn_b1"]).reshape(NE, HC, 128).transpose(0, 2, 1)
    r["b2"] = np.asarray(i["L0_ffn_b2"])
    r["iota"] = np.tile(np.arange(NE, dtype=f), (GT, 1))
    return {k: np.ascontiguousarray(v) for k, v in r.items()}


def kernel(**inputs):
    import concourse.bacc as bacc
    from concourse.bass_utils import run_bass_kernel_spmd

    nc = bacc.Bacc("TRN2", target_bir_lowering=False, num_devices=1)
    arrays = laid_out(inputs)
    a = {k: nc.dram_tensor("in_" + k, v.shape, mybir.dt.from_np(v.dtype), kind="ExternalInput").ap()
         for k, v in arrays.items()}
    out = nc.dram_tensor("out", (TOK, E), F32, kind="ExternalOutput").ap()
    build(nc, a, out)
    r = run_bass_kernel_spmd(nc, [{"in_" + k: v for k, v in arrays.items()}], core_ids=[0])
    return r.results[0]["out"].reshape(B, SEQ, E)
```

```python
from contextlib import ExitStack

import concourse.bass as bass
import numpy as np
from concourse import mybir

F32 = mybir.dt.float32
F16 = mybir.dt.float16
U32 = mybir.dt.uint32
ALU = mybir.AluOpType
ACT = mybir.ActivationFunctionType
AX_X = mybir.AxisListType.X

B, CIN, HW, P = 16, 3, 112, 16
HP = HW // P
SEQ = HP * HP
TOK = B * SEQ
GT = B * HP
NG = TOK // GT
PIX = P * P
PAD = P + 2
PP = PAD * PAD
CH = 64
E = 192
EK = E // 2
QN = 4
NBAT = 2 * QN
QUADS = TOK // QN
GQ = GT // QN
RING = 4
AHEAD = 3
WBAT = E // NBAT
HALF = PIX // 2
TAPS = 9
IMR = CIN * TAPS
IML = NBAT * PP - 2 * PAD - 2
S = 16.0
EPS = 1e-5
VOCAB = 256
KQ = CIN * 2
HEADS, DH = 12, 16
HPAD = 32
NCH = HEADS * HPAD // 128
NPAIR = B // 2
SC = NCH * SEQ
NE, HID = 8, 768
HC = HID // 128
HT = TOK // 2


def build(nc, a, out):
    with ExitStack() as ctx:
        def sb(name, shape, dt=F32):
            return ctx.enter_context(nc.sbuf_tensor(name, shape, dt))

        def ps(name, shape):
            return ctx.enter_context(nc.psum_tensor(name, shape, F32))

        h_tok = sb("h_tok", [GT, NG, E])
        ident = sb("ident", [128, 128])
        expo = sb("expo", [128, 32])
        PS = [ps(f"bank{i}", [128, 512]) for i in range(8)]
        tokenizer(nc, a, h_tok, ident, expo, PS)
        tower(nc, a, out, h_tok, ident, expo, PS)


def tokenizer(nc, a, h_tok, ident, expo, PS):
    with ExitStack() as ctx:
        def sb(name, shape, dt=F32):
            return ctx.enter_context(nc.sbuf_tensor(name, shape, dt))

        def sem(name):
            return ctx.enter_context(nc.semaphore(name))

        xh_dram = nc.dram_tensor("xh_dram", [CIN, TOK * PP], F16, kind="Internal").ap()
        xl_dram = nc.dram_tensor("xl_dram", [CIN, TOK * PP], F16, kind="Internal").ap()
        z_dram = nc.dram_tensor("z_dram", [IMR, E, PP], F32, kind="Internal").ap()

        big = sb("big", [128, HALF * E])
        mid = sb("mid", [128, GT * HALF])
        wc = big[:, :].bitcast(F16).rearrange("p (q m e) -> p q m e", m=2, e=E)
        g2_h = mid[:, 0:GT * HALF // 2].bitcast(F16).rearrange("p (q n) -> p q n", n=GT)
        g2_l = mid[:, GT * HALF // 2:GT * HALF].bitcast(F16).rearrange("p (q n) -> p q n", n=GT)

        CW = CIN * HP
        XA = 12
        o = 0
        x_raw = big[0:GT, o:o + CW * PIX].rearrange("p (c q) -> p c q", q=PIX); o += CW * PIX
        x_n = big[0:GT, o:o + CW * PIX].rearrange("p (c q) -> p c q", q=PIX); o += CW * PIX
        x_h = big[0:GT, o:o + CW * PP // 2].bitcast(F16); o += CW * PP // 2
        x_l = big[0:GT, o:o + CW * PP // 2].bitcast(F16)
        x_hp = x_h.rearrange("p (c r q) -> p c r q", r=PAD, q=PAD)
        x_lp = x_l.rearrange("p (c r q) -> p c r q", r=PAD, q=PAD)

        o = 0
        xnT = mid[:, o:o + KQ * TOK].rearrange("p (k t) -> p k t", t=TOK); o += KQ * TOK
        z_in = mid[0:EK, o:o + IMR * PP].rearrange("p (t r q) -> p t r q", r=PAD, q=PAD)
        assert o + IMR * PP <= GT * HALF
        proj_in = []
        for i in range(2):
            proj_in.append(mid[:, o:o + NBAT * PIX].rearrange("p (n q) -> p n q", q=PIX)); o += NBAT * PIX
        z_pad = []
        for i in range(2):
            z_pad.append(mid[0:IMR, o:o + NBAT * PP].rearrange("p (n r q) -> p n r q", r=PAD, q=PAD)); o += NBAT * PP
        assert o <= GT * HALF

        img = [sb(f"img{i}", [128, NBAT, PAD, PAD], F16) for i in range(2)]
        im2 = [sb(f"im2_{i}", [3 * IMR, NBAT, PAD, PAD], F16) for i in range(2)]
        g1 = [sb(f"g1_{i}", [128, QN, PIX]) for i in range(2)]
        g2b = sb("g2b", [128, RING, QN, HALF])
        g2 = [g2b[:, i] for i in range(RING)]
        g1_0, g1_1 = (g[:, :, :].rearrange("p a b -> p (a b)") for g in g1)
        g2_flat = g2b[:, :, :, :].rearrange("p a b c -> p (a b c)")
        v_t = g1_0[0:EK, 0:CIN * PIX].rearrange("p (a q) -> p a q", q=PIX)
        v_sb = g2_flat[:, TOK:TOK + KQ * E].rearrange("p (k e) -> p k e", e=E)
        w_f = g1_0[:, 0:TAPS * CH].rearrange("p (t c) -> p t c", c=CH)
        w_f2 = g1_1[:, 0:TAPS * CH].rearrange("p (t c) -> p t c", c=CH)
        onehot = g2_flat[0:2 * HP + 1, 0:TOK]
        emb_rows = g1_1[0:2 * HP + 1, TAPS * CH:TAPS * CH + E]

        r1_h, r1_l = sb("r1_h", [128, TAPS, CH], F16), sb("r1_l", [128, TAPS, CH], F16)
        r2_h, r2_l = sb("r2_h", [128, TAPS, CH], F16), sb("r2_l", [128, TAPS, CH], F16)
        c1_f = sb("c1_f", [3 * IMR, 128])
        c1_w, c1_l = sb("c1_w", [3 * IMR, 128], F16), sb("c1_l", [3 * IMR, 128], F16)
        cz_f = sb("cz_f", [128, IMR])
        cz_h, cz_l = sb("cz_h", [128, IMR], F16), sb("cz_l", [128, IMR], F16)
        vecs = sb("vecs", [128, 7])
        zeros = sb("zeros", [128, 2 * QN])
        sbias = sb("sbias", [128, 2, 2 * QN])
        nbias = sb("nbias", [128, 2, QN])
        gamma, beta = sb("gamma", [128, 2, QN]), sb("beta", [128, 2, QN])
        per_n = sb("per_n", [128, 2, 2 * QN])
        bb = sb("bb", [CH, 1])
        bbr = sb("bbr", [CH, GT])
        avg = [sb("avg1", [128, 128]), sb("avg2", [128, 128])]
        psum_w = sb("psum_w", [CH, E])

        st0 = sb("st0", [GT, CW, 6])
        m0 = sb("m0", [GT, 6, CW])
        st = [sb(f"stat{i}", [128, 2, QN, 6]) for i in range(2)]
        rr = sb("rr", [128, 2, 2, 2 * QN])
        rs = sb("rs", [128, 2, 2, QN])
        sq, m2n = sb("sq", [128, 2, 2 * QN]), sb("m2n", [128, 2, 2 * QN])
        ms = sb("ms", [128, 2, 2, QN])
        vv = sb("vv", [128, 5, 2, QN])
        gn = [sb(f"gn{i}", [128, 2, 2, QN]) for i in range(2)]
        acc_tmp = sb("acc_tmp", [GT, E])

        c1p = [PS[0:2], PS[2:4]]
        cab = [PS[4], PS[5]]
        accp, stp = PS[6], PS[7]

        s_x = [sem(f"s_x{c}") for c in range(CIN)]; s_xc = sem("s_xc"); s_const = sem("s_const"); s_r1 = sem("s_r1")
        s_w = sem("s_w"); s_c1l = sem("s_c1l"); s_exp = sem("s_exp"); s_bb = sem("s_bb"); s_w2 = sem("s_w2")
        s_d0 = sem("s_d0"); s_p0 = sem("s_p0"); s_xn = sem("s_xn"); s_xz = sem("s_xz"); s_xh = sem("s_xh")
        s_xs = sem("s_xs"); s_xst = sem("s_xst"); s_tr = sem("s_tr"); s_trc = sem("s_trc"); s_imz = sem("s_imz")
        w_in = [sem("w_in0"), sem("w_in1")]; w_sc = sem("w_sc"); w_hi = sem("w_hi"); w_split = sem("w_split")
        w_free = sem("w_free"); w_z = sem("w_z"); w_zc = sem("w_zc"); w_zcp = sem("w_zcp"); w_zst = [sem("w_zst0"), sem("w_zst1")]
        w_conv = sem("w_conv"); w_evh = sem("w_evh"); w_evl = sem("w_evl")
        v_in = [sem(f"v_in{c}") for c in range(CIN)]; v_sum = sem("v_sum"); v_d = sem("v_d"); v_acc = sem("v_acc"); v_accc = sem("v_accc"); v_tr = sem("v_tr"); v_trc = sem("v_trc")
        s_res = sem("s_res"); s_resc = sem("s_resc")
        im_in = [sem("im_in0"), sem("im_in1")]; p_c1 = sem("p_c1"); p_gelu1 = sem("p_gelu1"); p_h1 = sem("p_h1")
        p_img = sem("p_img"); p_conv = sem("p_conv"); p_gelu2 = sem("p_gelu2"); p_h2 = sem("p_h2")
        p_g2 = sem("p_g2")
        p_raw = sem("p_raw")
        p_bn = sem("p_bn")
        p_r = sem("p_r")
        p_av = sem("p_av")
        p_avc = sem("p_avc")
        p_var = sem("p_var")
        p_pow = sem("p_pow")
        p_gn = sem("p_gn")
        p_acc = sem("p_acc"); p_accc = sem("p_accc"); chain_m = sem("chain_m"); chain_c = sem("chain_c"); s_zero = sem("s_zero")

        block = ctx.enter_context(nc.Block())
        CONST = [
            (vecs[:], a["vecs"]), (ident[:], a["ident"]), (avg[0][:], a["avg1"]), (avg[1][:], a["avg2"]),
            (c1_f[:], a["c1"]), (onehot, a["onehot"]), (emb_rows, a["emb_rows"]),
            (cz_f[0:CH], a["cz"]), (cz_f[CH:128], a["cz"]),
            (w_f[0:CH], a["r2"]), (w_f[CH:128], a["r2"]), (w_f2[0:CH], a["r1"]), (w_f2[CH:128], a["r1"]),
        ]
        NCONST = 16 * len(CONST)

        def conv(pe, slot, q, bank, wh, wl, lo, hi):
            for n in range(lo, hi):
                w = (wh, wl)[n // TAPS]
                t = n % TAPS
                dy, dx = divmod(t, 3)
                for h in range(2):
                    last = pe.matmul(bank[CH * h:CH * h + CH, :], w[:, t, :],
                                     img[slot][:, QN * q:QN * q + QN, dy + 8 * h:dy + 8 * h + 8, dx:dx + P],
                                     start=(n == 0), stop=(n == 2 * TAPS - 1))
            return last

        def schedule(eng, steps):
            steps(0, first=True)
            with eng.Fori(1, NG) as r:
                steps(r)
            with eng.Fori(1, NG - 1) as g:
                steps(g * 7, done=g)
                with eng.Fori(1, 7) as r:
                    steps(g * 7 + r)
            steps(7 * (NG - 1), done=NG - 1)
            with eng.Fori(1, 6) as r:
                steps(r + 7 * (NG - 1))
            steps(7 * NG - 1, last=True)

        V_ORDER = [(0, 1), (0, 0), (0, 2), (1, 1), (1, 0), (1, 2)]

        def shifted(c, t):
            dy, dx = divmod(t, 3)
            return z_in[:, c * TAPS + t, 2 - dy:2 - dy + P, 2 - dx:2 - dx + P]

        def interior(t):
            return t[:, :, 1:1 + P, 1:1 + P]

        @block.sync
        def _(sp):
            for c in range(CIN):
                sp.dma_start(x_raw[:, c * HP:(c + 1) * HP, :], a["x"][:, c]).then_inc(s_x[c], 16)
            for dst, src in CONST:
                sp.dma_start(dst, src).then_inc(s_const, 16)
            sp.wait_ge(s_w, 8)
            sp.dma_start(c1_w[2 * IMR:3 * IMR, :], c1_l[2 * IMR:3 * IMR, :]).then_inc(s_c1l, 16)
            with sp.Fori(0, WBAT // 2) as i:
                for s in range(2):
                    sp.wait_ge(w_free, i * 2 + (s + 1))
                    sp.wait_ge(w_split, i * 2 + (s + 1))
                    for h in range(2):
                        sp.dma_start(proj_in[s][CH * h:CH * h + CH],
                                     a["proj"][:, bass.ds(i * (2 * NBAT) + s * NBAT, NBAT), :]).then_inc(w_in[s], 16)

            def im_load(b, s):
                for j, t in enumerate((xh_dram, xl_dram, xh_dram)):
                    for c in range(CIN):
                        at = t[c, bass.ds(b * (NBAT * PP), IML)]
                        src = bass.AP(at.tensor, at.offset, [[PAD, 3], [1, 3], [1, IML]])
                        r0 = j * IMR + c * TAPS
                        dst = im2[s][r0:r0 + TAPS].rearrange("p n r q -> p (n r q)")[:, 0:IML]
                        sp.dma_start(dst, src).then_inc(im_in[s], 16)

            sp.wait_ge(s_xst, 6 * 16)
            im_load(0, 0)
            im_load(1, 1)
            for s in range(2):
                sp.wait_ge(w_zst[s], 16 * (WBAT // 2) + 16)
            sp.wait_ge(w_free, WBAT + 2)
            sp.wait_ge(w_split, WBAT + 2)
            for h in range(2):
                for c, before, n in ((1, v_sum, 1), (0, v_acc, 1), (2, v_sum, 2)):
                    if h:
                        sp.wait_ge(before, n)
                    sp.dma_start(z_in[:, c * TAPS:(c + 1) * TAPS].rearrange("p t r q -> p t (r q)"),
                                 z_dram[c * TAPS:(c + 1) * TAPS, h * EK:(h + 1) * EK, :].rearrange("t e q -> e t q"))\
                        .then_inc(v_in[c], 16)
            with sp.Fori(0, QUADS // 4 - 1) as i:
                for s in range(2):
                    sp.wait_ge(p_c1, i * 4 + (2 * s + 2))
                    im_load(i * 2 + (s + 2), s)

        @block.tensor
        def _(pe):
            pe.wait_ge(s_const, NCONST)
            n = 0
            for w in range(HP):
                for k in range(KQ):
                    bank = PS[(n // 4) % 4]
                    if n == 0:
                        pe.wait_ge(s_xn, CW)
                    if n % 4 == 0 and n >= 16:
                        pe.wait_ge(s_trc, n // 4 - 3)
                    c, hh = divmod(k, 2)
                    mm = pe.transpose(bank[:, (n % 4) * GT:(n % 4) * GT + GT],
                                      x_n[:, c * HP + w, hh * 128:hh * 128 + 128], ident[0:GT, 0:GT])
                    n += 1
                    if n % 4 == 0 or n == HP * KQ:
                        mm.then_inc(s_tr, 1)
            pe.wait_ge(s_w, 8)
            pe.wait_ge(s_trc, (HP * KQ + 3) // 4)
            with pe.Fori(0, WBAT // 2) as i:
                for s in range(2):
                    k1 = i * 2 + (s + 1)
                    pe.wait_ge(w_split, k1 + 2)
                    pe.wait_ge(w_zc, k1)
                    for q in range(2):
                        for h in range(2):
                            for m, w in enumerate((cz_h, cz_l)):
                                mm = pe.matmul(PS[2 * q + h][0:IMR, :], w[:, :],
                                               img[s][:, QN * q:QN * q + QN, 1 + 8 * h:9 + 8 * h, 1:1 + P],
                                               start=(m == 0), stop=(m == 1))
                    mm.then_inc(w_z, 1)
                    for q in range(2):
                        pe.wait_ge(w_evl, i * 4 + (2 * s + q + 1))
                        conv(pe, s, q, cab[q], r2_h, r2_l, 0, 2 * TAPS).then_inc(w_conv, 1)
            def v_accumulate(h):
                pe.wait_ge(v_in[0], 16 * h + 16)
                if h:
                    pe.wait_ge(v_accc, h)
                for t in range(TAPS):
                    mm = pe.matmul(PS[6][0:EK, 0:PIX], ident[0:EK, 0:EK], shifted(0, t), start=(t == 0), stop=(t == TAPS - 1))
                mm.then_inc(v_acc, 1)

            v_accumulate(0)
            for k, (h, c) in enumerate(V_ORDER):
                if k == 2:
                    v_accumulate(1)
                if c == 0:
                    pe.wait_ge(v_accc, h + 1)
                else:
                    pe.wait_ge(v_sum, 2 * h + c)
                if k >= 2:
                    pe.wait_ge(v_trc, k - 1)
                for hh in range(2):
                    mm = pe.transpose(PS[k % 2][:, hh * EK:hh * EK + EK], v_t[:, c, hh * 128:hh * 128 + 128],
                                      ident[0:EK, 0:EK])
                mm.then_inc(v_tr, 1)
            pe.wait_ge(v_trc, 2 * CIN)
            pe.wait_ge(s_bb, 1)
            for g in range(NG):
                bank = PS[2 + g % 2]
                if g >= 2:
                    pe.wait_ge(s_resc, g - 1)
                tk = slice(g * GT, g * GT + GT)
                for k in range(KQ):
                    pe.matmul(bank[0:GT, 0:E], xnT[:, k, tk], v_sb[:, k, :], start=(k == 0), stop=False)
                pe.matmul(bank[0:GT, 0:E], bbr[:, :], psum_w[:, :], start=False, stop=False)
                pe.matmul(bank[0:GT, 0:E], onehot[:, tk], emb_rows, start=False, stop=True).then_inc(s_res, 1)

            pe.wait_ge(s_c1l, 16)
            pe.wait_ge(s_resc, NG)

            def conv1(v, j, load):
                if j % 2 == 0:
                    pe.wait_ge(im_in[j // 2], load * 144 + 144)
                pe.wait_ge(p_gelu1, v + 1)
                for b in range(2):
                    mm = pe.matmul(c1p[j % 2][b][:, :], c1_w[:, :],
                                   im2[j // 2][:, QN * (j % 2) + 2 * b:QN * (j % 2) + 2 * b + 2, 0:P, 0:P],
                                   start=True, stop=True)
                mm.then_inc(p_c1, 1)

            def average(b, later=True):
                pe.wait_ge(p_r, b + 1)
                if later:
                    pe.wait_ge(p_avc, b)
                for L in range(2):
                    mm = pe.matmul(stp[:, L * 2 * QN:(L + 1) * 2 * QN], avg[L][:, :],
                                   rs[:, L].rearrange("p a n -> p (a n)"), start=True, stop=True)
                mm.then_inc(p_av, 1)

            def product(g):
                pe.wait_ge(p_g2, g * GQ + RING)
                if not isinstance(g, int) or g > 1:
                    pe.wait_ge(p_accc, g - 1)
                for q in range(HALF):
                    pe.matmul(accp[0:GT, 0:2 * E], g2_h[:, q, :], wc[:, q, :, :], start=(q == 0),
                              stop=(q == HALF - 1), skip_group_check=True)
                    mm = pe.matmul(accp[0:GT, 0:E], g2_l[:, q, :], wc[:, q, 0, :], start=False,
                                   stop=(q == HALF - 1), skip_group_check=True)
                mm.then_inc(p_acc, 1)

            def pe_steps(i, first=False, last=False, done=None):
                for j in range(RING):
                    u = i * 4 + j
                    v = i * 4 + (j + AHEAD)
                    nxt = not (last and j >= 1)
                    if nxt:
                        conv1(v, (j + AHEAD) % 4, i + (j + AHEAD) // 4)
                    pe.wait_ge(p_img, i * 4 + (j + 3))
                    pe.wait_ge(p_raw, i * 4 + (j + 1))
                    sl, q, bank = j // 2, j % 2, cab[j % 2]
                    conv(pe, sl, q, bank, r1_h, r1_l, 0, 2 * TAPS).then_inc(p_conv, 1)
                    average(v)
                    if j == 2 and done is not None:
                        product(done)

            for v in range(AHEAD):
                conv1(v, v, 0)
                average(v, v > 0)
            schedule(pe, pe_steps)
            average(QUADS + AHEAD)
            product(NG)

        @block.scalar
        def _(act):
            act.wait_ge(s_imz, 4)
            act.sem_inc(w_zc, 1)
            act.sem_inc(p_gelu1, 2)
            act.sem_inc(p_raw, 2)
            act.wait_ge(s_xc, 1)
            for c in range(XA):
                act.activation(x_n[:, c, :], x_raw[:, c, :], ACT.Identity, bias=m0[:, 4, c:c + 1],
                               scale=m0[:, 5, c:c + 1]).then_inc(s_xn, 1)
            act.wait_ge(s_xn, CW)
            act.wait_ge(s_xz, 2)
            x_n4 = x_n.rearrange("p c (r q) -> p c r q", q=P)
            act.activation(interior(x_hp), x_n4, ACT.Copy).then_inc(s_xh, 1)
            for r in range((HP * KQ + 3) // 4):
                act.wait_ge(s_tr, r + 1)
                for n in range(4 * r, min(4 * r + 4, HP * KQ)):
                    w, k = divmod(n, KQ)
                    cp = act.activation(xnT[:, k, :].rearrange("p (t w) -> p t w", w=HP)[:, :, w],
                                        PS[r % 4][:, (n % 4) * GT:(n % 4) * GT + GT], ACT.Copy)
                cp.then_inc(s_trc, 1)
            act.wait_ge(s_xh, 1)
            act.wait_ge(s_xs, 2)
            for c in range(CIN):
                for src, dst in ((x_h, xh_dram), (x_l, xl_dram)):
                    act.dma_start(dst[c, :].rearrange("(p q) -> p q", p=GT),
                                 src[:, c * HP * PP:(c + 1) * HP * PP]).then_inc(s_xst, 16)
            with act.Fori(0, WBAT // 2) as i:
                for s in range(2):
                    act.wait_ge(w_z, i * 2 + (s + 1))
                    act.wait_ge(w_zst[s], i * 16 + 16)
                    for q in range(2):
                        for h in range(2):
                            cp = act.activation(z_pad[s][:, QN * q:QN * q + QN, 1 + 8 * h:9 + 8 * h, 1:1 + P],
                                                PS[2 * q + h][0:IMR, :].rearrange("p (n r c) -> p n r c", n=QN, r=8),
                                                ACT.Copy)
                            cp.then_inc(w_zcp, 1)
                    act.wait_ge(w_zcp, i * 8 + (4 * s + 4))
                    act.sem_inc(w_zc, 1)
                    act.dma_start(z_dram[:, bass.ds(i * (2 * NBAT) + s * NBAT, NBAT), :],
                                  z_pad[s].rearrange("p n r c -> p n (r c)")).then_inc(w_zst[s], 16)
                    for q in range(2):
                        act.wait_ge(w_conv, i * 4 + (2 * s + q + 1))
                        act.wait_ge(s_xst, 6 * 16)
                        act.activation(wc[:, :, 0, bass.ds(i * (2 * NBAT) + (s * NBAT + QN * q), QN)],
                                       cab[q][:, :].rearrange("p (n q) -> p q n", n=QN), ACT.Copy).then_inc(w_evh, 1)
            def v_copy(h):
                act.wait_ge(v_acc, h + 1)
                if h:
                    act.wait_ge(v_tr, 2)
                act.activation(v_t[:, 0, :], PS[6][0:EK, 0:PIX], ACT.Copy).then_inc(v_accc, 1)

            v_copy(0)
            for k, (h, c) in enumerate(V_ORDER):
                if k == 2:
                    v_copy(1)
                act.wait_ge(v_tr, k + 1)
                for hh in range(2):
                    cp = act.activation(v_sb[:, 2 * c + hh, h * EK:h * EK + EK], PS[k % 2][:, hh * EK:hh * EK + EK],
                                        ACT.Copy, scale=1.0 / (S * S))
                cp.then_inc(v_trc, 1)

            def gelu(L, w, j):
                b = w + (0, AHEAD + 1)[L]
                act.wait_ge(p_gn, b + 1)
                if L == 0:
                    act.wait_ge(p_img, w + 1)
                for n in range(QN):
                    coef = gn[j % 2][:, :, L]
                    if L == 0:
                        src = c1p[j % 2][n // 2][:, (n % 2) * PIX:(n % 2) * PIX + PIX]
                        dst = g1[j % 2][:, n, :]
                    else:
                        src = dst = g2[j][:, n, :]
                    op = act.activation(dst, src, ACT.Gelu, bias=coef[:, 1, n:n + 1], scale=coef[:, 0, n:n + 1])
                op.then_inc((p_gelu1, p_gelu2)[L], 1)

            def raw(w, j):
                act.wait_ge(p_conv, w + 1)
                act.wait_ge(p_g2, w + 1)
                act.activation(g2[j].rearrange("p n q -> p (n q)"), cab[j % 2][:, :], ACT.Copy).then_inc(p_raw, 1)

            def high1(w, j):
                act.wait_ge(p_gelu1, w + 3)
                act.activation(interior(img[j // 2][:, QN * (j % 2):QN * (j % 2) + QN]),
                               g1[j % 2][:, :, :].rearrange("p n (r q) -> p n r q", q=P), ACT.Copy)\
                    .then_inc(p_h1, 1)

            def act_steps(i, first=False, last=False, done=None):
                for j in range(RING):
                    u = i * 4 + j
                    if not (first and j == 0):
                        raw(i * 4 + (j - 1), (j - 1) % 4)
                    if not (first and j <= 2):
                        gelu(1, i * 4 + (j - 3), (j - 3) % 4)
                    if not (last and j == 3):
                        high1(u + 1, (j + 1) % 4)
                    if not (last and j >= 2):
                        gelu(0, u + 2, (j + 2) % 4)

            gelu(0, 0, 0)
            high1(0, 0)
            gelu(0, 1, 1)
            schedule(act, act_steps)
            raw(QUADS - 1, 3)
            gelu(1, QUADS - 3, 1)
            gelu(1, QUADS - 2, 2)
            gelu(1, QUADS - 1, 3)

        @block.vector
        def _(dve):
            def memzero(t):
                return dve.memset(t, 0.0)
            for i in range(2):
                dve.memset(img[i][:, :, :, :].rearrange("p n r q -> p (n r q)").bitcast(U32), 0).then_inc(s_imz, 1)
            dve.memset(expo[:, 0:8], -0.5).then_inc(s_exp, 1)
            dve.memset(expo[:, 8:32], 0.5).then_inc(s_exp, 1)
            dve.sem_inc(w_free, 2)
            dve.sem_inc(w_split, 2)
            dve.sem_inc(w_evl, 2)
            for s in range(2):
                dve.sem_inc(w_zst[s], 16)
            dve.sem_inc(p_img, 2)
            dve.sem_inc(p_g2, RING)
            dn = [0]

            def d_link(ins):
                dn[0] += 1
                ins.then_inc(s_d0, 1)
                dve.wait_ge(s_d0, dn[0])

            for c in range(CW):
                if c % HP == 0:
                    dve.wait_ge(s_x[c // HP], 16)
                ins = dve.bn_stats(st0[:, c, :], x_raw[:, c, :])
            d_link(ins)
            me, mo, qe, qo = st0[:, :, 1], st0[:, :, 4], st0[:, :, 2], st0[:, :, 5]
            d_link(dve.tensor_tensor(m0[:, 0, :], me, mo, ALU.add))
            d_link(dve.tensor_scalar(m0[:, 0, :], m0[:, 0, :], 0.5, None, ALU.mult))
            d_link(dve.tensor_tensor(m0[:, 1, :], me, mo, ALU.subtract))
            d_link(dve.tensor_tensor(m0[:, 1, :], m0[:, 1, :], m0[:, 1, :], ALU.mult))
            d_link(dve.tensor_tensor(m0[:, 2, :], qe, qo, ALU.add))
            d_link(dve.scalar_tensor_tensor(m0[:, 2, :], m0[:, 1, :], PIX / 4.0, m0[:, 2, :], ALU.mult, ALU.add))
            dve.tensor_scalar(m0[:, 2, :], m0[:, 2, :], 1.0 / (PIX - 1), None, ALU.mult).then_inc(s_p0, 1)
            for i in range(2):
                dve.memset(z_pad[i].rearrange("p n r q -> p (n r q)"), 0.0).then_inc(s_imz, 1)
            dve.wait_ge(s_p0, 2)
            d_link(dve.tensor_scalar(m0[:, 4, :], m0[:, 3, :], 1e-6, 4.0, ALU.add, ALU.mult))
            d_link(dve.reciprocal(m0[:, 5, :], m0[:, 4, :]))
            d_link(dve.scalar_tensor_tensor(m0[:, 4, :], m0[:, 0, :], -1.0, m0[:, 5, :], ALU.mult, ALU.mult))
            dve.sem_inc(s_xc, 1)
            for c in range(XA, CW):
                dve.tensor_scalar(x_n[:, c, :], x_raw[:, c, :], m0[:, 5, c:c + 1], m0[:, 4, c:c + 1], ALU.mult, ALU.add)\
                    .then_inc(s_xn, 1)
            dve.wait_ge(s_const, NCONST)
            wn = [0]

            def w_link(ins):
                wn[0] += 1
                ins.then_inc(s_w2, 1)
                dve.wait_ge(s_w2, wn[0])

            for f, hi, lo in ((w_f, r2_h[:, :, :], r2_l[:, :, :]), (w_f2, r1_h[:, :, :], r1_l[:, :, :]),
                              (c1_f[:, :], c1_w[:, :], c1_l[:, :]), (cz_f[:, :], cz_h[:, :], cz_l[:, :])):
                w_link(dve.tensor_scalar(f, f, S, None, ALU.mult))
                w_link(dve.tensor_copy(hi, f))
                dve.tensor_tensor(lo, f, hi, ALU.subtract).then_inc(s_w, 2)
            dve.memset(zeros[:, :], 0.0).then_inc(s_zero, 1)
            for i in range(2):
                dve.memset(st[i][:, :, :, :].rearrange("p a b c -> p (a b c)"), 0.0).then_inc(s_zero, 1)
            dve.wait_ge(s_zero, 3)
            for L in range(2):
                for dst, src, f, w in ((sbias, 0, S, 2 * QN), (nbias, 0, -S, QN), (gamma, 1, 1.0, QN), (beta, 2, 1.0, QN)):
                    dve.tensor_scalar(dst[:, L, :], zeros[:, 0:w], vecs[:, 3 * L + src:3 * L + src + 1], f,
                                      ALU.add, ALU.mult).then_inc(s_zero, 1)
                dve.memset(per_n[:, L, :], 2.0 / (PIX if L == 0 else HALF)).then_inc(s_zero, 1)
            w_link(dve.tensor_tensor(bb[:, :], vecs[0:CH, 0:1], vecs[0:CH, 6:7], ALU.add))
            w_link(dve.memset(bbr[:, :], 1.0 / S))
            w_link(dve.tensor_scalar(bbr[:, :], bbr[:, :], bb[:, 0:1], None, ALU.mult))
            dve.wait_ge(s_imz, 4)

            def split_rows(k, s, i, n):
                rows = proj_in[s].rearrange("p n (r q) -> p n r q", q=P)
                dve.wait_ge(w_in[s], n * 32 + 32)
                dve.tensor_scalar(proj_in[s], proj_in[s], S, None, ALU.mult).then_inc(w_sc, 1)
                dve.wait_ge(w_sc, k + 1)
                dve.tensor_copy(interior(img[s]), rows).then_inc(w_hi, 1)
                dve.tensor_reduce(psum_w[:, bass.ds(k * NBAT, NBAT)], proj_in[s][0:CH], AX_X, ALU.add)\
                    .then_inc(w_free, 1)

            def low_weights(i, s):
                for q in range(2):
                    dve.wait_ge(w_evh, i * 4 + (2 * s + q + 1))
                    at = bass.ds(i * (2 * NBAT) + (s * NBAT + QN * q), QN)
                    dve.tensor_tensor(wc[:, :, 1, at], cab[q][:, :].rearrange("p (n q) -> p q n", n=QN),
                                      wc[:, :, 0, at], ALU.subtract).then_inc(w_evl, 1)

            dve.wait_ge(s_xh, 1)
            x_n4 = x_n.rearrange("p c (r q) -> p c r q", q=P)
            dve.tensor_tensor(interior(x_lp[:, HP:CW]), x_n4[:, HP:CW], interior(x_hp[:, HP:CW]), ALU.subtract)\
                .then_inc(s_xs, 1)
            split_rows(0, 0, 0, 0)
            with dve.Fori(0, WBAT // 2 - 1) as i:
                split_rows(i * 2 + 1, 1, i, i)
                low_weights(i, 0)
                split_rows(i * 2 + 2, 0, i, i + 1)
                low_weights(i, 1)
            split_rows(WBAT - 1, 1, 0, WBAT // 2 - 1)
            low_weights(WBAT // 2 - 1, 0)
            low_weights(WBAT // 2 - 1, 1)
            dve.wait_ge(w_free, WBAT + 2)
            dve.sem_inc(s_bb, 1)
            vd = 0
            for h in range(2):
                for c in range(1, CIN):
                    dve.wait_ge(v_in[c], 16 * h + 16)
                    if h:
                        dve.wait_ge(v_tr, V_ORDER.index((0, c)) + 1)
                    o = v_t[:, c, :].rearrange("p (r q) -> p r q", q=P)
                    for t in range(TAPS):
                        if t == 0:
                            ins = dve.tensor_copy(o, shifted(c, t))
                        else:
                            dve.wait_ge(v_d, vd)
                            ins = dve.tensor_tensor(o, shifted(c, t), o, ALU.add)
                        vd += 1
                        ins.then_inc(v_d, 1)
                    dve.wait_ge(v_d, vd)
                    dve.sem_inc(v_sum, 1)
            for g in range(NG):
                dve.wait_ge(s_res, g + 1)
                dve.tensor_copy(h_tok[:, g, :], PS[2 + g % 2][0:GT, 0:E]).then_inc(s_resc, 1)

            LINKS = 4

            def stats(L, w, j, patches=range(QN)):
                dve.wait_ge((p_c1, p_raw)[L], w + (1, 3)[L])
                for n in patches:
                    src = c1p[j % 2][n // 2][:, (n % 2) * PIX:(n % 2) * PIX + PIX] if L == 0 else g2[j][:, n, :]
                    op = dve.bn_stats(st[j % 2 if L == 0 else (j + AHEAD + 1) % 2][:, L, n, :], src)
                return op

            def mean(b, k):
                f = st[k][:, :, :, :].rearrange("p l n (m f) -> p l (n m) f", f=3)
                dve.wait_ge(p_bn, b + 1)
                dve.tensor_tensor(rr[:, :, 0], f[:, :, :, 1], sbias[:, :, :], ALU.add).then_inc(chain_m, 1)
                dve.tensor_tensor(m2n[:, :, :], f[:, :, :, 2], per_n[:, :, :], ALU.mult).then_inc(chain_m, 1)

            def mean_square(b):
                dve.wait_ge(chain_m, b * LINKS + 1)
                dve.tensor_tensor(sq[:, :, :], rr[:, :, 0], rr[:, :, 0], ALU.mult).then_inc(chain_m, 1)

            def second_moment(b):
                dve.wait_ge(chain_m, b * LINKS + 3)
                dve.tensor_tensor(rr[:, :, 1], m2n[:, :, :], sq[:, :, :], ALU.add).then_inc(chain_m, 1)

            def both_halves(b):
                r = rr[:, :, :, :].rearrange("p l a (n m) -> p l a n m", m=2)
                dve.wait_ge(chain_m, b * LINKS + 4)
                dve.tensor_tensor(rs[:, :, :, :], r[:, :, :, :, 0], r[:, :, :, :, 1], ALU.add).then_inc(p_r, 1)

            def copy_average(b):
                dve.wait_ge(p_av, b + 1)
                dve.tensor_copy(ms[:, :, :, :].rearrange("p l a b -> p (l a b)"), stp[:, 0:4 * QN]).then_inc(p_avc, 1)

            def minus_square(b):
                m = ms[:, :, 0, :]
                dve.wait_ge(p_avc, b + 1)
                dve.scalar_tensor_tensor(vv[:, 0], m, -1.0, m, ALU.mult, ALU.mult).then_inc(chain_c, 1)
                dve.tensor_tensor(vv[:, 3], m, nbias[:, :, :], ALU.add).then_inc(chain_c, 1)

            def variance(b):
                dve.wait_ge(chain_c, b * LINKS + 1)
                dve.scalar_tensor_tensor(vv[:, 1], vv[:, 0], EPS * S * S, ms[:, :, 1, :], ALU.add, ALU.add)\
                    .then_inc(p_var, 1)

            def scale(b, k, g1_done, g2_done):
                dve.wait_ge(p_gelu1, g1_done)
                if g2_done is not None:
                    dve.wait_ge(p_gelu2, g2_done)
                dve.wait_ge(p_pow, b + 1)
                dve.tensor_tensor(gn[k][:, 0], vv[:, 2], gamma[:, :, :], ALU.mult).then_inc(chain_c, 1)

            def shift(b, k):
                dve.wait_ge(chain_c, b * LINKS + 3)
                dve.tensor_tensor(vv[:, 4], vv[:, 3], gn[k][:, 0], ALU.mult).then_inc(chain_c, 1)

            def bias(b, k):
                dve.wait_ge(chain_c, b * LINKS + 4)
                dve.tensor_tensor(gn[k][:, 1], beta[:, :, :], vv[:, 4], ALU.subtract).then_inc(p_gn, 1)

            def high2(w, j, at):
                dve.wait_ge(p_gelu2, w + 1)
                dve.tensor_scalar(g2_h[:, :, at], g2[j].rearrange("p n q -> p q n"), 1.0, None, ALU.mult)\
                    .then_inc(p_h2, 1)

            def low2(w, j, at):
                dve.wait_ge(p_h2, w + 1)
                dve.tensor_tensor(g2_l[:, :, at], g2[j].rearrange("p n q -> p q n"), g2_h[:, :, at], ALU.subtract)\
                    .then_inc(p_g2, 1)

            def take_product(g):
                dve.wait_ge(p_acc, g)
                dve.tensor_scalar(acc_tmp[:, :], accp[0:GT, E:2 * E], 1.0 / (S * S), None, ALU.mult).then_inc(s_d0, 1)
                gi = g - 1
                hg = h_tok[:, gi, :] if isinstance(g, int) else h_tok[:, bass.ds(gi, 1), :].rearrange("p o e -> p (o e)")
                dve.wait_ge(s_d0, gi * 3 + (dn[0] + 1))
                dve.tensor_tensor(hg, hg, acc_tmp[:, :], ALU.add).then_inc(s_d0, 1)
                dve.wait_ge(s_d0, gi * 3 + (dn[0] + 2))
                dve.scalar_tensor_tensor(hg, accp[0:GT, 0:E], 1.0 / (S * S), hg, ALU.mult, ALU.add).then_inc(s_d0, 1)
                dve.wait_ge(s_d0, gi * 3 + (dn[0] + 3))
                dve.sem_inc(p_accc, 1)

            def dve_step(i, j, front=True, back=True, split=True, coef=True, done=None, at=None,
                         first=False, tail=False):
                cb, ck = i * 4 + (j + 2), j % 2
                b, k = i * 4 + (j + 3), (j + 1) % 2
                stat = front or back
                if coef:
                    copy_average(cb)
                    minus_square(cb)
                    variance(cb)
                if front:
                    last = stats(0, b, (j + 3) % 4)
                if split:
                    if done is not None and j == 3:
                        take_product(done)
                    high2(i * 4 + (j - 3), (j - 3) % 4, at)
                if coef:
                    scale(cb, ck, (QUADS + 2 if tail else cb + 1), None if first else i * 4 + (j - 3))
                if back:
                    last = stats(1, i * 4 + (j - 1), (j - 1) % 4, range(0, 1))
                if coef:
                    shift(cb, ck)
                if back:
                    last = stats(1, i * 4 + (j - 1), (j - 1) % 4, range(1, 2))
                if coef:
                    bias(cb, ck)
                if back:
                    last = stats(1, i * 4 + (j - 1), (j - 1) % 4, range(2, QN))
                if stat:
                    last.then_inc(p_bn, 1)
                    mean(b, k)
                    mean_square(b)
                    second_moment(b)
                    both_halves(b)
                if split:
                    low2(i * 4 + (j - 3), (j - 3) % 4, at)

            def dve_steps(i, first=False, last=False, done=None, at=None):
                for j in range(RING):
                    c = None
                    if j == 3:
                        c = bass.ds(at * (4 * QN), QN)
                    elif done is not None:
                        c = bass.ds(GT + (j - 3) * QN, QN)
                    elif not first:
                        c = bass.ds(at * (4 * QN) + (j - 3) * QN, QN)
                    dve_step(i, j, front=not (last and j >= 1), back=not (first and j == 0), split=c is not None,
                             done=done, at=c, first=first, tail=last and j >= 2)

            for u in range(-AHEAD, 0):
                dve_step(0, u, back=False, split=False, coef=u > -AHEAD, first=True)
            dve_steps(0, first=True, at=0)
            with dve.Fori(1, 7) as r:
                dve_steps(r, at=r)
            with dve.Fori(1, NG - 1) as g:
                dve_steps(g * 7, done=g, at=0)
                with dve.Fori(1, 7) as r:
                    dve_steps(g * 7 + r, at=r)
            dve_steps(7 * (NG - 1), done=NG - 1, at=0)
            with dve.Fori(1, 6) as r:
                dve_steps(r + 7 * (NG - 1), at=r)
            dve_steps(7 * NG - 1, last=True, at=6)
            dve_step(QUADS // 4, 0, front=False, at=bass.ds(GT - 3 * QN, QN), tail=True)
            dve_step(QUADS // 4, 1, front=False, back=False, at=bass.ds(GT - 2 * QN, QN), tail=True)
            high2(QUADS - 1, 3, bass.ds(GT - QN, QN))
            low2(QUADS - 1, 3, bass.ds(GT - QN, QN))
            take_product(NG)

        @block.gpsimd
        def _(pool):
            pool.memset(x_h.bitcast(U32), 0).then_inc(s_xz, 1)
            pool.memset(x_l.bitcast(U32), 0).then_inc(s_xz, 1)
            pool.wait_ge(s_exp, 2)
            pool.wait_ge(s_p0, 1)
            pool.tensor_tensor(m0[:, 3, :], m0[:, 2, :], expo[0:GT, 8:8 + CW], ALU.pow).then_inc(s_p0, 1)
            x_n4 = x_n.rearrange("p c (r q) -> p c r q", q=P)
            pool.wait_ge(s_xh, 1)
            pool.tensor_tensor(interior(x_lp[:, 0:HP]), x_n4[:, 0:HP], interior(x_hp[:, 0:HP]), ALU.subtract).then_inc(s_xs, 1)
            pool.wait_ge(s_xs, 2)
            with pool.Fori(0, WBAT // 2) as i:
                for s in range(2):
                    rows = proj_in[s].rearrange("p n (r q) -> p n r q", q=P)
                    pool.wait_ge(w_hi, i * 2 + (s + 1))
                    pool.tensor_tensor(interior(img[s])[CH:128], rows[CH:128], interior(img[s])[CH:128],
                                       ALU.subtract).then_inc(w_split, 1)

            def power(b):
                pool.wait_ge(p_var, b + 1)
                pool.tensor_tensor(vv[:, 2], vv[:, 1], expo[:, 0:2 * QN].rearrange("p (l n) -> p l n", l=2), ALU.pow)\
                    .then_inc(p_pow, 1)

            def low1(w, j):
                dst = interior(img[j // 2][:, QN * (j % 2):QN * (j % 2) + QN])[CH:128]
                src = g1[j % 2][CH:128, :, :].rearrange("p n (r q) -> p n r q", q=P)
                pool.wait_ge(p_h1, w + 1)
                pool.tensor_tensor(dst, src, dst, ALU.subtract).then_inc(p_img, 1)

            def pool_steps(i, first=False, last=False, done=None):
                for j in range(RING):
                    u = i * 4 + j
                    pool.wait_ge(p_img, u + 3)
                    power(u + 2)
                    if not (last and j == 3):
                        pool.wait_ge(p_pow, u + 3)
                        low1(u + 1, (j + 1) % 4)

            pool.wait_ge(w_split, WBAT + 2)
            power(0)
            pool.wait_ge(p_pow, 1)
            low1(0, 0)
            pool.wait_ge(p_img, 3)
            power(1)
            pool.wait_ge(p_pow, 2)
            schedule(pool, pool_steps)
            power(QUADS + 2)
            power(QUADS + 3)


def tower(nc, a, out, h_tok, ident, expo, PS):
    with ExitStack() as ctx:
        def sb(name, shape, dt=F32):
            return ctx.enter_context(nc.sbuf_tensor(name, shape, dt))

        def sem(name):
            return ctx.enter_context(nc.semaphore(name))

        x_tok = sb("x_tok", [GT, NG, E])
        h1_tok = sb("h1_tok", [GT, NG, E])
        x_T = sb("x_T", [EK, 2 * TOK + 64])
        x_T2 = x_T[:, 0:2 * TOK].rearrange("p (k t) -> p k t", t=TOK)
        qk_T = [sb("q_T", [128, NCH * TOK + 64]), sb("k_T", [128, NCH * TOK + 64])]
        ctx_T = sb("ctx_T", [128, NCH, TOK])
        v1 = sb("v1", [128, NPAIR, HEADS, HPAD])
        v2 = sb("v2", [64, B, HEADS, HPAD])
        vn = sb("vn", [128, HEADS, HPAD])
        prob = [sb(f"prob{i}", [128, HEADS, SEQ]) for i in range(2)]
        prob_T = [sb(f"prob_T{i}", [SEQ, HEADS, 128]) for i in range(2)]
        mx, sm, ri = sb("mx", [128, HEADS]), sb("sm", [128, HEADS]), sb("ri", [128, HEADS])
        wqk = [[sb(f"w{n}{L}", [EK, 2, 128 * NCH]) for n in "qk"] for L in range(2)]
        wv = [sb(f"wv{L}", [EK, 2, E]) for L in range(2)]
        wo = [sb(f"wo{L}", [128, NCH, E]) for L in range(2)]
        bqk = [sb(f"bqk{L}", [128, 2 * NCH]) for L in range(2)]
        rows = sb("rows", [128, 8, E])
        wg = sb("wg", [EK, 2, NE])
        b1 = [sb(f"b1_{i}", [128, HC]) for i in range(2)]
        b2 = sb("b2", [NE, E])
        iota = sb("iota", [GT, NE])
        ln_st, ln_mv = sb("ln_st", [GT, NG, 6]), sb("ln_mv", [GT, NG, 2])
        ln_r = sb("ln_r", [GT, 2, NG])
        lg, top, gate, gtmp = (sb(n, [GT, NG, NE]) for n in ("lg", "top", "gate", "gtmp"))
        topi = sb("topi", [GT, NG, NE], U32)
        idx = sb("idx", [GT, NG, 2])
        gg = sb("gg", [GT, 4, NG])
        gate_T = sb("gate_T", [NE, NG * GT])
        w1 = [sb(f"w1_{i}", [EK, 2, HID]) for i in range(2)]
        w2 = [sb(f"w2_{i}", [128, HC, E]) for i in range(2)]
        hid = sb("hid", [128, HC, TOK])

        t_const = sem("t_const"); t_attn = [sem("t_attn0"), sem("t_attn1")]
        t_x = sem("t_x")
        t_tr = sem("t_tr"); t_trc = sem("t_trc")
        t_qk = sem("t_qk"); t_qkc = sem("t_qkc"); t_v = sem("t_v"); t_vc = sem("t_vc")
        t_sc = sem("t_sc"); t_sub = sem("t_sub"); t_exp = sem("t_exp"); t_p = sem("t_p")
        t_ptr = sem("t_ptr"); t_ptc = sem("t_ptc"); t_ctx = sem("t_ctx"); t_ctxc = sem("t_ctxc")
        t_o = sem("t_o"); t_oc = sem("t_oc")
        t_var = sem("t_var"); t_rs = sem("t_rs"); t_d = sem("t_d"); t_z = sem("t_z"); t_vz = sem("t_vz")
        t_lg = sem("t_lg"); t_lgd = sem("t_lgd"); t_ge = sem("t_ge"); t_gate = sem("t_gate")
        t_gt = sem("t_gt"); t_gtc = sem("t_gtc"); t_b2 = sem("t_b2"); t_b2c = sem("t_b2c")
        e_w = [sem("e_w0"), sem("e_w1")]; e_used = sem("e_used")
        e_h = sem("e_h"); e_hg = sem("e_hg"); e_y = sem("e_y"); e_yc = sem("e_yc")
        t_done = sem("t_done"); t_h1 = sem("t_h1"); s_out = sem("s_out")
        block = ctx.enter_context(nc.Block())

        CONST = [(rows[:], a["rows"]), (wg[:], a["wg"]), (b2[:], a["b2"]), (iota[:], a["iota"])]
        ATTN = [[(wqk[L][0][:], a[f"wq{L}"]), (wqk[L][1][:], a[f"wk{L}"]), (wv[L][:], a[f"wv{L}"]),
                 (wo[L][:], a[f"wo{L}"]), (bqk[L][:], a[f"bqk{L}"])] for L in range(2)]
        NBANK = 4

        def score_view(bank_cols=SC):
            return [PS[j][:, 0:SC] for j in range(4)]

        @block.sync
        def _(sp):
            for L in range(2):
                for dst, src in ATTN[L]:
                    sp.dma_start(dst, src).then_inc(t_attn[L], 16)
                if L == 0:
                    for dst, src in CONST:
                        sp.dma_start(dst, src).then_inc(t_const, 16)
            with sp.Fori(0, NE // 2) as i:
                for s in range(2):
                    sp.wait_ge(e_used, i * 2 + (s + 1))
                    sp.dma_start(w1[s][:], a["w1"][bass.ds(i * 2 + s, 1)].rearrange("o p k h -> (o p) k h"))\
                        .then_inc(e_w[s], 16)
                    sp.dma_start(w2[s][:], a["w2"][bass.ds(i * 2 + s, 1)].rearrange("o p k h -> (o p) k h"))\
                        .then_inc(e_w[s], 16)
                    sp.dma_start(b1[s][:], a["b1"][bass.ds(i * 2 + s, 1)].rearrange("o p k -> (o p) k"))\
                        .then_inc(e_w[s], 16)
            sp.wait_ge(t_done, 1)
            sp.dma_start(out.rearrange("(g p) e -> p g e", p=GT), h_tok[:, :, :]).then_inc(s_out, 16)
            sp.wait_ge(s_out, 16)

        @block.tensor
        def _(pe):
            def transpose_tokens(n, src):
                pe.wait_ge(t_x, n + 1)
                for g in range(NG):
                    k = n * NG + g
                    if g >= 2 or n:
                        pe.wait_ge(t_trc, k - 1)
                    for c in range(2):
                        mm = pe.transpose(PS[6 + g % 2][0:EK, c * GT:c * GT + GT], src[:, g, c * EK:c * EK + EK],
                                          ident[0:GT, 0:GT])
                    mm.then_inc(t_tr, 1)

            def attention(L):
                pe.wait_ge(t_attn[L], 16 * len(ATTN[L]))
                pe.wait_ge(t_trc, (L + 1) * NG)
                n = 0
                for m in range(2):
                    for j in range(NCH):
                        for h in range(2):
                            k = L * 12 + n
                            if k >= 2:
                                pe.wait_ge(t_qkc, k - 1)
                            for c in range(2):
                                mm = pe.matmul(PS[4 + n % 2][:, 0:HT], wqk[L][m][:, c, 128 * j:128 * j + 128],
                                               x_T2[:, c, h * HT:h * HT + HT], start=(c == 0), stop=(c == 1))
                            mm.then_inc(t_qk, 1)
                            n += 1
                for n in range(NPAIR):
                    k = L * NPAIR + n
                    if k >= 2:
                        pe.wait_ge(t_vc, k - 1)
                    for r in range(2):
                        o = PS[6 + n % 2][64 * r:64 * r + 64, 0:E] if L == 0 else PS[6 + n % 2][0:64, r * E:r * E + E]
                        t0 = (2 * n + r) * SEQ
                        for c in range(2):
                            mm = pe.matmul(o, x_T[:, c * TOK + t0:c * TOK + t0 + 64], wv[L][:, c, :],
                                           start=(c == 0), stop=(c == 1))
                    mm.then_inc(t_v, 1)
                pe.wait_ge(t_qkc, (L + 1) * 12)
                pe.wait_ge(t_vc, (L + 1) * NPAIR)
                lhs, rhs = (qk_T[1], qk_T[0]) if L == 0 else (qk_T[0], qk_T[1])
                for n in range(NPAIR + 1 + L):
                    k = L * NPAIR + n
                    if n < NPAIR:
                        if k >= 1:
                            pe.wait_ge(t_sub, k)
                        for j in range(4):
                            for r in range(2):
                                for c in range(NCH):
                                    t0 = c * TOK + (2 * n + r) * SEQ
                                    mm = pe.matmul(PS[j][64 * r:64 * r + 64, c * SEQ:c * SEQ + SEQ],
                                                   lhs[32 * j:32 * j + 32, t0:t0 + 64],
                                                   rhs[32 * j:32 * j + 32, t0:t0 + SEQ], start=True, stop=True)
                        mm.then_inc(t_sc, 1)
                    if n == 0:
                        continue
                    k, n0 = k - 1, n - 1
                    if n <= NPAIR:
                        pe.wait_ge(t_p, k + 1)
                    if L == 0:
                        if k >= 1:
                            pe.wait_ge(t_ctxc, k)
                        for r in range(2):
                            for hd in range(HEADS):
                                c, j = divmod(hd, 4)
                                mm = pe.matmul(PS[4 + r][32 * j:32 * j + 32, c * SEQ:c * SEQ + SEQ],
                                               vn[64 * r:64 * r + SEQ, hd, :],
                                               prob[n0 % 2][64 * r:64 * r + SEQ, c * 4 + j, :], start=True, stop=True)
                        mm.then_inc(t_ctx, 1)
                    else:
                        if n0 < NPAIR:
                            if n0 >= 1:
                                pe.wait_ge(t_ptc, n0)
                            for hd in range(HEADS):
                                mm = pe.transpose(PS[4 + hd // 4][0:SEQ, (hd % 4) * 128:(hd % 4) * 128 + 128],
                                                  prob[n0 % 2][:, hd, :], ident[:, :])
                            mm.then_inc(t_ptr, 1)
                        if n0 == 0:
                            continue
                        m = n0 - 1
                        pe.wait_ge(t_ptc, m + 1)
                        pe.wait_ge(t_ctxc, NPAIR + m)
                        for r in range(2):
                            for hd in range(HEADS):
                                c, j = divmod(hd, 4)
                                mm = pe.matmul(PS[7][32 * j:32 * j + 32, (r * NCH + c) * SEQ:(r * NCH + c) * SEQ + SEQ],
                                               v2[0:SEQ, 2 * m + r, hd, :], prob_T[m % 2][:, hd, 64 * r:64 * r + SEQ],
                                               start=True, stop=True)
                        mm.then_inc(t_ctx, 1)
                pe.wait_ge(t_ctxc, (L + 1) * NPAIR)
                for g in range(NG):
                    k = L * NG + g
                    if k >= 2:
                        pe.wait_ge(t_oc, k - 1)
                    for c in range(NCH):
                        mm = pe.matmul(PS[g % 2][0:GT, 0:E], ctx_T[:, c, g * GT:g * GT + GT], wo[L][:, c, :],
                                       start=(c == 0), stop=(c == NCH - 1))
                    mm.then_inc(t_o, 1)

            pe.wait_ge(t_z, 1)
            transpose_tokens(0, h_tok)
            attention(0)
            transpose_tokens(1, x_tok)
            attention(1)
            transpose_tokens(2, x_tok)
            pe.wait_ge(t_trc, 3 * NG)
            pe.wait_ge(t_const, 16 * len(CONST))
            for g in range(NG):
                for c in range(2):
                    mm = pe.matmul(PS[0][0:GT, g * NE:g * NE + NE], x_T2[:, c, g * GT:g * GT + GT], wg[:, c, :],
                                   start=(c == 0), stop=(c == 1))
            mm.then_inc(t_lg, 1)
            pe.wait_ge(t_lgd, 1)
            with pe.Fori(0, NE // 2) as i:
                for s in range(2):
                    pe.wait_ge(e_w[s], i * 48 + 48)
                    for n in range(2 * HC):
                        hc, h = n // 2, n % 2
                        pe.wait_ge(e_hg, i * (4 * HC) + (s * 2 * HC + n + 1))
                        for c in range(2):
                            mm = pe.matmul(PS[n % 4][:, 0:HT], w1[s][:, c, 128 * hc:128 * hc + 128],
                                           x_T2[:, c, h * HT:h * HT + HT], start=(c == 0), stop=(c == 1))
                        mm.then_inc(e_h, 1)
                    pe.wait_ge(e_hg, i * (4 * HC) + (s * 2 * HC + 2 * HC + 4))
                    for g in range(NG):
                        pe.wait_ge(e_yc, i * (2 * NG) + (s * NG + g + 1))
                        for hc in range(HC):
                            mm = pe.matmul(PS[4 + (s * NG + g) % 2][0:GT, 0:E], hid[:, hc, g * GT:g * GT + GT],
                                           w2[s][:, hc, :], start=(hc == 0), stop=(hc == HC - 1))
                        mm.then_inc(e_y, 1)
            pe.wait_ge(e_hg, NE * 2 * HC + 4)
            for g in range(NG):
                mm = pe.transpose(PS[1 + g // 4][0:NE, (g % 4) * GT:(g % 4) * GT + GT], gate[:, g, :], ident[0:GT, 0:GT])
            mm.then_inc(t_gt, 1)
            pe.wait_ge(t_gtc, 1)
            pe.wait_ge(e_yc, NE * NG + 2)
            for g in range(NG):
                if g >= 2:
                    pe.wait_ge(t_b2c, g - 1)
                pe.matmul(PS[3 + g % 2][0:GT, 0:E], gate_T[:, g * GT:g * GT + GT], b2[:, :], start=True, stop=True)\
                    .then_inc(t_b2, 1)

        @block.scalar
        def _(act):
            act.sem_inc(e_hg, 4)

            def tokens_out(n):
                for g in range(NG):
                    act.wait_ge(t_tr, n * NG + g + 1)
                    act.activation(x_T2[:, :, g * GT:g * GT + GT],
                                   PS[6 + g % 2][0:EK, 0:2 * GT].rearrange("p (k t) -> p k t", t=GT), ACT.Copy)\
                        .then_inc(t_trc, 1)

            def attention(L):
                n = 0
                for m in range(2):
                    for j in range(NCH):
                        for h in range(2):
                            act.wait_ge(t_qk, L * 12 + n + 1)
                            act.activation(qk_T[m][:, j * TOK + h * HT:j * TOK + h * HT + HT], PS[4 + n % 2][:, 0:HT],
                                           ACT.Identity, bias=bqk[L][:, m * NCH + j:m * NCH + j + 1]).then_inc(t_qkc, 1)
                            n += 1
                for n in range(NPAIR + 1 + L):
                    if n < NPAIR:
                        k = L * NPAIR + n
                        act.wait_ge(t_sub, k + 1)
                        p = prob[n % 2][:, :, :]
                        act.activation(p, p, ACT.Exp, scale=DH ** -0.5).then_inc(t_exp, 1)
                    if L == 1 and 1 <= n <= NPAIR:
                        act.wait_ge(t_ptr, n)
                        if n >= 3:
                            act.wait_ge(t_ctx, NPAIR + n - 2)
                        for b in range(3):
                            cp = act.activation(prob_T[(n - 1) % 2][:, 4 * b:4 * b + 4, :],
                                                PS[4 + b][0:SEQ, :].rearrange("p (h t) -> p h t", t=128), ACT.Copy)
                        cp.then_inc(t_ptc, 1)
                    n0 = n - 1 - L
                    if n0 >= 0:
                        act.wait_ge(t_ctx, L * NPAIR + n0 + 1)
                        for r in range(2):
                            src = PS[4 + r][:, 0:SC] if L == 0 else PS[7][:, r * SC:r * SC + SC]
                            t0 = (2 * n0 + r) * SEQ
                            cp = act.activation(ctx_T[:, :, t0:t0 + SEQ], src.rearrange("p (c t) -> p c t", t=SEQ), ACT.Copy)
                        cp.then_inc(t_ctxc, 1)

            tokens_out(0)
            attention(0)
            tokens_out(1)
            attention(1)
            tokens_out(2)
            act.wait_ge(t_ge, 1)
            act.activation(gg[:, 1, :], gg[:, 0, :], ACT.Exp).then_inc(t_ge, 1)
            with act.Fori(0, NE // 2) as i:
                for s in range(2):
                    act.wait_ge(e_used, i * 2 + (s + 2))
                    act.wait_ge(e_w[s], i * 48 + 48)
                    for n in range(2 * HC):
                        hc, h = n // 2, n % 2
                        act.wait_ge(e_h, i * (4 * HC) + (s * 2 * HC + n + 1))
                        act.activation(hid[:, hc, h * HT:h * HT + HT], PS[n % 4][:, 0:HT], ACT.Gelu,
                                       bias=b1[s][:, hc:hc + 1]).then_inc(e_hg, 1)
            act.wait_ge(t_gt, 1)
            act.activation(gate_T[:, 0:4 * GT], PS[1][0:NE, 0:4 * GT], ACT.Copy)
            act.activation(gate_T[:, 4 * GT:NG * GT], PS[2][0:NE, 0:3 * GT], ACT.Copy).then_inc(t_gtc, 1)

        @block.gpsimd
        def _(pool):
            pool.memset(v1[:, :, :, :], 0.0).then_inc(t_vz, 1)
            pool.memset(v2[:, :, :, :], 0.0).then_inc(t_vz, 1)
            pool.wait_ge(t_vz, 2)
            for n in range(4):
                pool.wait_ge(t_var, n + 1)
                pool.tensor_tensor(ln_r[:, 1, :], ln_r[:, 0, :], expo[0:GT, 0:NG], ALU.pow).then_inc(t_rs, 1)

        @block.vector
        def _(dve):
            dn = [0]

            def link(ins):
                dn[0] += 1
                ins.then_inc(t_d, 1)
                dve.wait_ge(t_d, dn[0])

            lns = [0]

            def layernorm(dst, w=None):
                for g in range(NG):
                    ins = dve.bn_stats(ln_st[:, g, :], h_tok[:, g, :])
                link(ins)
                for g in range(NG):
                    ins = dve.bn_aggr(ln_mv[:, g, :], ln_st[:, g, :])
                link(ins)
                dve.tensor_scalar(ln_r[:, 0, :], ln_mv[:, :, 1], EPS, None, ALU.add).then_inc(t_var, 1)
                lns[0] += 1
                dve.wait_ge(t_rs, lns[0])
                for g in range(NG):
                    ins = dve.tensor_scalar(dst[:, g, :], h_tok[:, g, :], ln_mv[:, g, 0:1], ln_r[:, 1, g:g + 1],
                                            ALU.subtract, ALU.mult)
                link(ins)
                if w is not None:
                    wb, bb = (rows[0:GT, w + m:w + m + 1, :].to_broadcast([GT, NG, E]) for m in range(2))
                    link(dve.tensor_tensor(dst[:, :, :], dst[:, :, :], wb, ALU.mult))
                    link(dve.tensor_tensor(dst[:, :, :], dst[:, :, :], bb, ALU.add))

            def attention(L):
                dve.wait_ge(t_vz, 2)
                for n in range(NPAIR):
                    dve.wait_ge(t_v, L * NPAIR + n + 1)
                    if L == 0:
                        dve.tensor_tensor(v1[:, n, :, 0:DH], PS[6 + n % 2][:, 0:E].rearrange("p (h d) -> p h d", d=DH),
                                          rows[:, 0, :].rearrange("p (h d) -> p h d", d=DH), ALU.add).then_inc(t_vc, 1)
                    else:
                        for r in range(2):
                            ins = dve.tensor_tensor(v2[:, 2 * n + r, :, 0:DH],
                                                    PS[6 + n % 2][0:64, r * E:r * E + E].rearrange("p (h d) -> p h d", d=DH),
                                                    rows[0:64, 1, :].rearrange("p (h d) -> p h d", d=DH), ALU.add)
                        ins.then_inc(t_vc, 1)
                for n in range(NPAIR):
                    k = L * NPAIR + n
                    dve.wait_ge(t_sc, k + 1)
                    p = prob[n % 2]
                    pj = p[:, :, :].rearrange("p (c j) t -> p j c t", j=4)
                    mj = mx[:, :].rearrange("p (c j) -> p j c", j=4)
                    for j in range(4):
                        ins = dve.tensor_reduce(mj[:, j, :], PS[j][:, 0:SC].rearrange("p (c t) -> p c t", t=SEQ), AX_X, ALU.max)
                    link(ins)
                    if L == 1 and n >= 2:
                        dve.wait_ge(t_ptr, n - 1)
                    elif k >= 2:
                        dve.wait_ge(t_ctx, min(k - 1, NPAIR))
                    for j in range(4):
                        ins = dve.tensor_tensor(pj[:, j], PS[j][:, 0:SC].rearrange("p (c t) -> p c t", t=SEQ),
                                                mj[:, j, :].unsqueeze(2).to_broadcast([128, NCH, SEQ]), ALU.subtract)
                    ins.then_inc(t_sub, 1)
                    dve.wait_ge(t_exp, k + 1)
                    link(dve.tensor_reduce(sm[:, :], p[:, :, :], AX_X, ALU.add))
                    link(dve.reciprocal(ri[:, :], sm[:, :]))
                    if L == 0:
                        if k >= 1:
                            dve.wait_ge(t_ctx, k)
                        dve.tensor_tensor(vn[:, :, :], v1[:, n, :, :], ri[:, :].unsqueeze(2).to_broadcast([128, HEADS, HPAD]),
                                          ALU.mult).then_inc(t_p, 1)
                    else:
                        dve.tensor_tensor(p[:, :, :], p[:, :, :], ri[:, :].unsqueeze(2).to_broadcast([128, HEADS, SEQ]),
                                          ALU.mult).then_inc(t_p, 1)
                for g in range(NG):
                    dve.wait_ge(t_o, L * NG + g + 1)
                    dve.tensor_tensor(h_tok[:, g, :], h_tok[:, g, :], PS[g % 2][0:GT, 0:E], ALU.add).then_inc(t_oc, 1)
                dve.wait_ge(t_oc, (L + 1) * NG)
                link(dve.tensor_tensor(h_tok[:, :, :], h_tok[:, :, :], rows[0:GT, 2 + L:3 + L, :].to_broadcast([GT, NG, E]),
                                       ALU.add))

            for t in (x_T[:, 2 * TOK:], qk_T[0][:, NCH * TOK:], qk_T[1][:, NCH * TOK:]):
                ins = dve.memset(t, 0.0)
            ins.then_inc(t_z, 1)
            dve.sem_inc(e_used, 2)
            dve.sem_inc(e_yc, 2)
            dve.wait_ge(t_z, 1)
            dve.wait_ge(t_const, 16 * len(CONST))
            dve.sem_inc(t_x, 1)
            attention(0)
            layernorm(h_tok)
            layernorm(x_tok, 4)
            dve.sem_inc(t_x, 1)
            dve.tensor_copy(h1_tok[:, :, :], h_tok[:, :, :]).then_inc(t_h1, 1)
            attention(1)
            layernorm(x_tok, 6)
            dve.sem_inc(t_x, 1)
            dve.wait_ge(t_h1, 1)
            link(dve.tensor_tensor(h_tok[:, :, :], h_tok[:, :, :], h1_tok[:, :, :], ALU.add))
            dve.wait_ge(t_lg, 1)
            dve.tensor_copy(lg[:, :, :].rearrange("p g e -> p (g e)"), PS[0][0:GT, 0:NG * NE]).then_inc(t_lgd, 1)
            dve.wait_ge(t_lgd, 1)
            for g in range(NG):
                ins = dve.max(top[:, g, :], lg[:, g, :])
            link(ins)
            for g in range(NG):
                ins = dve.max_index(topi[:, g, :], top[:, g, :], lg[:, g, :])
            link(ins)
            link(dve.tensor_copy(idx[:, :, :], topi[:, :, 0:2]))
            dve.tensor_tensor(gg[:, 0, :], top[:, :, 1], top[:, :, 0], ALU.subtract).then_inc(t_ge, 1)
            dve.wait_ge(t_ge, 2)
            link(dve.tensor_scalar(gg[:, 2, :], gg[:, 1, :], 1.0, None, ALU.add))
            link(dve.reciprocal(gg[:, 2, :], gg[:, 2, :]))
            link(dve.tensor_tensor(gg[:, 3, :], gg[:, 1, :], gg[:, 2, :], ALU.mult))
            for m, t in enumerate((gate, gtmp)):
                link(dve.tensor_tensor(t[:, :, :], iota[:, :].unsqueeze(1).to_broadcast([GT, NG, NE]),
                                       idx[:, :, m:m + 1].to_broadcast([GT, NG, NE]), ALU.is_equal))
                link(dve.tensor_tensor(t[:, :, :], t[:, :, :], gg[:, 2 + m, :].unsqueeze(2).to_broadcast([GT, NG, NE]),
                                       ALU.mult))
            dve.tensor_tensor(gate[:, :, :], gate[:, :, :], gtmp[:, :, :], ALU.add).then_inc(t_gate, 1)
            dve.wait_ge(t_gate, 1)
            with dve.Fori(0, NE // 2) as i:
                for s in range(2):
                    for g in range(NG):
                        dve.wait_ge(e_y, i * (2 * NG) + (s * NG + g + 1))
                        dve.wait_ge(e_yc, i * (2 * NG) + (s * NG + 2))
                        dve.scalar_tensor_tensor(h_tok[:, g, :], PS[4 + (s * NG + g) % 2][0:GT, 0:E],
                                                 gate[:, g, bass.ds(i * 2 + s, 1)], h_tok[:, g, :], ALU.mult, ALU.add)\
                            .then_inc(e_yc, 1)
                    dve.sem_inc(e_used, 1)
            dve.wait_ge(e_yc, NE * NG + 2)
            for g in range(NG):
                dve.wait_ge(t_b2, g + 1)
                dve.tensor_tensor(h_tok[:, g, :], h_tok[:, g, :], PS[3 + g % 2][0:GT, 0:E], ALU.add).then_inc(t_b2c, 1)
            dve.wait_ge(t_b2c, NG)
            layernorm(h_tok)
            dve.sem_inc(t_done, 1)


def laid_out(i):
    f = np.float32
    x = np.asarray(i["x"]).reshape(B, CIN, HP, P, HP, P).transpose(0, 2, 1, 4, 3, 5)
    r = {"x": x.reshape(GT, CIN, HP, PIX)}
    c1 = np.asarray(i["L0_tok_conv1_w"])
    r["c1"] = np.tile(c1.reshape(CH, IMR).T, (3, 2))
    r["cz"] = c1.reshape(CH, IMR)
    r["r1"] = np.asarray(i["L0_tok_rconv1_w"]).transpose(1, 2, 3, 0).reshape(CH, TAPS, CH)
    r2 = np.asarray(i["L0_tok_rconv2_w"])
    r["r2"] = r2[:, :, ::-1, ::-1].transpose(0, 2, 3, 1).reshape(CH, TAPS, CH)
    r["proj"] = np.asarray(i["L0_tok_proj_w"]).reshape(E, CH, PIX).transpose(1, 0, 2)
    names = ["conv1_b", "gn1_g", "gn1_b", "rconv1_b", "gn2_g", "gn2_b", "rconv2_b"]
    r["vecs"] = np.tile(np.stack([np.asarray(i["L0_tok_" + n]) for n in names], 1), (2, 1))
    r["ident"] = np.eye(128, dtype=f)
    ch = np.arange(128)
    pair = (ch[:, None] % CH) // 2 == (ch[None, :] % CH) // 2
    r["avg1"] = np.where(pair & (ch[:, None] // CH == ch[None, :] // CH), 0.25, 0.0).astype(f)
    r["avg2"] = np.where(pair, 0.125, 0.0).astype(f)
    at = np.arange(HP, dtype=f)
    lo = (at / f(HP) * f(VOCAB)).astype(np.int32)
    hi = ((at + 1) / f(HP) * f(VOCAB)).astype(np.int32)
    pos = (lo + hi) // 2
    r["emb_rows"] = np.concatenate([np.asarray(i["L0_tok_row_emb"])[pos], np.asarray(i["L0_tok_col_emb"])[pos],
                                    np.asarray(i["L0_tok_proj_b"])[None]])
    t = np.arange(TOK) % SEQ
    hot = np.zeros((2 * HP + 1, TOK), f)
    hot[t // HP, np.arange(TOK)] = 1
    hot[HP + t % HP, np.arange(TOK)] = 1
    hot[2 * HP] = 1
    r["onehot"] = hot
    def pad_heads(w):
        o = np.zeros((*w.shape[:-1], HEADS, HPAD), f)
        o[..., :DH] = w.reshape(*w.shape[:-1], HEADS, DH)
        return o.reshape(*w.shape[:-1], HEADS * HPAD)

    def two(w):
        return w.reshape(2, EK, w.shape[-1]).transpose(1, 0, 2)

    qkv = np.asarray(i["L0_ffn_qkv_w"]).reshape(3, E, E)
    qkvb = np.asarray(i["L0_ffn_qkv_b"]).reshape(3, E)
    w = [[np.asarray(i[f"L0_attn_W{n}"]).transpose(1, 0, 2).reshape(E, E) for n in "qkv"], [m.T for m in qkv]]
    bias = [[np.asarray(i[f"L0_attn_b{n}"]).reshape(E) for n in "qkv"], list(qkvb)]
    wo = [np.asarray(i["L0_attn_Wo"]), np.asarray(i["L0_ffn_proj_w"]).T]
    for L in range(2):
        r[f"wq{L}"], r[f"wk{L}"] = two(pad_heads(w[L][0])), two(pad_heads(w[L][1]))
        r[f"wv{L}"] = two(w[L][2])
        r[f"wo{L}"] = pad_heads(wo[L].T).T.reshape(NCH, 128, E).transpose(1, 0, 2)
        r[f"bqk{L}"] = np.concatenate([pad_heads(b[None]).reshape(NCH, 128).T for b in bias[L][:2]], 1)
    rows = [bias[0][2], bias[1][2], i["L0_attn_bo"], i["L0_ffn_proj_b"], i["L0_ffn_norm1_w"], i["L0_ffn_norm1_b"],
            i["L0_ffn_norm2_w"], i["L0_ffn_norm2_b"]]
    r["rows"] = np.tile(np.stack([np.asarray(v) for v in rows])[None], (128, 1, 1))
    r["wg"] = two(np.asarray(i["L0_ffn_w_gate"]))
    r["w1"] = np.asarray(i["L0_ffn_W1"]).reshape(NE, 2, EK, HID).transpose(0, 2, 1, 3)
    r["w2"] = np.asarray(i["L0_ffn_W2"]).reshape(NE, HC, 128, E).transpose(0, 2, 1, 3)
    r["b1"] = np.asarray(i["L0_ffn_b1"]).reshape(NE, HC, 128).transpose(0, 2, 1)
    r["b2"] = np.asarray(i["L0_ffn_b2"])
    r["iota"] = np.tile(np.arange(NE, dtype=f), (GT, 1))
    return {k: np.ascontiguousarray(v) for k, v in r.items()}


def kernel(**inputs):
    import concourse.bacc as bacc
    from concourse.bass_utils import run_bass_kernel_spmd

    nc = bacc.Bacc("TRN2", target_bir_lowering=False, num_devices=1)
    arrays = laid_out(inputs)
    a = {k: nc.dram_tensor("in_" + k, v.shape, mybir.dt.from_np(v.dtype), kind="ExternalInput").ap()
         for k, v in arrays.items()}
    out = nc.dram_tensor("out", (TOK, E), F32, kind="ExternalOutput").ap()
    build(nc, a, out)
    r = run_bass_kernel_spmd(nc, [{"in_" + k: v for k, v in arrays.items()}], core_ids=[0])
    return r.results[0]["out"].reshape(B, SEQ, E)
```

```python
from contextlib import ExitStack

import concourse.bass as bass
import numpy as np
from concourse import mybir

F32 = mybir.dt.float32
F16 = mybir.dt.float16
U32 = mybir.dt.uint32
ALU = mybir.AluOpType
ACT = mybir.ActivationFunctionType
AX_X = mybir.AxisListType.X

B, CIN, HW, P = 16, 3, 112, 16
HP = HW // P
SEQ = HP * HP
TOK = B * SEQ
GT = B * HP
NG = TOK // GT
PIX = P * P
PAD = P + 2
PP = PAD * PAD
CH = 64
E = 192
EK = E // 2
QN = 4
NBAT = 2 * QN
QUADS = TOK // QN
GQ = GT // QN
RING = 4
AHEAD = 3
WBAT = E // NBAT
HALF = PIX // 2
TAPS = 9
IMR = CIN * TAPS
IML = NBAT * PP - 2 * PAD - 2
S = 16.0
EPS = 1e-5
VOCAB = 256
KQ = CIN * 2
HEADS, DH = 12, 16
HPAD = 32
NCH = HEADS * HPAD // 128
NPAIR = B // 2
SC = NCH * SEQ
NE, HID = 8, 768
HC = HID // 128
HT = TOK // 2


def build(nc, a, out):
    with ExitStack() as ctx:
        def sb(name, shape, dt=F32):
            return ctx.enter_context(nc.sbuf_tensor(name, shape, dt))

        def ps(name, shape):
            return ctx.enter_context(nc.psum_tensor(name, shape, F32))

        h_tok = sb("h_tok", [GT, NG, E])
        ident = sb("ident", [128, 128])
        expo = sb("expo", [128, 32])
        PS = [ps(f"bank{i}", [128, 512]) for i in range(8)]
        tokenizer(nc, a, h_tok, ident, expo, PS)
        tower(nc, a, out, h_tok, ident, expo, PS)


def tokenizer(nc, a, h_tok, ident, expo, PS):
    with ExitStack() as ctx:
        def sb(name, shape, dt=F32):
            return ctx.enter_context(nc.sbuf_tensor(name, shape, dt))

        def sem(name):
            return ctx.enter_context(nc.semaphore(name))

        x_dram = nc.dram_tensor("x_dram", [3 * CIN, TOK * PP], F16, kind="Internal").ap()
        z_dram = nc.dram_tensor("z_dram", [IMR, E, PP], F32, kind="Internal").ap()

        big = sb("big", [128, HALF * E])
        mid = sb("mid", [128, GT * HALF])
        wc = big[:, :].bitcast(F16).rearrange("p (q m e) -> p q m e", m=2, e=E)
        g2_h = mid[:, 0:GT * HALF // 2].bitcast(F16).rearrange("p (q n) -> p q n", n=GT)
        g2_l = mid[:, GT * HALF // 2:GT * HALF].bitcast(F16).rearrange("p (q n) -> p q n", n=GT)

        CW = CIN * HP
        XA = 12
        o = 0
        x_raw = big[0:GT, o:o + CW * PIX].rearrange("p (c q) -> p c q", q=PIX); o += CW * PIX
        x_n = big[0:GT, o:o + CW * PIX].rearrange("p (c q) -> p c q", q=PIX); o += CW * PIX
        x_h = big[0:GT, o:o + CW * PP // 2].bitcast(F16); o += CW * PP // 2
        x_l = big[0:GT, o:o + CW * PP // 2].bitcast(F16)
        x_hp = x_h.rearrange("p (c r q) -> p c r q", r=PAD, q=PAD)
        x_lp = x_l.rearrange("p (c r q) -> p c r q", r=PAD, q=PAD)

        o = 0
        xnT = mid[:, o:o + KQ * TOK].rearrange("p (k t) -> p k t", t=TOK); o += KQ * TOK
        z_in = mid[0:EK, o:o + IMR * PP].rearrange("p (t r q) -> p t r q", r=PAD, q=PAD)
        assert o + IMR * PP <= GT * HALF
        proj_in = []
        for i in range(2):
            proj_in.append(mid[:, o:o + NBAT * PIX].rearrange("p (n q) -> p n q", q=PIX)); o += NBAT * PIX
        z_pad = []
        for i in range(2):
            z_pad.append(mid[0:IMR, o:o + NBAT * PP].rearrange("p (n r q) -> p n r q", r=PAD, q=PAD)); o += NBAT * PP
        assert o <= GT * HALF

        img = [sb(f"img{i}", [128, NBAT, PAD, PAD], F16) for i in range(2)]
        pair = sb("pair", [128, NBAT, PAD, PAD], F16)
        im2 = [sb(f"im2_{i}", [3 * IMR, NBAT, PAD, PAD], F16) for i in range(2)]
        g1 = [sb(f"g1_{i}", [128, QN, PIX]) for i in range(2)]
        g2b = sb("g2b", [128, RING, QN, HALF])
        g2 = [g2b[:, i] for i in range(RING)]
        g1_0, g1_1 = (g[:, :, :].rearrange("p a b -> p (a b)") for g in g1)
        g2_flat = g2b[:, :, :, :].rearrange("p a b c -> p (a b c)")
        v_t = g1_0[0:EK, 0:CIN * PIX].rearrange("p (a q) -> p a q", q=PIX)
        v_sb = g2_flat[:, TOK:TOK + KQ * E].rearrange("p (k e) -> p k e", e=E)
        w_f = g1_0[:, 0:TAPS * CH].rearrange("p (t c) -> p t c", c=CH)
        w_f2 = g1_1[:, 0:TAPS * CH].rearrange("p (t c) -> p t c", c=CH)
        onehot = g2_flat[0:2 * HP + 1, 0:TOK]
        emb_rows = g1_1[0:2 * HP + 1, TAPS * CH:TAPS * CH + E]

        r1_h, r1_l = sb("r1_h", [128, TAPS, CH], F16), sb("r1_l", [128, TAPS, CH], F16)
        r2_h, r2_l = sb("r2_h", [128, TAPS, CH], F16), sb("r2_l", [128, TAPS, CH], F16)
        r1_p, r2_p = sb("r1_p", [128, 3, CH], F16), sb("r2_p", [128, 3, CH], F16)
        c1_f = g1_0[0:3 * IMR, CIN * PIX:CIN * PIX + 128]
        c1_w, c1_l = sb("c1_w", [3 * IMR, 128], F16), sb("c1_l", [3 * IMR, 128], F16)
        cz_f = g1_0[:, CIN * PIX + 128:CIN * PIX + 128 + IMR]
        cz_h, cz_l = sb("cz_h", [128, IMR], F16), sb("cz_l", [128, IMR], F16)
        vecs = sb("vecs", [128, 7])
        zeros = sb("zeros", [128, 2 * QN])
        sbias = sb("sbias", [128, 2, 2 * QN])
        nbias = sb("nbias", [128, 2, QN])
        gamma, beta = sb("gamma", [128, 2, QN]), sb("beta", [128, 2, QN])
        per_n = sb("per_n", [128, 2, 2 * QN])
        bb = sb("bb", [CH, 1])
        bbr = g2_flat[0:CH, TOK + KQ * E:TOK + KQ * E + GT]
        avg = [sb("avg1", [128, 128]), sb("avg2", [128, 128])]
        psum_w = g1_1[0:CH, TAPS * CH + E:TAPS * CH + 2 * E]

        pixel_stats = mid[0:GT, o:o + 12 * CW]
        st0 = pixel_stats[:, 0:6 * CW].rearrange("p (c f) -> p c f", f=6)
        m0 = pixel_stats[:, 6 * CW:].rearrange("p (f c) -> p f c", c=CW)
        st = [sb(f"stat{i}", [128, 2, QN, 6]) for i in range(2)]
        rr = sb("rr", [128, 2, 2, 2 * QN])
        rs = sb("rs", [128, 2, 2, QN])
        sq, m2n = sb("sq", [128, 2, 2 * QN]), sb("m2n", [128, 2, 2 * QN])
        ms = sb("ms", [128, 2, 2, QN])
        vv = sb("vv", [128, 5, 2, QN])
        gn = [sb(f"gn{i}", [128, 2, 2, QN]) for i in range(2)]
        acc_tmp = r2_h[0:GT, :, :].rearrange("p a b -> p (a b)").bitcast(F32)[:, 0:E]

        c1p = [PS[0:2], PS[2:4]]
        cab = [PS[4], PS[5]]
        accp, stp = PS[6], PS[7]

        s_x = [sem(f"s_x{c}") for c in range(CIN)]; s_xc = sem("s_xc"); s_const = sem("s_const")
        s_w = sem("s_w"); s_c1l = sem("s_c1l"); s_exp = sem("s_exp"); s_bb = sem("s_bb"); s_w2 = sem("s_w2")
        s_d0 = sem("s_d0"); s_p0 = sem("s_p0"); s_xn = sem("s_xn"); s_xz = sem("s_xz"); s_xh = sem("s_xh")
        s_xs = sem("s_xs"); s_xst = sem("s_xst"); s_xcp = sem("s_xcp"); s_tr = sem("s_tr"); s_trc = sem("s_trc"); s_imz = sem("s_imz")
        w_in = [sem("w_in0"), sem("w_in1")]; w_sc = sem("w_sc"); w_hi = sem("w_hi"); w_split = sem("w_split")
        w_free = sem("w_free"); w_z = sem("w_z"); w_zc = sem("w_zc"); w_zcp = sem("w_zcp"); w_zst = [sem("w_zst0"), sem("w_zst1")]
        w_conv = sem("w_conv"); w_pair = [sem("w_pair0"), sem("w_pair1")]; p_pair = [sem("p_pair0"), sem("p_pair1")]; s_pz = sem("s_pz"); w_evh = sem("w_evh"); w_evl = sem("w_evl")
        v_in = [sem(f"v_in{c}") for c in range(CIN)]; v_sum = sem("v_sum"); v_d = sem("v_d"); v_acc = sem("v_acc"); v_accc = sem("v_accc"); v_tr = sem("v_tr"); v_trc = sem("v_trc")
        s_res = sem("s_res"); s_resc = sem("s_resc")
        im_in = [sem("im_in0"), sem("im_in1")]; p_c1 = sem("p_c1"); p_gelu1 = sem("p_gelu1"); p_h1 = sem("p_h1")
        p_img = sem("p_img"); p_conv = sem("p_conv"); p_gelu2 = sem("p_gelu2"); p_h2 = sem("p_h2")
        p_g2 = sem("p_g2")
        p_raw = sem("p_raw")
        p_bn = sem("p_bn")
        p_r = sem("p_r")
        p_av = sem("p_av")
        p_avc = sem("p_avc")
        p_var = sem("p_var")
        p_pow = sem("p_pow")
        p_gn = sem("p_gn")
        p_acc = sem("p_acc"); p_accc = sem("p_accc"); chain_m = sem("chain_m"); chain_c = sem("chain_c"); s_zero = sem("s_zero")

        block = ctx.enter_context(nc.Block())
        CONST = [
            (vecs[:], a["vecs"]), (ident[:], a["ident"]), (avg[0][:], a["avg1"]), (avg[1][:], a["avg2"]),
            (c1_f[:], a["c1"]), (onehot, a["onehot"]), (emb_rows, a["emb_rows"]),
            (cz_f[0:CH], a["cz"]), (cz_f[CH:128], a["cz"]),
            (w_f[0:CH], a["r2"]), (w_f[CH:128], a["r2"]), (w_f2[0:CH], a["r1"]), (w_f2[CH:128], a["r1"]),
        ]
        NCONST = 16 * len(CONST)

        def conv(pe, slot, q, bank, wh, wl, wp, ready, n):
            for k in range(TAPS + 6):
                if k < TAPS + 3:
                    w, src, t = (wh, img[slot], k) if k < TAPS else (wl, img[slot], k - 3)
                else:
                    w, src, t = wp, pair, k - TAPS - 3
                if k == TAPS + 3:
                    pe.wait_ge(ready, n)
                dy, dx = divmod(t, 3)
                for h in range(2):
                    last = pe.matmul(bank[CH * h:CH * h + CH, :], w[:, t, :],
                                     src[:, QN * q:QN * q + QN, dy + 8 * h:dy + 8 * h + 8, dx:dx + P],
                                     start=(k == 0), stop=(k == TAPS + 5))
            return last

        def copy_pair(eng, slot, q, done):
            src = img[slot][0:CH, QN * q:QN * q + QN].rearrange("p n r q -> p (n r q)")
            dst = pair[:, QN * q:QN * q + QN].rearrange("p n r q -> p (n r q)")
            eng.dma_start(dst[0:CH, :], src).then_inc(done, 16)
            eng.dma_start(dst[CH:128, 0:QN * PP - PAD], src[:, PAD:]).then_inc(done, 16)

        def schedule(eng, steps):
            steps(0, first=True)
            with eng.Fori(1, NG) as r:
                steps(r)
            with eng.Fori(1, NG - 1) as g:
                steps(g * 7, done=g)
                with eng.Fori(1, 7) as r:
                    steps(g * 7 + r)
            steps(7 * (NG - 1), done=NG - 1)
            with eng.Fori(1, 6) as r:
                steps(r + 7 * (NG - 1))
            steps(7 * NG - 1, last=True)

        V_ORDER = [(0, 1), (0, 0), (0, 2), (1, 1), (1, 0), (1, 2)]

        def shifted(c, t):
            dy, dx = divmod(t, 3)
            return z_in[:, c * TAPS + t, 2 - dy:2 - dy + P, 2 - dx:2 - dx + P]

        def interior(t):
            return t[:, :, 1:1 + P, 1:1 + P]

        @block.sync
        def _(sp):
            for c in range(CIN):
                sp.dma_start(x_raw[:, c * HP:(c + 1) * HP, :], a["x"][:, c]).then_inc(s_x[c], 16)
            for dst, src in CONST:
                sp.dma_start(dst, src).then_inc(s_const, 16)
            def load_rows(i, s, k):
                sp.wait_ge(w_free, k + 1)
                sp.wait_ge(w_split, k + 1)
                for h in range(2):
                    sp.dma_start(proj_in[s][CH * h:CH * h + CH],
                                 a["proj"][:, bass.ds(i * (2 * NBAT) + s * NBAT, NBAT), :]).then_inc(w_in[s], 16)

            def pair_rows(i, s, k):
                sp.wait_ge(w_hi, k + 1)
                for q in range(2):
                    sp.wait_ge(w_evl, k * 2 + (q + 1))
                    copy_pair(sp, s, q, w_pair[q])

            load_rows(0, 0, 0)
            sp.wait_ge(s_w, 8)
            for dy in range(3):
                low = slice(dy * IMR + 2 * TAPS, (dy + 1) * IMR)
                sp.dma_start(c1_w[low, :], c1_l[low, :]).then_inc(s_c1l, 16)
            sp.wait_ge(s_pz, 1)
            with sp.Fori(0, WBAT // 2 - 1) as i:
                load_rows(i, 1, i * 2 + 1)
                pair_rows(i, 0, i * 2)
                load_rows(i + 1, 0, i * 2 + 2)
                pair_rows(i, 1, i * 2 + 1)
            load_rows(WBAT // 2 - 1, 1, WBAT - 1)
            pair_rows(WBAT // 2 - 1, 0, WBAT - 2)
            sp.wait_ge(s_xst, 2 * 16)
            sp.dma_start(x_dram[2 * CIN:3 * CIN, :], x_dram[0:CIN, :]).then_inc(s_xcp, 16)
            pair_rows(WBAT // 2 - 1, 1, WBAT - 1)

            def im_load(b, s):
                for dy in range(3):
                    at = x_dram[0, bass.ds(b * (NBAT * PP) + dy * PAD, IML)]
                    src = bass.AP(at.tensor, at.offset, [[TOK * PP, 3 * CIN], [1, 3], [1, IML]])
                    dst = im2[s][dy * IMR:(dy + 1) * IMR].rearrange("p n r q -> p (n r q)")[:, 0:IML]
                    sp.dma_start(dst, src).then_inc(im_in[s], 16)

            sp.wait_ge(s_xcp, 16)
            im_load(0, 0)
            im_load(1, 1)
            for s in range(2):
                sp.wait_ge(w_zst[s], 16 * (WBAT // 2) + 16)
            sp.wait_ge(w_free, WBAT + 2)
            sp.wait_ge(w_split, WBAT + 2)
            for h in range(2):
                for c, before, n in ((1, v_sum, 1), (0, v_acc, 1), (2, v_sum, 2)):
                    if h:
                        sp.wait_ge(before, n)
                    sp.dma_start(z_in[:, c * TAPS:(c + 1) * TAPS].rearrange("p t r q -> p t (r q)"),
                                 z_dram[c * TAPS:(c + 1) * TAPS, h * EK:(h + 1) * EK, :].rearrange("t e q -> e t q"))\
                        .then_inc(v_in[c], 16)

            def next_im(b, s, n):
                sp.wait_ge(p_c1, n)
                im_load(b, s)

            def pair_patches(w, j):
                sp.wait_ge(p_h1, w + 1)
                sp.wait_ge(p_raw, w + 1)
                copy_pair(sp, j // 2, j % 2, p_pair[j % 2])

            def sp_steps(i, odd=True, even=True):
                if odd:
                    next_im(i * 2 + 3, 1, i * 4 + 4)
                pair_patches(i * 4 + 1, 1)
                pair_patches(i * 4 + 2, 2)
                if even:
                    next_im(i * 2 + 4, 0, i * 4 + 6)
                pair_patches(i * 4 + 3, 3)

            next_im(2, 0, 2)
            pair_patches(0, 0)
            with sp.Fori(0, QUADS // 4 - 2) as i:
                sp_steps(i)
                pair_patches(i * 4 + 4, 0)
            sp_steps(QUADS // 4 - 2, even=False)
            pair_patches(QUADS - 4, 0)
            sp_steps(QUADS // 4 - 1, odd=False, even=False)

        @block.tensor
        def _(pe):
            pe.wait_ge(s_const, NCONST)
            n = 0
            for w in range(HP):
                for k in range(KQ):
                    bank = PS[(n // 4) % 4]
                    if n == 0:
                        pe.wait_ge(s_xn, CW)
                    if n % 4 == 0 and n >= 16:
                        pe.wait_ge(s_trc, n // 4 - 3)
                    c, hh = divmod(k, 2)
                    mm = pe.transpose(bank[:, (n % 4) * GT:(n % 4) * GT + GT],
                                      x_n[:, c * HP + w, hh * 128:hh * 128 + 128], ident[0:GT, 0:GT])
                    n += 1
                    if n % 4 == 0 or n == HP * KQ:
                        mm.then_inc(s_tr, 1)
            pe.wait_ge(s_w, 12)
            pe.wait_ge(s_trc, (HP * KQ + 3) // 4)
            with pe.Fori(0, WBAT // 2) as i:
                for s in range(2):
                    k1 = i * 2 + (s + 1)
                    pe.wait_ge(w_split, k1 + 2)
                    pe.wait_ge(w_zc, k1)
                    for q in range(2):
                        for h in range(2):
                            for m, w in enumerate((cz_h, cz_l)):
                                mm = pe.matmul(PS[2 * q + h][0:IMR, :], w[:, :],
                                               img[s][:, QN * q:QN * q + QN, 1 + 8 * h:9 + 8 * h, 1:1 + P],
                                               start=(m == 0), stop=(m == 1))
                    mm.then_inc(w_z, 1)
                    for q in range(2):
                        pe.wait_ge(w_evl, i * 4 + (2 * s + q + 1))
                        conv(pe, s, q, cab[q], r2_h, r2_l, r2_p, w_pair[q], i * 64 + (s * 32 + 32)).then_inc(w_conv, 1)
            def v_accumulate(h):
                pe.wait_ge(v_in[0], 16 * h + 16)
                if h:
                    pe.wait_ge(v_accc, h)
                for t in range(TAPS):
                    mm = pe.matmul(PS[6][0:EK, 0:PIX], ident[0:EK, 0:EK], shifted(0, t), start=(t == 0), stop=(t == TAPS - 1))
                mm.then_inc(v_acc, 1)

            v_accumulate(0)
            for k, (h, c) in enumerate(V_ORDER):
                if k == 2:
                    v_accumulate(1)
                if c == 0:
                    pe.wait_ge(v_accc, h + 1)
                else:
                    pe.wait_ge(v_sum, 2 * h + c)
                if k >= 2:
                    pe.wait_ge(v_trc, k - 1)
                for hh in range(2):
                    mm = pe.transpose(PS[k % 2][:, hh * EK:hh * EK + EK], v_t[:, c, hh * 128:hh * 128 + 128],
                                      ident[0:EK, 0:EK])
                mm.then_inc(v_tr, 1)
            pe.wait_ge(v_trc, 2 * CIN)
            pe.wait_ge(s_bb, 1)
            for g in range(NG):
                bank = PS[2 + g % 2]
                if g >= 2:
                    pe.wait_ge(s_resc, g - 1)
                tk = slice(g * GT, g * GT + GT)
                for k in range(KQ):
                    pe.matmul(bank[0:GT, 0:E], xnT[:, k, tk], v_sb[:, k, :], start=(k == 0), stop=False)
                pe.matmul(bank[0:GT, 0:E], bbr[:, :], psum_w[:, :], start=False, stop=False)
                pe.matmul(bank[0:GT, 0:E], onehot[:, tk], emb_rows, start=False, stop=True).then_inc(s_res, 1)

            pe.wait_ge(s_c1l, 3 * 16)
            pe.wait_ge(s_resc, NG)

            def conv1(v, j, load):
                if j % 2 == 0:
                    pe.wait_ge(im_in[j // 2], load * 48 + 48)
                pe.wait_ge(p_gelu1, v + 1)
                for b in range(2):
                    mm = pe.matmul(c1p[j % 2][b][:, :], c1_w[:, :],
                                   im2[j // 2][:, QN * (j % 2) + 2 * b:QN * (j % 2) + 2 * b + 2, 0:P, 0:P],
                                   start=True, stop=True)
                mm.then_inc(p_c1, 1)

            def average(b, later=True):
                pe.wait_ge(p_r, b + 1)
                if later:
                    pe.wait_ge(p_avc, b)
                for L in range(2):
                    mm = pe.matmul(stp[:, L * 2 * QN:(L + 1) * 2 * QN], avg[L][:, :],
                                   rs[:, L].rearrange("p a n -> p (a n)"), start=True, stop=True)
                mm.then_inc(p_av, 1)

            def product(g):
                pe.wait_ge(p_g2, g * GQ + RING)
                if not isinstance(g, int) or g > 1:
                    pe.wait_ge(p_accc, g - 1)
                for q in range(HALF):
                    pe.matmul(accp[0:GT, 0:2 * E], g2_h[:, q, :], wc[:, q, :, :], start=(q == 0),
                              stop=(q == HALF - 1), skip_group_check=True)
                    mm = pe.matmul(accp[0:GT, 0:E], g2_l[:, q, :], wc[:, q, 0, :], start=False,
                                   stop=(q == HALF - 1), skip_group_check=True)
                mm.then_inc(p_acc, 1)

            def pe_steps(i, first=False, last=False, done=None):
                for j in range(RING):
                    u = i * 4 + j
                    v = i * 4 + (j + AHEAD)
                    nxt = not (last and j >= 1)
                    if nxt and not (done is not None and j == 3):
                        conv1(v, (j + AHEAD) % 4, i + (j + AHEAD) // 4)
                    pe.wait_ge(p_img, i * 4 + (j + 3))
                    pe.wait_ge(p_raw, i * 4 + (j + 1))
                    sl, q, bank = j // 2, j % 2, cab[j % 2]
                    conv(pe, sl, q, bank, r1_h, r1_l, r1_p, p_pair[q], i * 64 + (sl * 32 + 32)).then_inc(p_conv, 1)
                    average(v)
                    if j == 2 and done is not None:
                        conv1(i * 4 + 6, 2, i + 1)
                        product(done)

            for v in range(AHEAD):
                conv1(v, v, 0)
                average(v, v > 0)
            schedule(pe, pe_steps)
            average(QUADS + AHEAD)
            product(NG)

        @block.scalar
        def _(act):
            act.wait_ge(s_imz, 4)
            act.sem_inc(w_zc, 1)
            act.sem_inc(p_gelu1, 2)
            act.sem_inc(p_raw, 2)
            act.wait_ge(s_xc, 1)
            for c in range(XA):
                act.activation(x_n[:, c, :], x_raw[:, c, :], ACT.Identity, bias=m0[:, 4, c:c + 1],
                               scale=m0[:, 5, c:c + 1]).then_inc(s_xn, 1)
            act.wait_ge(s_xn, CW)
            act.wait_ge(s_xz, 2)
            x_n4 = x_n.rearrange("p c (r q) -> p c r q", q=P)
            act.activation(interior(x_hp), x_n4, ACT.Copy).then_inc(s_xh, 1)
            for r in range((HP * KQ + 3) // 4):
                act.wait_ge(s_tr, r + 1)
                for n in range(4 * r, min(4 * r + 4, HP * KQ)):
                    w, k = divmod(n, KQ)
                    cp = act.activation(xnT[:, k, :].rearrange("p (t w) -> p t w", w=HP)[:, :, w],
                                        PS[r % 4][:, (n % 4) * GT:(n % 4) * GT + GT], ACT.Copy)
                cp.then_inc(s_trc, 1)
            act.wait_ge(s_xh, 1)
            act.wait_ge(s_xs, 2)
            for part, src in enumerate((x_h, x_l)):
                act.dma_start(x_dram[part * CIN:(part + 1) * CIN, :].rearrange("c (p q) -> p c q", p=GT),
                              src.rearrange("p (c q) -> p c q", c=CIN)).then_inc(s_xst, 16)
            with act.Fori(0, WBAT // 2) as i:
                for s in range(2):
                    act.wait_ge(w_z, i * 2 + (s + 1))
                    act.wait_ge(w_zst[s], i * 16 + 16)
                    for q in range(2):
                        for h in range(2):
                            cp = act.activation(z_pad[s][:, QN * q:QN * q + QN, 1 + 8 * h:9 + 8 * h, 1:1 + P],
                                                PS[2 * q + h][0:IMR, :].rearrange("p (n r c) -> p n r c", n=QN, r=8),
                                                ACT.Copy)
                            cp.then_inc(w_zcp, 1)
                    act.wait_ge(w_zcp, i * 8 + (4 * s + 4))
                    act.sem_inc(w_zc, 1)
                    act.dma_start(z_dram[:, bass.ds(i * (2 * NBAT) + s * NBAT, NBAT), :],
                                  z_pad[s].rearrange("p n r c -> p n (r c)")).then_inc(w_zst[s], 16)
                    for q in range(2):
                        act.wait_ge(w_conv, i * 4 + (2 * s + q + 1))
                        act.wait_ge(s_xst, 2 * 16)
                        act.activation(wc[:, :, 0, bass.ds(i * (2 * NBAT) + (s * NBAT + QN * q), QN)],
                                       cab[q][:, :].rearrange("p (n q) -> p q n", n=QN), ACT.Copy).then_inc(w_evh, 1)
            def v_copy(h):
                act.wait_ge(v_acc, h + 1)
                if h:
                    act.wait_ge(v_tr, 2)
                act.activation(v_t[:, 0, :], PS[6][0:EK, 0:PIX], ACT.Copy).then_inc(v_accc, 1)

            v_copy(0)
            for k, (h, c) in enumerate(V_ORDER):
                if k == 2:
                    v_copy(1)
                act.wait_ge(v_tr, k + 1)
                for hh in range(2):
                    cp = act.activation(v_sb[:, 2 * c + hh, h * EK:h * EK + EK], PS[k % 2][:, hh * EK:hh * EK + EK],
                                        ACT.Copy, scale=1.0 / (S * S))
                cp.then_inc(v_trc, 1)

            def gelu(L, w, j):
                b = w + (0, AHEAD + 1)[L]
                act.wait_ge(p_gn, b + 1)
                if L == 0:
                    act.wait_ge(p_img, w + 1)
                for n in range(QN):
                    coef = gn[j % 2][:, :, L]
                    if L == 0:
                        src = c1p[j % 2][n // 2][:, (n % 2) * PIX:(n % 2) * PIX + PIX]
                        dst = g1[j % 2][:, n, :]
                    else:
                        src = dst = g2[j][:, n, :]
                    op = act.activation(dst, src, ACT.Gelu, bias=coef[:, 1, n:n + 1], scale=coef[:, 0, n:n + 1])
                op.then_inc((p_gelu1, p_gelu2)[L], 1)

            def raw(w, j):
                act.wait_ge(p_conv, w + 1)
                act.wait_ge(p_g2, w + 1)
                act.activation(g2[j].rearrange("p n q -> p (n q)"), cab[j % 2][:, :], ACT.Copy).then_inc(p_raw, 1)

            def high1(w, j):
                act.wait_ge(p_gelu1, w + 3)
                act.activation(interior(img[j // 2][:, QN * (j % 2):QN * (j % 2) + QN]),
                               g1[j % 2][:, :, :].rearrange("p n (r q) -> p n r q", q=P), ACT.Copy)\
                    .then_inc(p_h1, 1)

            def act_steps(i, first=False, last=False, done=None):
                for j in range(RING):
                    u = i * 4 + j
                    if not (first and j == 0):
                        raw(i * 4 + (j - 1), (j - 1) % 4)
                    if not (first and j <= 2):
                        gelu(1, i * 4 + (j - 3), (j - 3) % 4)
                    if not (last and j == 3):
                        high1(u + 1, (j + 1) % 4)
                    if not (last and j >= 2):
                        gelu(0, u + 2, (j + 2) % 4)

            gelu(0, 0, 0)
            high1(0, 0)
            gelu(0, 1, 1)
            schedule(act, act_steps)
            raw(QUADS - 1, 3)
            gelu(1, QUADS - 3, 1)
            gelu(1, QUADS - 2, 2)
            gelu(1, QUADS - 1, 3)

        @block.vector
        def _(dve):
            for i in range(2):
                dve.memset(img[i][:, :, :, :].rearrange("p n r q -> p (n r q)").bitcast(U32), 0).then_inc(s_imz, 1)
            dve.memset(expo[:, 0:8], -0.5).then_inc(s_exp, 1)
            dve.memset(expo[:, 8:32], 0.5).then_inc(s_exp, 1)
            dve.sem_inc(w_free, 2)
            dve.sem_inc(w_split, 2)
            dve.sem_inc(w_evl, 2)
            for s in range(2):
                dve.sem_inc(w_zst[s], 16)
            dve.sem_inc(p_img, 2)
            dve.sem_inc(p_g2, RING)
            dn = [0]

            def d_link(ins):
                dn[0] += 1
                ins.then_inc(s_d0, 1)
                dve.wait_ge(s_d0, dn[0])

            for c in range(CW):
                if c % HP == 0:
                    dve.wait_ge(s_x[c // HP], 16)
                ins = dve.bn_stats(st0[:, c, :], x_raw[:, c, :])
            d_link(ins)
            me, mo, qe, qo = st0[:, :, 1], st0[:, :, 4], st0[:, :, 2], st0[:, :, 5]
            d_link(dve.tensor_tensor(m0[:, 0, :], me, mo, ALU.add))
            d_link(dve.tensor_scalar(m0[:, 0, :], m0[:, 0, :], 0.5, None, ALU.mult))
            d_link(dve.tensor_tensor(m0[:, 1, :], me, mo, ALU.subtract))
            d_link(dve.tensor_tensor(m0[:, 1, :], m0[:, 1, :], m0[:, 1, :], ALU.mult))
            d_link(dve.tensor_tensor(m0[:, 2, :], qe, qo, ALU.add))
            d_link(dve.scalar_tensor_tensor(m0[:, 2, :], m0[:, 1, :], PIX / 4.0, m0[:, 2, :], ALU.mult, ALU.add))
            dve.tensor_scalar(m0[:, 2, :], m0[:, 2, :], 1.0 / (PIX - 1), None, ALU.mult).then_inc(s_p0, 1)
            for i in range(2):
                dve.memset(z_pad[i].rearrange("p n r q -> p (n r q)"), 0.0).then_inc(s_imz, 1)
            dve.wait_ge(s_p0, 2)
            d_link(dve.tensor_scalar(m0[:, 4, :], m0[:, 3, :], 1e-6, 4.0, ALU.add, ALU.mult))
            d_link(dve.reciprocal(m0[:, 5, :], m0[:, 4, :]))
            d_link(dve.scalar_tensor_tensor(m0[:, 4, :], m0[:, 0, :], -1.0, m0[:, 5, :], ALU.mult, ALU.mult))
            dve.sem_inc(s_xc, 1)
            for c in range(XA, CW):
                dve.tensor_scalar(x_n[:, c, :], x_raw[:, c, :], m0[:, 5, c:c + 1], m0[:, 4, c:c + 1], ALU.mult, ALU.add)\
                    .then_inc(s_xn, 1)
            dve.wait_ge(s_const, NCONST)
            wn = [0]

            def w_link(ins):
                wn[0] += 1
                ins.then_inc(s_w2, 1)
                dve.wait_ge(s_w2, wn[0])

            for f, hi, lo in ((w_f, r2_h[:, :, :], r2_l[:, :, :]), (w_f2, r1_h[:, :, :], r1_l[:, :, :]),
                              (c1_f[:, :], c1_w[:, :], c1_l[:, :]), (cz_f[:, :], cz_h[:, :], cz_l[:, :])):
                w_link(dve.tensor_scalar(f, f, S, None, ALU.mult))
                w_link(dve.tensor_copy(hi, f))
                dve.tensor_tensor(lo, f, hi, ALU.subtract).then_inc(s_w, 2)
            dve.wait_ge(s_w, 8)
            for lo, p in ((r2_l, r2_p), (r1_l, r1_p)):
                dve.tensor_copy(p[0:CH, :, :], lo[0:CH, 0:3, :]).then_inc(s_w, 1)
                dve.tensor_copy(p[CH:128, :, :], lo[CH:128, 3:6, :]).then_inc(s_w, 1)
            dve.memset(zeros[:, :], 0.0).then_inc(s_zero, 1)
            for i in range(2):
                dve.memset(st[i][:, :, :, :].rearrange("p a b c -> p (a b c)"), 0.0).then_inc(s_zero, 1)
            dve.wait_ge(s_zero, 3)
            for L in range(2):
                for dst, src, f, w in ((sbias, 0, S, 2 * QN), (nbias, 0, -S, QN), (gamma, 1, 1.0, QN), (beta, 2, 1.0, QN)):
                    dve.tensor_scalar(dst[:, L, :], zeros[:, 0:w], vecs[:, 3 * L + src:3 * L + src + 1], f,
                                      ALU.add, ALU.mult).then_inc(s_zero, 1)
                dve.memset(per_n[:, L, :], 2.0 / (PIX if L == 0 else HALF)).then_inc(s_zero, 1)
            w_link(dve.tensor_tensor(bb[:, :], vecs[0:CH, 0:1], vecs[0:CH, 6:7], ALU.add))
            w_link(dve.memset(bbr[:, :], 1.0 / S))
            w_link(dve.tensor_scalar(bbr[:, :], bbr[:, :], bb[:, 0:1], None, ALU.mult))
            dve.wait_ge(s_imz, 4)

            def high_rows(k, s, n):
                dve.wait_ge(w_in[s], n * 32 + 32)
                dve.tensor_scalar(proj_in[s], proj_in[s], S, None, ALU.mult).then_inc(w_sc, 1)
                dve.wait_ge(w_sc, k + 1)
                dve.tensor_copy(interior(img[s]), proj_in[s].rearrange("p n (r q) -> p n r q", q=P)).then_inc(w_hi, 1)

            def sum_rows(k, s):
                dve.tensor_reduce(psum_w[:, bass.ds(k * NBAT, NBAT)], proj_in[s][0:CH], AX_X, ALU.add)\
                    .then_inc(w_free, 1)

            def split_rows(k, s, n):
                high_rows(k, s, n)
                sum_rows(k, s)

            def low_weights(i, s):
                for q in range(2):
                    dve.wait_ge(w_evh, i * 4 + (2 * s + q + 1))
                    at = bass.ds(i * (2 * NBAT) + (s * NBAT + QN * q), QN)
                    dve.tensor_tensor(wc[:, :, 1, at], cab[q][:, :].rearrange("p (n q) -> p q n", n=QN),
                                      wc[:, :, 0, at], ALU.subtract).then_inc(w_evl, 1)

            high_rows(0, 0, 0)
            dve.wait_ge(s_xh, 1)
            x_n4 = x_n.rearrange("p c (r q) -> p c r q", q=P)
            dve.tensor_tensor(interior(x_lp[:, HP:CW]), x_n4[:, HP:CW], interior(x_hp[:, HP:CW]), ALU.subtract)\
                .then_inc(s_xs, 1)
            sum_rows(0, 0)
            with dve.Fori(0, WBAT // 2 - 1) as i:
                split_rows(i * 2 + 1, 1, i)
                low_weights(i, 0)
                split_rows(i * 2 + 2, 0, i + 1)
                low_weights(i, 1)
            split_rows(WBAT - 1, 1, WBAT // 2 - 1)
            low_weights(WBAT // 2 - 1, 0)
            low_weights(WBAT // 2 - 1, 1)
            dve.wait_ge(w_free, WBAT + 2)
            dve.sem_inc(s_bb, 1)
            vd = 0
            for h in range(2):
                for c in range(1, CIN):
                    dve.wait_ge(v_in[c], 16 * h + 16)
                    if h:
                        dve.wait_ge(v_tr, V_ORDER.index((0, c)) + 1)
                    o = v_t[:, c, :].rearrange("p (r q) -> p r q", q=P)
                    for t in range(TAPS):
                        if t == 0:
                            ins = dve.tensor_copy(o, shifted(c, t))
                        else:
                            dve.wait_ge(v_d, vd)
                            ins = dve.tensor_tensor(o, shifted(c, t), o, ALU.add)
                        vd += 1
                        ins.then_inc(v_d, 1)
                    dve.wait_ge(v_d, vd)
                    dve.sem_inc(v_sum, 1)
            for g in range(NG):
                dve.wait_ge(s_res, g + 1)
                dve.tensor_copy(h_tok[:, g, :], PS[2 + g % 2][0:GT, 0:E]).then_inc(s_resc, 1)

            LINKS = 4

            def stats(L, w, j, patches=range(QN)):
                dve.wait_ge((p_c1, p_raw)[L], w + (1, 3)[L])
                for n in patches:
                    src = c1p[j % 2][n // 2][:, (n % 2) * PIX:(n % 2) * PIX + PIX] if L == 0 else g2[j][:, n, :]
                    op = dve.bn_stats(st[j % 2 if L == 0 else (j + AHEAD + 1) % 2][:, L, n, :], src)
                return op

            def mean(b, k):
                f = st[k][:, :, :, :].rearrange("p l n (m f) -> p l (n m) f", f=3)
                dve.wait_ge(p_bn, b + 1)
                dve.tensor_tensor(rr[:, :, 0], f[:, :, :, 1], sbias[:, :, :], ALU.add).then_inc(chain_m, 1)
                dve.tensor_tensor(m2n[:, :, :], f[:, :, :, 2], per_n[:, :, :], ALU.mult).then_inc(chain_m, 1)

            def mean_square(b):
                dve.wait_ge(chain_m, b * LINKS + 1)
                dve.tensor_tensor(sq[:, :, :], rr[:, :, 0], rr[:, :, 0], ALU.mult).then_inc(chain_m, 1)

            def second_moment(b):
                dve.wait_ge(chain_m, b * LINKS + 3)
                dve.tensor_tensor(rr[:, :, 1], m2n[:, :, :], sq[:, :, :], ALU.add).then_inc(chain_m, 1)

            def both_halves(b):
                r = rr[:, :, :, :].rearrange("p l a (n m) -> p l a n m", m=2)
                dve.wait_ge(chain_m, b * LINKS + 4)
                dve.tensor_tensor(rs[:, :, :, :], r[:, :, :, :, 0], r[:, :, :, :, 1], ALU.add).then_inc(p_r, 1)

            def copy_average(b):
                dve.wait_ge(p_av, b + 1)
                dve.tensor_copy(ms[:, :, :, :].rearrange("p l a b -> p (l a b)"), stp[:, 0:4 * QN]).then_inc(p_avc, 1)

            def minus_square(b):
                m = ms[:, :, 0, :]
                dve.wait_ge(p_avc, b + 1)
                dve.scalar_tensor_tensor(vv[:, 0], m, -1.0, m, ALU.mult, ALU.mult).then_inc(chain_c, 1)
                dve.tensor_tensor(vv[:, 3], m, nbias[:, :, :], ALU.add).then_inc(chain_c, 1)

            def variance(b):
                dve.wait_ge(chain_c, b * LINKS + 1)
                dve.scalar_tensor_tensor(vv[:, 1], vv[:, 0], EPS * S * S, ms[:, :, 1, :], ALU.add, ALU.add)\
                    .then_inc(p_var, 1)

            def scale(b, k, g1_done, g2_done):
                dve.wait_ge(p_gelu1, g1_done)
                if g2_done is not None:
                    dve.wait_ge(p_gelu2, g2_done)
                dve.wait_ge(p_pow, b + 1)
                dve.tensor_tensor(gn[k][:, 0], vv[:, 2], gamma[:, :, :], ALU.mult).then_inc(chain_c, 1)

            def shift(b, k):
                dve.wait_ge(chain_c, b * LINKS + 3)
                dve.tensor_tensor(vv[:, 4], vv[:, 3], gn[k][:, 0], ALU.mult).then_inc(chain_c, 1)

            def bias(b, k):
                dve.wait_ge(chain_c, b * LINKS + 4)
                dve.tensor_tensor(gn[k][:, 1], beta[:, :, :], vv[:, 4], ALU.subtract).then_inc(p_gn, 1)

            def high2(w, j, at):
                dve.wait_ge(p_gelu2, w + 1)
                dve.tensor_scalar(g2_h[:, :, at], g2[j].rearrange("p n q -> p q n"), 1.0, None, ALU.mult)\
                    .then_inc(p_h2, 1)

            def low2(w, j, at):
                dve.wait_ge(p_h2, w + 1)
                dve.tensor_tensor(g2_l[:, :, at], g2[j].rearrange("p n q -> p q n"), g2_h[:, :, at], ALU.subtract)\
                    .then_inc(p_g2, 1)

            def take_product(g):
                dve.wait_ge(p_acc, g)
                dve.tensor_scalar(acc_tmp[:, :], accp[0:GT, E:2 * E], 1.0 / (S * S), None, ALU.mult).then_inc(s_d0, 1)
                gi = g - 1
                hg = h_tok[:, gi, :] if isinstance(g, int) else h_tok[:, bass.ds(gi, 1), :].rearrange("p o e -> p (o e)")
                dve.wait_ge(s_d0, gi * 3 + (dn[0] + 1))
                dve.tensor_tensor(hg, hg, acc_tmp[:, :], ALU.add).then_inc(s_d0, 1)
                dve.wait_ge(s_d0, gi * 3 + (dn[0] + 2))
                dve.scalar_tensor_tensor(hg, accp[0:GT, 0:E], 1.0 / (S * S), hg, ALU.mult, ALU.add).then_inc(s_d0, 1)
                dve.wait_ge(s_d0, gi * 3 + (dn[0] + 3))
                dve.sem_inc(p_accc, 1)

            def dve_step(i, j, front=True, back=True, split=True, coef=True, done=None, at=None,
                         first=False, tail=False):
                cb, ck = i * 4 + (j + 2), j % 2
                b, k = i * 4 + (j + 3), (j + 1) % 2
                stat = front or back
                if coef:
                    copy_average(cb)
                    minus_square(cb)
                    variance(cb)
                if back:
                    last = stats(1, i * 4 + (j - 1), (j - 1) % 4, range(0, 1))
                if front:
                    last = stats(0, b, (j + 3) % 4)
                if back:
                    last = stats(1, i * 4 + (j - 1), (j - 1) % 4, range(1, 2))
                if coef:
                    scale(cb, ck, (QUADS + 2 if tail else cb + 1), None if first else i * 4 + (j - 3))
                if back:
                    last = stats(1, i * 4 + (j - 1), (j - 1) % 4, range(2, 3))
                if coef:
                    shift(cb, ck)
                if back:
                    last = stats(1, i * 4 + (j - 1), (j - 1) % 4, range(3, QN))
                if stat:
                    last.then_inc(p_bn, 1)
                if coef:
                    bias(cb, ck)
                if stat:
                    mean(b, k)
                if stat:
                    mean_square(b)
                if split:
                    if done is not None and j == 3:
                        take_product(done)
                    high2(i * 4 + (j - 3), (j - 3) % 4, at)
                if stat:
                    second_moment(b)
                    both_halves(b)
                if split:
                    low2(i * 4 + (j - 3), (j - 3) % 4, at)

            def dve_steps(i, first=False, last=False, done=None, at=None):
                for j in range(RING):
                    c = None
                    if j == 3:
                        c = bass.ds(at * (4 * QN), QN)
                    elif done is not None:
                        c = bass.ds(GT + (j - 3) * QN, QN)
                    elif not first:
                        c = bass.ds(at * (4 * QN) + (j - 3) * QN, QN)
                    dve_step(i, j, front=not (last and j >= 1), back=not (first and j == 0), split=c is not None,
                             done=done, at=c, first=first, tail=last and j >= 2)

            for u in range(-AHEAD, 0):
                dve_step(0, u, back=False, split=False, coef=u > -AHEAD, first=True)
            dve_steps(0, first=True, at=0)
            with dve.Fori(1, 7) as r:
                dve_steps(r, at=r)
            with dve.Fori(1, NG - 1) as g:
                dve_steps(g * 7, done=g, at=0)
                with dve.Fori(1, 7) as r:
                    dve_steps(g * 7 + r, at=r)
            dve_steps(7 * (NG - 1), done=NG - 1, at=0)
            with dve.Fori(1, 6) as r:
                dve_steps(r + 7 * (NG - 1), at=r)
            dve_steps(7 * NG - 1, last=True, at=6)
            dve_step(QUADS // 4, 0, front=False, at=bass.ds(GT - 3 * QN, QN), tail=True)
            dve_step(QUADS // 4, 1, front=False, back=False, at=bass.ds(GT - 2 * QN, QN), tail=True)
            high2(QUADS - 1, 3, bass.ds(GT - QN, QN))
            low2(QUADS - 1, 3, bass.ds(GT - QN, QN))
            take_product(NG)

        @block.gpsimd
        def _(pool):
            pool.memset(x_h.bitcast(U32), 0).then_inc(s_xz, 1)
            pool.memset(x_l.bitcast(U32), 0).then_inc(s_xz, 1)
            pool.memset(pair[:, :, :, :].rearrange("p n r q -> p (n r q)").bitcast(U32), 0).then_inc(s_pz, 1)
            pool.wait_ge(s_exp, 2)
            pool.wait_ge(s_p0, 1)
            pool.tensor_tensor(m0[:, 3, :], m0[:, 2, :], expo[0:GT, 8:8 + CW], ALU.pow).then_inc(s_p0, 1)
            x_n4 = x_n.rearrange("p c (r q) -> p c r q", q=P)
            pool.wait_ge(s_xh, 1)
            pool.tensor_tensor(interior(x_lp[:, 0:HP]), x_n4[:, 0:HP], interior(x_hp[:, 0:HP]), ALU.subtract).then_inc(s_xs, 1)
            pool.wait_ge(s_xs, 2)
            with pool.Fori(0, WBAT // 2) as i:
                for s in range(2):
                    rows = proj_in[s].rearrange("p n (r q) -> p n r q", q=P)
                    pool.wait_ge(w_hi, i * 2 + (s + 1))
                    pool.tensor_tensor(interior(img[s])[CH:128], rows[CH:128], interior(img[s])[CH:128],
                                       ALU.subtract).then_inc(w_split, 1)

            def power(b):
                pool.wait_ge(p_var, b + 1)
                pool.tensor_tensor(vv[:, 2], vv[:, 1], expo[:, 0:2 * QN].rearrange("p (l n) -> p l n", l=2), ALU.pow)\
                    .then_inc(p_pow, 1)

            def low1(w, j):
                dst = interior(img[j // 2][:, QN * (j % 2):QN * (j % 2) + QN])[CH:128]
                src = g1[j % 2][CH:128, :, :].rearrange("p n (r q) -> p n r q", q=P)
                pool.wait_ge(p_h1, w + 1)
                pool.tensor_tensor(dst, src, dst, ALU.subtract).then_inc(p_img, 1)

            def pool_steps(i, first=False, last=False, done=None):
                for j in range(RING):
                    u = i * 4 + j
                    pool.wait_ge(p_img, u + 3)
                    power(u + 2)
                    if not (last and j == 3):
                        pool.wait_ge(p_pow, u + 3)
                        low1(u + 1, (j + 1) % 4)

            pool.wait_ge(w_split, WBAT + 2)
            power(0)
            pool.wait_ge(p_pow, 1)
            low1(0, 0)
            pool.wait_ge(p_img, 3)
            power(1)
            pool.wait_ge(p_pow, 2)
            schedule(pool, pool_steps)
            power(QUADS + 2)
            power(QUADS + 3)


def tower(nc, a, out, h_tok, ident, expo, PS):
    with ExitStack() as ctx:
        def sb(name, shape, dt=F32):
            return ctx.enter_context(nc.sbuf_tensor(name, shape, dt))

        def sem(name):
            return ctx.enter_context(nc.semaphore(name))

        x_tok = sb("x_tok", [GT, NG, E])
        h1_tok = sb("h1_tok", [GT, NG, E])
        x_T = sb("x_T", [EK, 2 * TOK + 64])
        x_T2 = x_T[:, 0:2 * TOK].rearrange("p (k t) -> p k t", t=TOK)
        qk_T = [sb("q_T", [128, NCH * TOK + 64]), sb("k_T", [128, NCH * TOK + 64])]
        ctx_T = sb("ctx_T", [128, NCH, TOK])
        v1 = sb("v1", [128, NPAIR, HEADS, HPAD])
        v2b = sb("v2b", [128, B * HEADS * HPAD])
        v2 = v2b[0:64, :].rearrange("p (b h d) -> p b h d", b=B, h=HEADS)
        vn = sb("vn", [128, HEADS, HPAD])
        prob = [sb(f"prob{i}", [128, HEADS, SEQ]) for i in range(2)]
        prob_T = [sb(f"prob_T{i}", [SEQ, HEADS, 128]) for i in range(2)]
        mx, sm, ri = sb("mx", [128, HEADS]), sb("sm", [128, HEADS]), sb("ri", [128, HEADS])
        wqk = [[sb(f"w{n}{L}", [EK, 2, 128 * NCH]) for n in "qk"] for L in range(2)]
        wv = [sb(f"wv{L}", [EK, 2, E]) for L in range(2)]
        wo = [sb(f"wo{L}", [128, NCH, E]) for L in range(2)]
        bqk = [sb(f"bqk{L}", [128, 2 * NCH]) for L in range(2)]
        rows = sb("rows", [128, 8, E])
        wg = sb("wg", [EK, 2, NE])
        b1 = [sb(f"b1_{i}", [128, HC]) for i in range(2)]
        b2 = sb("b2", [NE, E])
        iota = sb("iota", [GT, NE])
        ln_st, ln_mv = sb("ln_st", [GT, NG, 6]), sb("ln_mv", [GT, NG, 2])
        ln_r = sb("ln_r", [GT, 2, NG])
        lg, top, gate, gtmp = (sb(n, [GT, NG, NE]) for n in ("lg", "top", "gate", "gtmp"))
        topi = sb("topi", [GT, NG, NE], U32)
        idx = sb("idx", [GT, NG, 2])
        gg = sb("gg", [GT, 4, NG])
        gate_T = sb("gate_T", [NE, NG * GT])
        w1 = [sb(f"w1_{i}", [EK, 2, HID]) for i in range(2)]
        w2 = [sb(f"w2_{i}", [128, HC, E]) for i in range(2)]
        w1_s = [sb(f"w1s_{i}", [EK, 2, 2, HID], F16) for i in range(2)]
        w2_s = [sb(f"w2s_{i}", [128, HC, 2, E], F16) for i in range(2)]
        b1_s = [sb(f"b1s_{i}", [128, HC]) for i in range(2)]
        gate_s = sb("gate_s", [GT, NG, NE])
        hid_h, hid_l = (v2b[:, m * HC * TOK // 2:(m + 1) * HC * TOK // 2].bitcast(F16)
                        .rearrange("p (c t) -> p c t", t=TOK) for m in range(2))
        v1f = v1[:, :, :, :].rearrange("p a b c -> p (a b c)")
        hid_f = [v1f[:, m * HT:(m + 1) * HT] for m in range(4)]
        x_h, x_l = (qk_T[0][0:EK, m * TOK:(m + 1) * TOK].bitcast(F16).rearrange("p (k t) -> p k t", t=TOK)
                    for m in range(2))

        t_const = sem("t_const"); t_attn = [sem("t_attn0"), sem("t_attn1")]
        t_x = sem("t_x")
        t_tr = sem("t_tr"); t_trc = sem("t_trc")
        t_qk = sem("t_qk"); t_qkc = sem("t_qkc"); t_v = sem("t_v"); t_vc = sem("t_vc")
        t_sc = sem("t_sc"); t_sub = sem("t_sub"); t_exp = sem("t_exp"); t_p = sem("t_p")
        t_ptr = sem("t_ptr"); t_ptc = sem("t_ptc"); t_ctx = sem("t_ctx"); t_ctxc = sem("t_ctxc")
        t_o = sem("t_o"); t_oc = sem("t_oc")
        t_var = sem("t_var"); t_rs = sem("t_rs"); t_d = sem("t_d"); t_z = sem("t_z"); t_vz = sem("t_vz")
        t_lg = sem("t_lg"); t_lgd = sem("t_lgd"); t_ge = sem("t_ge"); t_gate = sem("t_gate")
        t_gt = sem("t_gt"); t_gtc = sem("t_gtc"); t_b2 = sem("t_b2"); t_b2c = sem("t_b2c")
        e_w = [sem("e_w0"), sem("e_w1")]; m_w = sem("m_w"); m_x = sem("m_x")
        e_h = sem("e_h"); e_hg = sem("e_hg"); e_hi = sem("e_hi"); e_low = sem("e_low"); e_ya = sem("e_ya"); e_y = sem("e_y"); e_yc = sem("e_yc")
        t_done = sem("t_done"); t_h1 = sem("t_h1"); s_out = sem("s_out")
        block = ctx.enter_context(nc.Block())

        CONST = [(rows[:], a["rows"]), (wg[:], a["wg"]), (b2[:], a["b2"]), (iota[:], a["iota"])]
        ATTN = [[(wqk[L][0][:], a[f"wq{L}"]), (wqk[L][1][:], a[f"wk{L}"]), (wv[L][:], a[f"wv{L}"]),
                 (wo[L][:], a[f"wo{L}"]), (bqk[L][:], a[f"bqk{L}"])] for L in range(2)]
        @block.sync
        def _(sp):
            for L in range(2):
                for dst, src in ATTN[L]:
                    sp.dma_start(dst, src).then_inc(t_attn[L], 16)
                if L == 0:
                    for dst, src in CONST:
                        sp.dma_start(dst, src).then_inc(t_const, 16)
            def load_expert(i, s):
                for dst, src in ((w1[s], a["w1"]), (w2[s], a["w2"])):
                    sp.dma_start(dst[:], src[bass.ds(i * 2 + s, 1)].rearrange("o p k h -> (o p) k h")).then_inc(e_w[s], 16)
                sp.dma_start(b1[s][:], a["b1"][bass.ds(i * 2 + s, 1)].rearrange("o p k -> (o p) k")).then_inc(e_w[s], 16)

            load_expert(0, 0)
            load_expert(0, 1)
            with sp.Fori(1, NE // 2) as i:
                for s in range(2):
                    sp.wait_ge(m_w, i * 10 + (s * 5 - 5))
                    load_expert(i, s)
            sp.wait_ge(t_done, 1)
            sp.dma_start(out.rearrange("(g p) e -> p g e", p=GT), h_tok[:, :, :]).then_inc(s_out, 16)
            sp.wait_ge(s_out, 16)

        @block.tensor
        def _(pe):
            def transpose_tokens(n, src):
                for g in range(NG):
                    pe.wait_ge(t_x, n * NG + g + 1)
                    k = n * NG + g
                    if g >= 2 or n:
                        pe.wait_ge(t_trc, k - 1)
                    for c in range(2):
                        mm = pe.transpose(PS[6 + g % 2][0:EK, c * GT:c * GT + GT], src[:, g, c * EK:c * EK + EK],
                                          ident[0:GT, 0:GT])
                    mm.then_inc(t_tr, 1)

            def attention(L):
                pe.wait_ge(t_attn[L], 16 * len(ATTN[L]))
                pe.wait_ge(t_trc, (L + 1) * NG)
                n = 0
                for m in range(2):
                    for j in range(NCH):
                        for h in range(2):
                            k = L * 12 + n
                            if k >= 2:
                                pe.wait_ge(t_qkc, k - 1)
                            for c in range(2):
                                mm = pe.matmul(PS[4 + n % 2][:, 0:HT], wqk[L][m][:, c, 128 * j:128 * j + 128],
                                               x_T2[:, c, h * HT:h * HT + HT], start=(c == 0), stop=(c == 1))
                            mm.then_inc(t_qk, 1)
                            n += 1
                for n in range(NPAIR):
                    k = L * NPAIR + n
                    if k >= 2:
                        pe.wait_ge(t_vc, k - 1)
                    for r in range(2):
                        o = PS[6 + n % 2][64 * r:64 * r + 64, 0:E] if L == 0 else PS[6 + n % 2][0:64, r * E:r * E + E]
                        t0 = (2 * n + r) * SEQ
                        for c in range(2):
                            mm = pe.matmul(o, x_T[:, c * TOK + t0:c * TOK + t0 + 64], wv[L][:, c, :],
                                           start=(c == 0), stop=(c == 1))
                    mm.then_inc(t_v, 1)
                pe.wait_ge(t_qkc, (L + 1) * 12)
                pe.wait_ge(t_vc, (L + 1) * NPAIR)
                lhs, rhs = (qk_T[1], qk_T[0]) if L == 0 else (qk_T[0], qk_T[1])
                for n in range(NPAIR + 1 + L):
                    k = L * NPAIR + n
                    if n < NPAIR:
                        if k >= 1:
                            pe.wait_ge(t_sub, k)
                        for c in range(NCH):
                            for j in range(4):
                                for r in range(2):
                                    t0 = c * TOK + (2 * n + r) * SEQ
                                    mm = pe.matmul(PS[j][64 * r:64 * r + 64, c * SEQ:c * SEQ + SEQ],
                                                   lhs[32 * j:32 * j + 32, t0:t0 + 64],
                                                   rhs[32 * j:32 * j + 32, t0:t0 + SEQ], start=True, stop=True)
                        mm.then_inc(t_sc, 1)
                    if n == 0:
                        continue
                    k, n0 = k - 1, n - 1
                    if n <= NPAIR:
                        pe.wait_ge(t_p, k + 1)
                    if L == 0:
                        if k >= 1:
                            pe.wait_ge(t_ctxc, k)
                        for hd in range(HEADS):
                            for r in range(2):
                                c, j = divmod(hd, 4)
                                mm = pe.matmul(PS[4 + r][32 * j:32 * j + 32, c * SEQ:c * SEQ + SEQ],
                                               vn[64 * r:64 * r + SEQ, hd, :],
                                               prob[n0 % 2][64 * r:64 * r + SEQ, c * 4 + j, :], start=True, stop=True)
                        mm.then_inc(t_ctx, 1)
                    else:
                        if n0 < NPAIR:
                            if n0 >= 1:
                                pe.wait_ge(t_ptc, n0)
                            for hd in range(HEADS):
                                mm = pe.transpose(PS[4 + hd // 4][0:SEQ, (hd % 4) * 128:(hd % 4) * 128 + 128],
                                                  prob[n0 % 2][:, hd, :], ident[:, :])
                            mm.then_inc(t_ptr, 1)
                        if n0 == 0:
                            continue
                        m = n0 - 1
                        pe.wait_ge(t_ptc, m + 1)
                        pe.wait_ge(t_ctxc, NPAIR + m)
                        for r in range(2):
                            for hd in range(HEADS):
                                c, j = divmod(hd, 4)
                                mm = pe.matmul(PS[7][32 * j:32 * j + 32, (r * NCH + c) * SEQ:(r * NCH + c) * SEQ + SEQ],
                                               v2[0:SEQ, 2 * m + r, hd, :], prob_T[m % 2][:, hd, 64 * r:64 * r + SEQ],
                                               start=True, stop=True)
                        mm.then_inc(t_ctx, 1)
                pe.wait_ge(t_ctxc, (L + 1) * NPAIR)
                for g in range(NG):
                    k = L * NG + g
                    if k >= 2:
                        pe.wait_ge(t_oc, k - 1)
                    for c in range(NCH):
                        mm = pe.matmul(PS[g % 2][0:GT, 0:E], ctx_T[:, c, g * GT:g * GT + GT], wo[L][:, c, :],
                                       start=(c == 0), stop=(c == NCH - 1))
                    mm.then_inc(t_o, 1)

            pe.wait_ge(t_z, 1)
            transpose_tokens(0, h_tok)
            attention(0)
            transpose_tokens(1, x_tok)
            attention(1)
            transpose_tokens(2, x_tok)
            pe.wait_ge(t_trc, 3 * NG)
            pe.wait_ge(t_const, 16 * len(CONST))
            for g in range(NG):
                for c in range(2):
                    mm = pe.matmul(PS[0][0:GT, g * NE:g * NE + NE], x_T2[:, c, g * GT:g * GT + GT], wg[:, c, :],
                                   start=(c == 0), stop=(c == 1))
            mm.then_inc(t_lg, 1)
            pe.wait_ge(t_lgd, 1)
            pe.wait_ge(m_x, 2)

            def hidden(i, s, chunks):
                pe.wait_ge(m_w, i * 10 + (s * 5 + 5))
                for n in chunks:
                    hc, h = n // 2, n % 2
                    pe.wait_ge(e_hg, i * (4 * HC) + (s * 2 * HC + n + 1))
                    terms = [(wp, xp, c) for c in range(2) for wp, xp in ((0, x_h), (0, x_l), (1, x_h))]
                    for m, (wp, xp, c) in enumerate(terms):
                        mm = pe.matmul(PS[n % 4][:, 0:HT], w1_s[s][:, wp, c, 128 * hc:128 * hc + 128],
                                       xp[:, c, h * HT:h * HT + HT], start=(m == 0), stop=(m == 5))
                    mm.then_inc(e_h, 1)

            def outputs(i, s):
                pe.wait_ge(e_low, i * (4 * HC) + (s * 2 * HC + 2 * HC + 4))
                for g in range(NG):
                    pe.wait_ge(e_yc, i * (2 * NG) + (s * NG + g + 1))
                    bank, gt = PS[4 + (s * NG + g) % 2], slice(g * GT, g * GT + GT)
                    for hc in range(HC):
                        pe.matmul(bank[0:GT, 0:2 * E], hid_h[:, hc, gt], w2_s[s][:, hc, :, :],
                                  start=(hc == 0), stop=(hc == HC - 1), skip_group_check=True)
                        mm = pe.matmul(bank[0:GT, 0:E], hid_l[:, hc, gt], w2_s[s][:, hc, 0, :], start=False,
                                       stop=(hc == HC - 1), skip_group_check=True)
                    mm.then_inc(e_y, 1)

            FIRST, REST = range(4), range(4, 2 * HC)
            hidden(0, 0, FIRST)
            with pe.Fori(0, NE // 2 - 1) as i:
                hidden(i, 0, REST)
                hidden(i, 1, FIRST)
                outputs(i, 0)
                hidden(i, 1, REST)
                hidden(i + 1, 0, FIRST)
                outputs(i, 1)
            hidden(NE // 2 - 1, 0, REST)
            hidden(NE // 2 - 1, 1, FIRST)
            outputs(NE // 2 - 1, 0)
            hidden(NE // 2 - 1, 1, REST)
            outputs(NE // 2 - 1, 1)
            pe.wait_ge(e_hg, NE * 2 * HC + 4)
            for g in range(NG):
                mm = pe.transpose(PS[1 + g // 4][0:NE, (g % 4) * GT:(g % 4) * GT + GT], gate[:, g, :], ident[0:GT, 0:GT])
            mm.then_inc(t_gt, 1)
            pe.wait_ge(t_gtc, 1)
            pe.wait_ge(e_yc, NE * NG + 2)
            for g in range(NG):
                if g >= 2:
                    pe.wait_ge(t_b2c, g - 1)
                pe.matmul(PS[3 + g % 2][0:GT, 0:E], gate_T[:, g * GT:g * GT + GT], b2[:, :], start=True, stop=True)\
                    .then_inc(t_b2, 1)

        @block.scalar
        def _(act):
            act.sem_inc(e_hg, 4)

            def tokens_out(n):
                for g in range(NG):
                    act.wait_ge(t_tr, n * NG + g + 1)
                    act.activation(x_T2[:, :, g * GT:g * GT + GT],
                                   PS[6 + g % 2][0:EK, 0:2 * GT].rearrange("p (k t) -> p k t", t=GT), ACT.Copy)\
                        .then_inc(t_trc, 1)

            def attention(L):
                n = 0
                for m in range(2):
                    for j in range(NCH):
                        for h in range(2):
                            act.wait_ge(t_qk, L * 12 + n + 1)
                            act.activation(qk_T[m][:, j * TOK + h * HT:j * TOK + h * HT + HT], PS[4 + n % 2][:, 0:HT],
                                           ACT.Identity, bias=bqk[L][:, m * NCH + j:m * NCH + j + 1]).then_inc(t_qkc, 1)
                            n += 1
                for n in range(NPAIR + 1 + L):
                    if n < NPAIR:
                        k = L * NPAIR + n
                        act.wait_ge(t_sub, k + 1)
                        p = prob[n % 2][:, :, :]
                        act.activation(p, p, ACT.Exp, scale=DH ** -0.5).then_inc(t_exp, 1)
                    if L == 1 and 1 <= n <= NPAIR:
                        act.wait_ge(t_ptr, n)
                        if n >= 3:
                            act.wait_ge(t_ctx, NPAIR + n - 2)
                        for b in range(3):
                            cp = act.activation(prob_T[(n - 1) % 2][:, 4 * b:4 * b + 4, :],
                                                PS[4 + b][0:SEQ, :].rearrange("p (h t) -> p h t", t=128), ACT.Copy)
                        cp.then_inc(t_ptc, 1)
                    n0 = n - 1 - L
                    if n0 >= 0:
                        act.wait_ge(t_ctx, L * NPAIR + n0 + 1)
                        for r in range(2):
                            src = PS[4 + r][:, 0:SC] if L == 0 else PS[7][:, r * SC:r * SC + SC]
                            t0 = (2 * n0 + r) * SEQ
                            cp = act.activation(ctx_T[:, :, t0:t0 + SEQ], src.rearrange("p (c t) -> p c t", t=SEQ), ACT.Copy)
                        cp.then_inc(t_ctxc, 1)

            tokens_out(0)
            attention(0)
            tokens_out(1)
            attention(1)
            tokens_out(2)
            act.wait_ge(t_ge, 1)
            act.activation(gg[:, 1, :], gg[:, 0, :], ACT.Exp).then_inc(t_ge, 1)
            with act.Fori(0, NE // 2) as i:
                for s in range(2):
                    def high(n):
                        if n == 0:
                            act.wait_ge(e_yc, i * (2 * NG) + (s * NG + 2))
                        act.wait_ge(e_hg, i * (4 * HC) + (s * 2 * HC + n + 5))
                        act.activation(hid_h[:, n // 2, (n % 2) * HT:(n % 2) * HT + HT], hid_f[n % 4], ACT.Copy, scale=S)\
                            .then_inc(e_hi, 1)

                    act.wait_ge(m_w, i * 10 + (s * 5 + 5))
                    for n in range(2 * HC):
                        act.wait_ge(e_h, i * (4 * HC) + (s * 2 * HC + n + 1))
                        act.wait_ge(e_low, i * (4 * HC) + (s * 2 * HC + n + 1))
                        act.activation(hid_f[n % 4], PS[n % 4][:, 0:HT], ACT.Gelu, bias=b1_s[s][:, n // 2:n // 2 + 1],
                                       scale=1.0 / (S * S)).then_inc(e_hg, 1)
                        if n:
                            high(n - 1)
                    high(2 * HC - 1)
            act.wait_ge(t_gt, 1)
            act.activation(gate_T[:, 0:4 * GT], PS[1][0:NE, 0:4 * GT], ACT.Copy)
            act.activation(gate_T[:, 4 * GT:NG * GT], PS[2][0:NE, 0:3 * GT], ACT.Copy).then_inc(t_gtc, 1)

        @block.gpsimd
        def _(pool):
            pool.memset(v1[:, :, :, :], 0.0).then_inc(t_vz, 1)
            pool.memset(v2b[0:64, :], 0.0).then_inc(t_vz, 1)
            pool.wait_ge(t_vz, 2)
            for n in range(4):
                pool.wait_ge(t_var, n + 1)
                pool.tensor_tensor(ln_r[:, 1, :], ln_r[:, 0, :], expo[0:GT, 0:NG], ALU.pow).then_inc(t_rs, 1)

        @block.vector
        def _(dve):
            dn = [0]

            def link(ins):
                dn[0] += 1
                ins.then_inc(t_d, 1)
                dve.wait_ge(t_d, dn[0])

            lns = [0]

            def layernorm(dst, w=None):
                for g in range(NG):
                    ins = dve.bn_stats(ln_st[:, g, :], h_tok[:, g, :])
                link(ins)
                for g in range(NG):
                    ins = dve.bn_aggr(ln_mv[:, g, :], ln_st[:, g, :])
                link(ins)
                dve.tensor_scalar(ln_r[:, 0, :], ln_mv[:, :, 1], EPS, None, ALU.add).then_inc(t_var, 1)
                lns[0] += 1
                dve.wait_ge(t_rs, lns[0])
                for g in range(NG):
                    ins = dve.tensor_scalar(dst[:, g, :], h_tok[:, g, :], ln_mv[:, g, 0:1], ln_r[:, 1, g:g + 1],
                                            ALU.subtract, ALU.mult)
                link(ins)
                if w is not None:
                    wb = rows[0:GT, w:w + 1, :].to_broadcast([GT, NG, E])
                    link(dve.tensor_tensor(dst[:, :, :], dst[:, :, :], wb, ALU.mult))
                    for g in range(NG):
                        dve.tensor_tensor(dst[:, g, :], dst[:, g, :], rows[0:GT, w + 1, :], ALU.add).then_inc(t_x, 1)

            def attention(L):
                dve.wait_ge(t_tr, (L + 1) * NG)
                if L == 1:
                    dve.wait_ge(t_h1, 1)
                link(dve.tensor_tensor(h_tok[:, :, :], h_tok[:, :, :], rows[0:GT, 2 + L:3 + L, :].to_broadcast([GT, NG, E]),
                                       ALU.add))
                dve.wait_ge(t_vz, 2)
                for n in range(NPAIR):
                    dve.wait_ge(t_v, L * NPAIR + n + 1)
                    if L == 0:
                        dve.tensor_tensor(v1[:, n, :, 0:DH], PS[6 + n % 2][:, 0:E].rearrange("p (h d) -> p h d", d=DH),
                                          rows[:, 0, :].rearrange("p (h d) -> p h d", d=DH), ALU.add).then_inc(t_vc, 1)
                    else:
                        for r in range(2):
                            ins = dve.tensor_tensor(v2[:, 2 * n + r, :, 0:DH],
                                                    PS[6 + n % 2][0:64, r * E:r * E + E].rearrange("p (h d) -> p h d", d=DH),
                                                    rows[0:64, 1, :].rearrange("p (h d) -> p h d", d=DH), ALU.add)
                        ins.then_inc(t_vc, 1)
                for n in range(NPAIR):
                    k = L * NPAIR + n
                    dve.wait_ge(t_sc, k + 1)
                    p = prob[n % 2]
                    pj = p[:, :, :].rearrange("p (c j) t -> p j c t", j=4)
                    mj = mx[:, :].rearrange("p (c j) -> p j c", j=4)
                    for j in range(4):
                        ins = dve.tensor_reduce(mj[:, j, :], PS[j][:, 0:SC].rearrange("p (c t) -> p c t", t=SEQ), AX_X, ALU.max)
                    link(ins)
                    if L == 1 and n >= 2:
                        dve.wait_ge(t_ptr, n - 1)
                    elif k >= 2:
                        dve.wait_ge(t_ctx, min(k - 1, NPAIR))
                    for j in range(4):
                        ins = dve.tensor_tensor(pj[:, j], PS[j][:, 0:SC].rearrange("p (c t) -> p c t", t=SEQ),
                                                mj[:, j, :].unsqueeze(2).to_broadcast([128, NCH, SEQ]), ALU.subtract)
                    ins.then_inc(t_sub, 1)
                    dve.wait_ge(t_exp, k + 1)
                    link(dve.tensor_reduce(sm[:, :], p[:, :, :], AX_X, ALU.add))
                    link(dve.reciprocal(ri[:, :], sm[:, :]))
                    if L == 0:
                        if k >= 1:
                            dve.wait_ge(t_ctx, k)
                        dve.tensor_tensor(vn[:, :, :], v1[:, n, :, :], ri[:, :].unsqueeze(2).to_broadcast([128, HEADS, HPAD]),
                                          ALU.mult).then_inc(t_p, 1)
                    else:
                        dve.tensor_tensor(p[:, :, :], p[:, :, :], ri[:, :].unsqueeze(2).to_broadcast([128, HEADS, SEQ]),
                                          ALU.mult).then_inc(t_p, 1)
                for g in range(NG):
                    dve.wait_ge(t_o, L * NG + g + 1)
                    dve.tensor_tensor(h_tok[:, g, :], h_tok[:, g, :], PS[g % 2][0:GT, 0:E], ALU.add).then_inc(t_oc, 1)
                dve.wait_ge(t_oc, (L + 1) * NG)

            def prepare(i, s, piece):
                w1f, w2f = w1[s][:, :, :], w2[s][:, :, :]
                n = i * 10 + s * 5
                if piece == 0:
                    dve.wait_ge(e_w[s], i * 48 + 48)
                    dve.tensor_scalar(w1_s[s][:, 0], w1f, S, None, ALU.mult).then_inc(m_w, 1)
                elif piece == 1:
                    dve.tensor_scalar(w2_s[s][:, :, 0, :], w2f, S, None, ALU.mult).then_inc(m_w, 1)
                    dve.tensor_copy(b1_s[s][:, :], b1[s][:, :]).then_inc(m_w, 1)
                elif piece == 2:
                    dve.wait_ge(m_w, n + 1)
                    dve.scalar_tensor_tensor(w1_s[s][:, 1], w1f, S, w1_s[s][:, 0], ALU.mult, ALU.subtract).then_inc(m_w, 1)
                else:
                    dve.wait_ge(m_w, n + 2)
                    dve.scalar_tensor_tensor(w2_s[s][:, :, 1, :], w2f, S, w2_s[s][:, :, 0, :], ALU.mult, ALU.subtract)\
                        .then_inc(m_w, 1)

            def expert(i, s, last=False):
                if not last:
                    prepare(i + s, 1 - s, 0)
                    prepare(i + s, 1 - s, 1)
                for n in range(2 * HC):
                    dve.wait_ge(e_hi, i * (4 * HC) + (s * 2 * HC + n + 1))
                    t = slice((n % 2) * HT, (n % 2) * HT + HT)
                    dve.scalar_tensor_tensor(hid_l[:, n // 2, t], hid_f[n % 4], S, hid_h[:, n // 2, t],
                                             ALU.mult, ALU.subtract).then_inc(e_low, 1)
                    if n in (3, 6) and not last:
                        prepare(i + s, 1 - s, 1 + n // 3)
                for g in range(NG):
                    bank = PS[4 + (s * NG + g) % 2]
                    gate_e = gate_s[:, g, bass.ds(i * 2 + s, 1)]
                    dve.wait_ge(e_yc, i * (2 * NG) + (s * NG + 2))
                    dve.wait_ge(e_y, i * (2 * NG) + (s * NG + g + 1))
                    dve.scalar_tensor_tensor(h_tok[:, g, :], bank[0:GT, E:2 * E], gate_e, h_tok[:, g, :],
                                             ALU.mult, ALU.add).then_inc(e_ya, 1)
                    dve.wait_ge(e_ya, i * (2 * NG) + (s * NG + g + 1))
                    dve.scalar_tensor_tensor(h_tok[:, g, :], bank[0:GT, 0:E], gate_e, h_tok[:, g, :],
                                             ALU.mult, ALU.add).then_inc(e_yc, 1)

            for t in (x_T[:, 2 * TOK:], qk_T[0][:, NCH * TOK:], qk_T[1][:, NCH * TOK:]):
                ins = dve.memset(t, 0.0)
            ins.then_inc(t_z, 1)
            dve.sem_inc(e_low, 4)
            dve.sem_inc(e_yc, 2)
            dve.wait_ge(t_z, 1)
            dve.sem_inc(t_x, NG)
            dve.wait_ge(t_const, 16 * len(CONST))
            attention(0)
            layernorm(h_tok)
            layernorm(x_tok, 4)
            dve.tensor_copy(h1_tok[:, :, :], h_tok[:, :, :]).then_inc(t_h1, 1)
            for piece in range(4):
                prepare(0, 0, piece)
            attention(1)
            layernorm(x_tok, 6)
            dve.wait_ge(t_h1, 1)
            link(dve.tensor_tensor(h_tok[:, :, :], h_tok[:, :, :], h1_tok[:, :, :], ALU.add))
            dve.wait_ge(t_trc, 3 * NG)
            dve.tensor_scalar(x_h, x_T2, S, None, ALU.mult).then_inc(m_x, 1)
            dve.wait_ge(m_x, 1)
            dve.scalar_tensor_tensor(x_l, x_T2, S, x_h, ALU.mult, ALU.subtract).then_inc(m_x, 1)
            dve.wait_ge(t_lg, 1)
            dve.tensor_copy(lg[:, :, :].rearrange("p g e -> p (g e)"), PS[0][0:GT, 0:NG * NE]).then_inc(t_lgd, 1)
            dve.wait_ge(t_lgd, 1)
            for g in range(NG):
                ins = dve.max(top[:, g, :], lg[:, g, :])
            link(ins)
            for g in range(NG):
                ins = dve.max_index(topi[:, g, :], top[:, g, :], lg[:, g, :])
            link(ins)
            link(dve.tensor_copy(idx[:, :, :], topi[:, :, 0:2]))
            dve.tensor_tensor(gg[:, 0, :], top[:, :, 1], top[:, :, 0], ALU.subtract).then_inc(t_ge, 1)
            dve.wait_ge(t_ge, 2)
            link(dve.tensor_scalar(gg[:, 2, :], gg[:, 1, :], 1.0, None, ALU.add))
            link(dve.reciprocal(gg[:, 2, :], gg[:, 2, :]))
            link(dve.tensor_tensor(gg[:, 3, :], gg[:, 1, :], gg[:, 2, :], ALU.mult))
            for m, t in enumerate((gate, gtmp)):
                link(dve.tensor_tensor(t[:, :, :], iota[:, :].unsqueeze(1).to_broadcast([GT, NG, NE]),
                                       idx[:, :, m:m + 1].to_broadcast([GT, NG, NE]), ALU.is_equal))
                link(dve.tensor_tensor(t[:, :, :], t[:, :, :], gg[:, 2 + m, :].unsqueeze(2).to_broadcast([GT, NG, NE]),
                                       ALU.mult))
            dve.tensor_tensor(gate[:, :, :], gate[:, :, :], gtmp[:, :, :], ALU.add).then_inc(t_gate, 1)
            dve.wait_ge(t_gate, 1)
            link(dve.tensor_scalar(gate_s[:, :, :], gate[:, :, :], 1.0 / (S * S), None, ALU.mult))
            with dve.Fori(0, NE // 2 - 1) as i:
                expert(i, 0)
                expert(i, 1)
            expert(NE // 2 - 1, 0)
            expert(NE // 2 - 1, 1, last=True)
            dve.wait_ge(e_yc, NE * NG + 2)
            for g in range(NG):
                dve.wait_ge(t_b2, g + 1)
                dve.tensor_tensor(h_tok[:, g, :], h_tok[:, g, :], PS[3 + g % 2][0:GT, 0:E], ALU.add).then_inc(t_b2c, 1)
            dve.wait_ge(t_b2c, NG)
            layernorm(h_tok)
            dve.sem_inc(t_done, 1)


def laid_out(i):
    f = np.float32
    x = np.asarray(i["x"]).reshape(B, CIN, HP, P, HP, P).transpose(0, 2, 1, 4, 3, 5)
    r = {"x": x.reshape(GT, CIN, HP, PIX)}
    c1 = np.asarray(i["L0_tok_conv1_w"])
    rows = np.tile(c1.transpose(2, 1, 3, 0).reshape(3, 1, TAPS, CH), (1, 3, 1, 2))
    r["c1"] = rows.reshape(3 * IMR, 2 * CH)
    r["cz"] = c1.reshape(CH, IMR)
    r["r1"] = np.asarray(i["L0_tok_rconv1_w"]).transpose(1, 2, 3, 0).reshape(CH, TAPS, CH)
    r2 = np.asarray(i["L0_tok_rconv2_w"])
    r["r2"] = r2[:, :, ::-1, ::-1].transpose(0, 2, 3, 1).reshape(CH, TAPS, CH)
    r["proj"] = np.asarray(i["L0_tok_proj_w"]).reshape(E, CH, PIX).transpose(1, 0, 2)
    names = ["conv1_b", "gn1_g", "gn1_b", "rconv1_b", "gn2_g", "gn2_b", "rconv2_b"]
    r["vecs"] = np.tile(np.stack([np.asarray(i["L0_tok_" + n]) for n in names], 1), (2, 1))
    r["ident"] = np.eye(128, dtype=f)
    ch = np.arange(128)
    pair = (ch[:, None] % CH) // 2 == (ch[None, :] % CH) // 2
    r["avg1"] = np.where(pair & (ch[:, None] // CH == ch[None, :] // CH), 0.25, 0.0).astype(f)
    r["avg2"] = np.where(pair, 0.125, 0.0).astype(f)
    at = np.arange(HP, dtype=f)
    lo = (at / f(HP) * f(VOCAB)).astype(np.int32)
    hi = ((at + 1) / f(HP) * f(VOCAB)).astype(np.int32)
    pos = (lo + hi) // 2
    r["emb_rows"] = np.concatenate([np.asarray(i["L0_tok_row_emb"])[pos], np.asarray(i["L0_tok_col_emb"])[pos],
                                    np.asarray(i["L0_tok_proj_b"])[None]])
    t = np.arange(TOK) % SEQ
    hot = np.zeros((2 * HP + 1, TOK), f)
    hot[t // HP, np.arange(TOK)] = 1
    hot[HP + t % HP, np.arange(TOK)] = 1
    hot[2 * HP] = 1
    r["onehot"] = hot
    def pad_heads(w):
        o = np.zeros((*w.shape[:-1], HEADS, HPAD), f)
        o[..., :DH] = w.reshape(*w.shape[:-1], HEADS, DH)
        return o.reshape(*w.shape[:-1], HEADS * HPAD)

    def two(w):
        return w.reshape(2, EK, w.shape[-1]).transpose(1, 0, 2)

    qkv = np.asarray(i["L0_ffn_qkv_w"]).reshape(3, E, E)
    qkvb = np.asarray(i["L0_ffn_qkv_b"]).reshape(3, E)
    w = [[np.asarray(i[f"L0_attn_W{n}"]).transpose(1, 0, 2).reshape(E, E) for n in "qkv"], [m.T for m in qkv]]
    bias = [[np.asarray(i[f"L0_attn_b{n}"]).reshape(E) for n in "qkv"], list(qkvb)]
    wo = [np.asarray(i["L0_attn_Wo"]), np.asarray(i["L0_ffn_proj_w"]).T]
    for L in range(2):
        r[f"wq{L}"], r[f"wk{L}"] = two(pad_heads(w[L][0])), two(pad_heads(w[L][1]))
        r[f"wv{L}"] = two(w[L][2])
        r[f"wo{L}"] = pad_heads(wo[L].T).T.reshape(NCH, 128, E).transpose(1, 0, 2)
        r[f"bqk{L}"] = np.concatenate([pad_heads(b[None]).reshape(NCH, 128).T for b in bias[L][:2]], 1)
    rows = [bias[0][2], bias[1][2], i["L0_attn_bo"], i["L0_ffn_proj_b"], i["L0_ffn_norm1_w"], i["L0_ffn_norm1_b"],
            i["L0_ffn_norm2_w"], i["L0_ffn_norm2_b"]]
    r["rows"] = np.tile(np.stack([np.asarray(v) for v in rows])[None], (128, 1, 1))
    r["wg"] = two(np.asarray(i["L0_ffn_w_gate"]))
    r["w1"] = np.asarray(i["L0_ffn_W1"]).reshape(NE, 2, EK, HID).transpose(0, 2, 1, 3)
    r["w2"] = np.asarray(i["L0_ffn_W2"]).reshape(NE, HC, 128, E).transpose(0, 2, 1, 3)
    r["b1"] = np.asarray(i["L0_ffn_b1"]).reshape(NE, HC, 128).transpose(0, 2, 1)
    r["b2"] = np.asarray(i["L0_ffn_b2"])
    r["iota"] = np.tile(np.arange(NE, dtype=f), (GT, 1))
    return {k: np.ascontiguousarray(v) for k, v in r.items()}


def kernel(**inputs):
    import concourse.bacc as bacc
    from concourse.bass_utils import run_bass_kernel_spmd

    nc = bacc.Bacc("TRN2", target_bir_lowering=False, num_devices=1)
    arrays = laid_out(inputs)
    a = {k: nc.dram_tensor("in_" + k, v.shape, mybir.dt.from_np(v.dtype), kind="ExternalInput").ap()
         for k, v in arrays.items()}
    out = nc.dram_tensor("out", (TOK, E), F32, kind="ExternalOutput").ap()
    build(nc, a, out)
    r = run_bass_kernel_spmd(nc, [{"in_" + k: v for k, v in arrays.items()}], core_ids=[0])
    return r.results[0]["out"].reshape(B, SEQ, E)
```
